# Optimizing a Trainium2 kernel written in Bass

```python
import numpy as np
import jax
import jax.numpy as jnp

def _softmax(x, axis=-1):
    return jax.nn.softmax(x, axis=axis)

def _gelu(x):
    return jax.nn.gelu(x, approximate=True)

def _silu(x):
    return jax.nn.silu(x)

def _sigmoid(x):
    return jax.nn.sigmoid(x)

def _layernorm(x, axis=-1, eps=1e-05):
    m = jnp.mean(x, axis=axis, keepdims=True)
    v = jnp.var(x, axis=axis, keepdims=True)
    return (x - m) / jnp.sqrt(v + eps)

def _scatter_add(tgt, idx, src, axis=0):
    return tgt.at[idx].add(src)

def _segment_sum(src, seg, n):
    return jax.ops.segment_sum(src, seg, n)
kernel_name = 'mk_lm_tower_d2_tok_ids256_r4_55a10f'

def setup_inputs(seed: int=0):
    np.random.seed(seed)
    _w = jnp.asarray

    def _rec_inputs():
        import jax
        import jax.numpy as jnp
        _rk = jax.random.key(seed)
        x = jax.random.randint(jax.random.fold_in(_rk, 1), (8, 1024), 0, 262137, jnp.int32)
        return x
    x = _rec_inputs()

    def _L0_tok_setup():
        import jax, jax.numpy as jnp
        import numpy as np
        NUM_EMB1 = 128
        NUM_EMB2 = 128
        EMB_DIM = 64
        BATCH, SEQ = (16, 1024)
        key = jax.random.key(seed)
        k1, k2, k3, k4, k5 = jax.random.split(key, 5)
        x = jax.random.randint(k1, (BATCH, SEQ), 0, NUM_EMB1 * NUM_EMB2, dtype=jnp.int64 if jax.config.jax_enable_x64 else jnp.int32)
        emb1 = jax.random.normal(k2, (NUM_EMB1, EMB_DIM), dtype=jnp.float32)
        emb2 = jax.random.normal(k3, (NUM_EMB2, EMB_DIM), dtype=jnp.float32)
        lim = 1.0 / np.sqrt(2 * EMB_DIM)
        W = jax.random.uniform(k4, (EMB_DIM, 2 * EMB_DIM), minval=-lim, maxval=lim, dtype=jnp.float32)
        b = jax.random.uniform(k5, (EMB_DIM,), minval=-lim, maxval=lim, dtype=jnp.float32)
        return {'x': x, 'emb1': emb1, 'emb2': emb2, 'W': W, 'b': b}
    _L0_tok_all = _L0_tok_setup()
    _L0_tok_in = {k: v for k, v in _L0_tok_all.items() if k in ('emb1', 'emb2', 'W', 'b')}
    del _L0_tok_all

    def _L0_attn_setup():
        import jax, jax.numpy as jnp
        import numpy as np
        key = jax.random.key(seed)
        inputs = jax.random.normal(key, (8, 512, 64), dtype=jnp.float32)
        return {'inputs': inputs}
    _L0_attn_all = _L0_attn_setup()
    _L0_attn_in = {k: v for k, v in _L0_attn_all.items() if k in ()}
    del _L0_attn_all

    def _L0_ffn_setup():
        import jax, jax.numpy as jnp
        import numpy as np
        C = 64
        HID = 256
        E = 8
        TEMP = 1.0
        key = jax.random.key(seed)
        ks = jax.random.split(key, 7)
        x = jax.random.normal(ks[0], (8, 4096, C), dtype=jnp.float32)
        W1 = jax.random.normal(ks[1], (C, HID), dtype=jnp.float32) * 0.02
        b1 = jnp.zeros((HID,), dtype=jnp.float32)
        Wg = jax.random.normal(ks[2], (HID, E), dtype=jnp.float32) * 0.02
        bg = jnp.zeros((E,), dtype=jnp.float32)
        Wd = jax.random.normal(ks[3], (E, HID, C), dtype=jnp.float32) * 0.02
        bd = jnp.zeros((E, C), dtype=jnp.float32)
        return {'x': x, 'W1': W1, 'b1': b1, 'Wg': Wg, 'bg': bg, 'Wd': Wd, 'bd': bd}
    _L0_ffn_all = _L0_ffn_setup()
    _L0_ffn_in = {k: v for k, v in _L0_ffn_all.items() if k in ('W1', 'b1', 'Wg', 'bg', 'Wd', 'bd')}
    del _L0_ffn_all

    def _L1_attn_setup():
        import jax, jax.numpy as jnp
        import numpy as np
        D_MODEL = 64
        EXPAND = 2
        D_STATE = 8
        E = D_MODEL * EXPAND
        BATCH = 8
        SEQ = 512
        BN_EPS = 1e-05
        key = jax.random.key(seed)
        ks = jax.random.split(key, 8)
        x = jax.random.normal(ks[0], (BATCH, SEQ, D_MODEL), jnp.float32)
        w1 = jax.random.normal(ks[1], (E, D_MODEL), jnp.float32) * 0.05
        b1 = jnp.zeros((E,), jnp.float32)
        wd = jax.random.normal(ks[2], (E, 1, 5), jnp.float32) * 0.1
        bd = jnp.zeros((E,), jnp.float32)
        gamma = jnp.ones((E,), jnp.float32)
        beta = jnp.zeros((E,), jnp.float32)
        rmean = jnp.zeros((E,), jnp.float32)
        rvar = jnp.ones((E,), jnp.float32)
        A = -jnp.ones((E,), jnp.float32) * 0.5
        Bm = jax.random.normal(ks[3], (E, D_STATE), jnp.float32) * 0.1
        Cm = jax.random.normal(ks[4], (E, D_STATE), jnp.float32) * 0.1
        Dv = jax.random.normal(ks[5], (E,), jnp.float32) * 0.1
        w2 = jax.random.normal(ks[6], (D_MODEL, E), jnp.float32) * 0.05
        b2 = jnp.zeros((D_MODEL,), jnp.float32)
        return dict(x=x, w1=w1, b1=b1, wd=wd, bd=bd, gamma=gamma, beta=beta, rmean=rmean, rvar=rvar, A=A, Bm=Bm, Cm=Cm, Dv=Dv, w2=w2, b2=b2)
    _L1_attn_all = _L1_attn_setup()
    _L1_attn_in = {k: v for k, v in _L1_attn_all.items() if k in ('w1', 'b1', 'wd', 'bd', 'gamma', 'beta', 'rmean', 'rvar', 'A', 'Bm', 'Cm', 'Dv', 'w2', 'b2')}
    del _L1_attn_all

    def _L1_ffn_setup():
        import jax, jax.numpy as jnp
        import numpy as np
        D_IN, D_HID, D_OUT = (64, 128, 64)
        N_EXPERTS, TOP_K = (64, 2)
        B, S = (8, 1024)
        key = jax.random.key(seed)
        ks = jax.random.split(key, 8)
        scale_in = 1.0 / np.sqrt(D_IN)
        scale_hid = 1.0 / np.sqrt(D_HID)
        return {'x': jax.random.normal(ks[0], (B, S, D_IN), dtype=jnp.float32), 'Wr': jax.random.uniform(ks[1], (D_IN, N_EXPERTS), jnp.float32, -scale_in, scale_in), 'br': jax.random.uniform(ks[2], (N_EXPERTS,), jnp.float32, -scale_in, scale_in), 'W1': jax.random.uniform(ks[3], (N_EXPERTS, D_IN, D_HID), jnp.float32, -scale_in, scale_in), 'b1': jax.random.uniform(ks[4], (N_EXPERTS, D_HID), jnp.float32, -scale_in, scale_in), 'W2': jax.random.uniform(ks[5], (N_EXPERTS, D_HID, D_OUT), jnp.float32, -scale_hid, scale_hid), 'b2': jax.random.uniform(ks[6], (N_EXPERTS, D_OUT), jnp.float32, -scale_hid, scale_hid)}
    _L1_ffn_all = _L1_ffn_setup()
    _L1_ffn_in = {k: v for k, v in _L1_ffn_all.items() if k in ('Wr', 'br', 'W1', 'b1', 'W2', 'b2')}
    del _L1_ffn_all
    return {'x': x, 'L0_tok_emb1': _L0_tok_in['emb1'], 'L0_tok_emb2': _L0_tok_in['emb2'], 'L0_tok_W': _L0_tok_in['W'], 'L0_tok_b': _L0_tok_in['b'], 'L0_ffn_W1': _L0_ffn_in['W1'], 'L0_ffn_b1': _L0_ffn_in['b1'], 'L0_ffn_Wg': _L0_ffn_in['Wg'], 'L0_ffn_bg': _L0_ffn_in['bg'], 'L0_ffn_Wd': _L0_ffn_in['Wd'], 'L0_ffn_bd': _L0_ffn_in['bd'], 'L1_attn_w1': _L1_attn_in['w1'], 'L1_attn_b1': _L1_attn_in['b1'], 'L1_attn_wd': _L1_attn_in['wd'], 'L1_attn_bd': _L1_attn_in['bd'], 'L1_attn_gamma': _L1_attn_in['gamma'], 'L1_attn_beta': _L1_attn_in['beta'], 'L1_attn_rmean': _L1_attn_in['rmean'], 'L1_attn_rvar': _L1_attn_in['rvar'], 'L1_attn_A': _L1_attn_in['A'], 'L1_attn_Bm': _L1_attn_in['Bm'], 'L1_attn_Cm': _L1_attn_in['Cm'], 'L1_attn_Dv': _L1_attn_in['Dv'], 'L1_attn_w2': _L1_attn_in['w2'], 'L1_attn_b2': _L1_attn_in['b2'], 'L1_ffn_Wr': _L1_ffn_in['Wr'], 'L1_ffn_br': _L1_ffn_in['br'], 'L1_ffn_W1': _L1_ffn_in['W1'], 'L1_ffn_b1': _L1_ffn_in['b1'], 'L1_ffn_W2': _L1_ffn_in['W2'], 'L1_ffn_b2': _L1_ffn_in['b2']}

def reference(x, L0_tok_emb1, L0_tok_emb2, L0_tok_W, L0_tok_b, L0_ffn_W1, L0_ffn_b1, L0_ffn_Wg, L0_ffn_bg, L0_ffn_Wd, L0_ffn_bd, L1_attn_w1, L1_attn_b1, L1_attn_wd, L1_attn_bd, L1_attn_gamma, L1_attn_beta, L1_attn_rmean, L1_attn_rvar, L1_attn_A, L1_attn_Bm, L1_attn_Cm, L1_attn_Dv, L1_attn_w2, L1_attn_b2, L1_ffn_Wr, L1_ffn_br, L1_ffn_W1, L1_ffn_b1, L1_ffn_W2, L1_ffn_b2):
    import jax
    import jax.numpy as jnp

    def _L0_tok_ref(x, emb1, emb2, W, b):
        import jax, jax.numpy as jnp
        import numpy as np
        NUM_EMB1 = 128
        NUM_EMB2 = 128
        EMB_DIM = 64
        BATCH, SEQ = (16, 1024)
        dim2 = NUM_EMB2
        x1 = emb1[x // dim2]
        x2 = emb2[x % dim2]
        h = jnp.concatenate([x1, x2], axis=-1)
        y = jnp.tanh(jnp.einsum('bsk,dk->bsd', h, W) + b)
        return y

    def _L0_attn_ref(inputs):
        import jax, jax.numpy as jnp
        import numpy as np
        d_k = jnp.asarray(inputs.shape[-1], dtype=inputs.dtype)
        scores = jnp.einsum('bnd,bmd->bnm', inputs, inputs) / jnp.sqrt(d_k)
        weights = jax.nn.softmax(scores, axis=-1)
        context = jnp.einsum('bnm,bmd->bnd', weights, inputs)
        return context

    def _L0_ffn_ref(x, W1, b1, Wg, bg, Wd, bd):
        import jax, jax.numpy as jnp
        import numpy as np
        C = 64
        HID = 256
        E = 8
        TEMP = 1.0
        orig_shape = x.shape
        xf = x.reshape(-1, orig_shape[-1])
        H = jax.nn.gelu(xf @ W1 + b1, approximate=False)
        probs = jax.nn.softmax((H @ Wg + bg) / TEMP, axis=-1)
        assign = jnp.argmax(probs, axis=-1)
        out = jnp.zeros_like(xf)
        for e in range(Wd.shape[0]):
            y = H @ Wd[e] + bd[e]
            sel = (assign == e)[:, None]
            out = out + jnp.where(sel, probs[:, e:e + 1] * y, 0.0)
        return out.reshape(orig_shape)

    def _L1_attn_ref(x, w1, b1, wd, bd, gamma, beta, rmean, rvar, A, Bm, Cm, Dv, w2, b2):
        import jax, jax.numpy as jnp
        import numpy as np
        D_MODEL = 64
        EXPAND = 2
        D_STATE = 8
        E = D_MODEL * EXPAND
        BATCH = 8
        SEQ = 512
        BN_EPS = 1e-05
        xc = jax.nn.silu(jnp.einsum('bld,ed->ble', x, w1) + b1)
        xcc = jnp.transpose(xc, (0, 2, 1))
        y = jax.lax.conv_general_dilated(xcc, wd, window_strides=(1,), padding=[(2, 2)], dimension_numbers=('NCH', 'OIH', 'NCH'), feature_group_count=E)
        y = y + bd[None, :, None]
        scale = gamma * jax.lax.rsqrt(rvar + BN_EPS)
        y = y * scale[None, :, None] + (beta - rmean * scale)[None, :, None]
        y = jax.nn.silu(y)
        x_local = jnp.transpose(y, (0, 2, 1))
        expA = jnp.exp(A)

        def step(h, xt):
            h = expA[None, :, None] * h + xt[:, :, None] * Bm[None]
            yt = jnp.einsum('bes,es->be', h, Cm) + Dv * xt
            return (h, yt)
        h0 = jnp.zeros((x.shape[0], E, D_STATE), x.dtype)
        _, ys = jax.lax.scan(step, h0, jnp.transpose(x_local, (1, 0, 2)))
        out = jnp.transpose(ys, (1, 0, 2))
        out = jnp.einsum('ble,de->bld', out, w2) + b2
        return out

    def _L1_ffn_ref(x, Wr, br, W1, b1, W2, b2):
        import jax, jax.numpy as jnp
        import numpy as np
        D_IN, D_HID, D_OUT = (64, 128, 64)
        N_EXPERTS, TOP_K = (64, 2)
        B, S = (8, 1024)
        Bx, Sx, D = x.shape
        xf = x.reshape(-1, D)
        T = xf.shape[0]
        E = Wr.shape[1]
        logits = xf @ Wr + br
        topk_logits, topk_idx = jax.lax.top_k(logits, TOP_K)
        gates = jax.nn.softmax(topk_logits, axis=1)
        combine = jnp.zeros((T, E), xf.dtype).at[jnp.arange(T)[:, None], topk_idx].add(gates)
        out = jnp.zeros((T, W2.shape[-1]), xf.dtype)
        for e in range(E):
            h = jax.nn.relu(xf @ W1[e] + b1[e])
            y = h @ W2[e] + b2[e]
            out = out + combine[:, e:e + 1] * y
        return out.reshape(Bx, Sx, -1)
    h = _L0_tok_ref(x, L0_tok_emb1, L0_tok_emb2, L0_tok_W, L0_tok_b)
    h = h + _L0_attn_ref(_layernorm(h, axis=-1))
    h = h + _L0_ffn_ref(_layernorm(h, axis=-1), L0_ffn_W1, L0_ffn_b1, L0_ffn_Wg, L0_ffn_bg, L0_ffn_Wd, L0_ffn_bd)
    h = h + _L1_attn_ref(_layernorm(h, axis=-1), L1_attn_w1, L1_attn_b1, L1_attn_wd, L1_attn_bd, L1_attn_gamma, L1_attn_beta, L1_attn_rmean, L1_attn_rvar, L1_attn_A, L1_attn_Bm, L1_attn_Cm, L1_attn_Dv, L1_attn_w2, L1_attn_b2)
    h = h + _L1_ffn_ref(_layernorm(h, axis=-1), L1_ffn_Wr, L1_ffn_br, L1_ffn_W1, L1_ffn_b1, L1_ffn_W2, L1_ffn_b2)
    return h

_drawn_inputs = setup_inputs


def setup_inputs(seed=0):
    import zlib

    import numpy as np

    out = dict(_drawn_inputs(seed))
    spreads = {'L0_ffn_b1': (0.0, 0.8),
     'L0_ffn_bg': (0.0, 0.366),
     'L0_ffn_bd': (0.0, 0.489),
     'L1_attn_b1': (0.0, 0.8),
     'L1_attn_bd': (0.0, 0.8),
     'L1_attn_gamma': (1.0, 0.6),
     'L1_attn_beta': (0.0, 0.8),
     'L1_attn_rmean': (0.0, 0.8),
     'L1_attn_rvar': (1.0, 0.6),
     'L1_attn_A': (-0.5, 0.6),
     'L1_attn_b2': (0.0, 2.0)}
    factors = {'L0_ffn_W1': 8.0,
     'L0_ffn_Wg': 8.0,
     'L0_ffn_Wd': 6.794,
     'L1_attn_w1': 8.0,
     'L1_attn_wd': 8.0,
     'L1_attn_Bm': 6.777,
     'L1_attn_Cm': 8.0,
     'L1_attn_Dv': 5.28,
     'L1_attn_w2': 4.825,
     'L1_ffn_b1': 25.2,
     'L1_ffn_Wr': 8.0,
     'L1_ffn_br': 8.0,
     'L1_ffn_W1': 8.0,
     'L1_ffn_W2': 8.0,
     'L1_ffn_b2': 64.0}
    for name, (base, spread) in spreads.items():
        noise = np.random.default_rng([zlib.crc32(name.encode()), seed]).standard_normal(out[name].shape)
        drawn = base * np.exp(spread * noise) if base else spread * noise
        out[name] = jnp.asarray(drawn.astype(out[name].dtype))
    for name, factor in factors.items():
        out[name] = (out[name] * factor).astype(out[name].dtype)
    return out
```

```python
from contextlib import ExitStack

import concourse.bass as bass
from concourse import mybir

ALU = mybir.AluOpType
ACT = mybir.ActivationFunctionType
AX = mybir.AxisListType.X
F32 = mybir.dt.float32
BF16 = mybir.dt.bfloat16
I32 = mybir.dt.int32
U32 = mybir.dt.uint32

P = 128
D = 64
SEQS, SEQ = 8, 1024
T = SEQ // P
HALVES = 2
PAIRS = SEQS // 2 // HALVES
TH = SEQS * T // HALVES
VOCAB = 128
HID = 256
CH = HID // P
E8 = 8
TAPS = 5
STATE = 8
EX = 64
HID2 = 128
TOP = 2
LN_EPS = 1e-5
BN_EPS = 1e-5
BLOCKS = TH * P * TOP // P + EX
GROUP = 4
GROUPS = BLOCKS // GROUP
SLOTS = BLOCKS * P
W65 = D + 1
RSQRT_SEED = 0x5F3759DF


def lm_tower(nc, a, out):
    ctx = ExitStack()
    with ctx:
        def sb(name, shape, dt=F32):
            return ctx.enter_context(nc.sbuf_tensor(name, shape, dt))

        def sem(name):
            return ctx.enter_context(nc.semaphore(name))

        idx_dram = nc.dram_tensor("idx_dram", [2, SEQS * SEQ], BF16)
        xs_dram = [nc.dram_tensor(f"xs_dram{h}", [SLOTS, D], F32) for h in range(HALVES)]
        ys_dram = [nc.dram_tensor(f"ys_dram{h}", [SLOTS, D], F32) for h in range(HALVES)]

        table_parts = sb("table_parts", [VOCAB, 3, 2, D], BF16)
        ffn_w1 = sb("ffn_w1", [D, HID])
        ffn_b1 = sb("ffn_b1", [P, CH])
        ffn_wg = sb("ffn_wg", [P, CH, E8])
        ffn_bg = sb("ffn_bg", [P, E8])
        ffn_wd = sb("ffn_wd", [P, CH, E8, D])
        ffn_bd = sb("ffn_bd", [T * E8, T, D])
        ssm_w1 = sb("ssm_w1", [P, D])
        ssm_w1t = sb("ssm_w1t", [D, P])
        ssm_col = sb("ssm_col", [P, 8])
        ssm_taps = sb("ssm_taps", [P, TAPS])
        ssm_bc = sb("ssm_bc", [P, 2, STATE])
        ssm_bn = sb("ssm_bn", [P, 6])
        ssm_w2bc = sb("ssm_w2bc", [P, D])
        ssm_w2d = sb("ssm_w2d", [P, D])
        ssm_b2 = sb("ssm_b2", [P, D])
        moe_wr = sb("moe_wr", [D, EX])
        moe_br = sb("moe_br", [P, EX])
        moe_w1 = sb("moe_w1", [W65, EX, HID2])
        moe_w2 = sb("moe_w2", [HID2, EX, D])
        moe_b2 = sb("moe_b2", [P, EX, D])
        ident = sb("ident", [P, P])
        before = sb("before", [P, P], BF16)
        ones = sb("ones", [P, P], BF16)
        iota_p = sb("iota_p", [P, 1])
        iota_e = sb("iota_e", [P, EX])
        rank_e8 = sb("rank_e8", [P, E8])

        idx_all = sb("idx_all", [P, 2, TH * P], BF16)

        h_all = sb("h_all", [P, HALVES * TH, D])
        xn_all = sb("xn_all", [P, HALVES * TH, D])
        top_val = sb("top_val", [P, HALVES * TH, TOP])
        top_idx = sb("top_idx", [P, HALVES * TH, TOP])

        hots = sb("hots", [P, 2, 2, SEQ], BF16)
        hot = [hots[:, s, :, :] for s in range(2)]
        h = [sb(f"h{s}", [P, T, D]) for s in range(2)]
        xca = sb("xca", [P, EX * (TH + 1) // 2])
        xc, acc = (xca[:, k * T * D:(k + 1) * T * D].rearrange("p (t d) -> p t d", d=D) for k in range(2))
        seg_keep = xca[:, :].bitcast(BF16).rearrange("p (e t) -> p e t", e=EX)
        stat = sb("stat", [P, 6, T])
        stat_i = sb("stat_i", [P, T], I32)
        xn = [sb(f"xn{s}", [P, T, W65]) for s in range(2)]
        xt = [sb(f"xt{s}", [D, SEQ]) for s in range(2)]
        ering = sb("ering", [P, 4, 512])
        ht = sb("ht", [P, 2, CH, SEQ])
        dtmp = sb("dtmp", [P, 2, E8, D])
        sq = dtmp[:, 0, :, :]
        gate = sb("gate", [P, 8, T, E8])
        gate1 = sb("gate1", [P, 4, T])
        selp = [sb(f"selp{s}", [P, T, E8]) for s in range(2)]
        fd = [sb(f"fd{s}", [P, T, E8]) for s in range(2)]
        fe = [sb(f"fe{s}", [P, T, E8]) for s in range(2)]
        selt = [sb(f"selt{s}", [T * E8, P]) for s in range(2)]
        pad = TAPS // 2
        up = sb("up", [P, 2, EX * (TH + 1) // 2])
        gst = sb("gst", [P, 2, EX * (TH + 1) // 2])
        lg = [up[:, s, pad:pad + T * EX].rearrange("p (t e) -> p t e", e=EX) for s in range(2)]
        v8 = [sb(f"v8{s}", [P, T, 8]) for s in range(2)]
        i8 = [sb(f"i8{s}", [P, T, 8], U32) for s in range(2)]
        used = [0]

        def early(rows_, cols, dt=F32):
            v = gst[0:rows_, used[0] // (EX * (TH + 1) // 2), used[0] % (EX * (TH + 1) // 2):][:, 0:cols]
            used[0] += cols
            return v if dt == F32 else v.bitcast(dt)

        emb, emb_t, tok_w = early(VOCAB, 2 * D), early(2 * D, VOCAB), early(D, 2 * D)
        tok_b, tok_wt, ssm_w2 = early(P, D), early(2 * D, D), early(D, P)
        table = early(VOCAB, 2 * D).rearrange("p (k d) -> p k d", k=2)
        ids = early(SEQS * T, P, I32)
        used[0] = EX * (TH + 1) // 2
        ids_i = early(SEQS * T, 2 * P, I32).rearrange("p (k n) -> p k n", k=2)
        ids_f = early(SEQS * T, 3 * P).rearrange("p (k n) -> p k n", k=3)
        ids_b = early(SEQS * T, P, BF16).rearrange("p (k n) -> p k n", k=2)
        yconv = [ht[:, s, 0, :] for s in range(2)]
        ysilu = [ht[:, s, 1, :] for s in range(2)]

        pick = [ht[:, k, 0, :].bitcast(BF16).rearrange("p (t e) -> p t e", e=EX) for k in range(TOP)]
        picks = ht[:, 0, 1, :].bitcast(BF16).rearrange("p (t e) -> p t e", e=EX)
        place = ering[:, :, :].rearrange("p a b -> p (a b)").rearrange("p (t e) -> p t e", e=EX)
        cnt = up[:, :, :].rearrange("p a b -> p (a b)").rearrange("p (e t) -> p e t", e=EX)
        cum = gst[:, :, :].rearrange("p a b -> p (a b)").rearrange("p (e t) -> p e t", e=EX)
        prod = hots[:, :, :, :].rearrange("p a b c -> p (a b c)").bitcast(F32).rearrange("p (t e) -> p t e", e=EX)
        nb = gate[:, 0:5, :, :].rearrange("p k t e -> p k (t e)")
        nb_i = sb("nb_i", [P, EX], I32)
        eb = sb("eb", [P, 1])
        slot_f = sb("slot_f", [P, TOP, TH])
        slot_i = sb("slot_i", [P, 4, TOP, TH], I32)
        rows = [sb(f"rows{k}", [P, TOP, TH], I32) for k in range(HALVES)]
        expert = [sb(f"expert{k}", [1, BLOCKS], I32) for k in range(HALVES)]
        gates = sb("gates", [P, HALVES * TH, 3])

        xb = ering[:, 2, :].rearrange("p (u j d) -> p u j d", u=2, d=D)
        xbt = ering[0:W65, 0:2, :]
        hb = ht[:, 0, :, 0:GROUP * HID2]
        hbt = ht[:, 1, :, 0:GROUP * P]
        yb = ering[:, 3, :].rearrange("p (u j d) -> p u j d", u=2, d=D)
        yg = [xn_all[:, :, :].rearrange("p (k t) d -> p k t d", k=TOP),
              idx_all[:, :, :].rearrange("p a b -> p (a b)").bitcast(F32).rearrange("p (k t d) -> p k t d", k=TOP, d=D)]
        zeros = ht[:, 0, :, :].rearrange("p a b -> p (a b)")

        wide = [ctx.enter_context(nc.psum_tensor(f"wide{i}", [P, 512], F32)) for i in range(4)]
        trp = [ctx.enter_context(nc.psum_tensor(f"trp{i}", [P, 512], F32)) for i in range(2)]
        outp = [ctx.enter_context(nc.psum_tensor(f"outp{i}", [P, 512], F32)) for i in range(2)]

        ids_loaded = sem("ids_loaded")
        w_loaded = sem("w_loaded")
        bd_loaded = sem("bd_loaded")
        moe_loaded = sem("moe_loaded")
        consts = sem("consts")
        seg_done = sem("seg_done")
        bd_zero = sem("bd_zero")
        zero_ready = sem("zero_ready")
        zero_stored = sem("zero_stored")
        ids_ready = sem("ids_ready")
        idx_stored = sem("idx_stored")
        idx_loaded = sem("idx_loaded")
        setup_t = sem("setup_t")
        setup_c = sem("setup_c")
        table_mm = sem("table_mm")
        table_ready = sem("table_ready")
        bn_var = sem("bn_var")
        bn_rstd = sem("bn_rstd")
        decay_ready = sem("decay_ready")
        setup_done = sem("setup_done")
        hot_ready, xn_ready, ctx_done = sem("hot_ready"), sem("xn_ready"), sem("ctx_done")
        fd_ready, selp_ready, d_done = sem("fd_ready"), sem("selp_ready"), sem("d_done")
        conv_done, scan_done = sem("conv_done"), sem("scan_done")
        tok_mm, tr_ready, s_ready, pv_done = sem("tok_mm"), sem("tr_ready"), sem("s_ready"), sem("pv_done")
        h_ready, flog_ready, d_ready = sem("h_ready"), sem("flog_ready"), sem("d_ready")
        selt_mm, bd_ready, u_ready = sem("selt_mm"), sem("bd_ready"), sem("u_ready")
        mout_ready, rlog_ready = sem("mout_ready"), sem("rlog_ready")
        tanh_done, xt_ready, exp_done = sem("tanh_done"), sem("xt_ready"), sem("exp_done")
        gelu_done, fexp_done, selt_done = sem("gelu_done"), sem("fexp_done"), sem("selt_done")
        silu1_done, silu2_done, xn_saved = sem("silu1_done"), sem("silu2_done"), sem("xn_saved")
        dve_step, waits_passed = sem("dve_step"), sem("waits_passed")
        picks_ready, place_mm, cnt_mm, cnt_ready = sem("picks_ready"), sem("place_mm"), sem("cnt_mm"), sem("cnt_ready")
        eb_ready, expert_mm, expert_ready, rows_ready = sem("eb_ready"), sem("expert_mm"), sem("expert_ready"), sem("rows_ready")
        gdiff_ready, gexp_done, pad_ready = sem("gdiff_ready"), sem("gexp_done"), sem("pad_ready")
        scattered = [sem(f"scattered{k}") for k in range(HALVES)]
        gathered = [sem(f"gathered{k}") for k in range(HALVES * TH // T)]
        xb_loaded = [sem(f"xb_loaded{u}") for u in range(2)]
        yb_stored = [sem(f"yb_stored{u}") for u in range(2)]
        xbt_mm, xbt_ready, hb_mm, hb_ready = sem("xbt_mm"), sem("xbt_ready"), sem("hb_mm"), sem("hb_ready")
        hbt_mm, hbt_ready, yb_mm, yb_ready = sem("hbt_mm"), sem("hbt_ready"), sem("yb_mm"), sem("yb_ready")
        out_ready, out_stored = sem("out_ready"), sem("out_stored")

        N_SETUP_LOADS = 23
        LN = ("attention", "experts8", "ssm", "router")
        TR = 2 * 2 * len(LN)
        SJ = 2 * 2 * T

        def count(it, half, n, k):
            return it * n + (half * PAIRS * n + k)

        def row(v):
            return v.rearrange("(a n) -> a n", a=1)

        def bcast_rows(v, n):
            return row(v).to_broadcast([n, v.shape[0]])

        def alone(eng):
            eng.sem_inc(waits_passed, 1)

        block = ctx.enter_context(nc.Block())

        @block.sync
        def _(sp):
            sp.dma_start(ids[:, :], a["x"].rearrange("b (t p) -> (b t) p", p=P)).then_inc(ids_loaded, 16)
            loads = [
                (emb[:, 0:D], a["L0_tok_emb1"]), (emb[:, D:2 * D], a["L0_tok_emb2"]),
                (tok_w[:, :], a["L0_tok_W"]), (tok_b[:, :], bcast_rows(a["L0_tok_b"], P)),
                (ffn_w1[:, :], a["L0_ffn_W1"]), (ffn_bg[:, :], bcast_rows(a["L0_ffn_bg"], P)),
                (ssm_w1[:, :], a["L1_attn_w1"]), (ssm_w2[:, :], a["L1_attn_w2"]),
                (ssm_b2[:, :], bcast_rows(a["L1_attn_b2"], P)),
                (ssm_taps[:, :], a["L1_attn_wd"].rearrange("e a k -> e (a k)")),
                (ssm_bc[:, 0, :], a["L1_attn_Bm"]), (ssm_bc[:, 1, :], a["L1_attn_Cm"]),
                (moe_wr[:, :], a["L1_ffn_Wr"]), (moe_br[:, :], bcast_rows(a["L1_ffn_br"], P)),
                (ffn_wg[:, :, :], a["L0_ffn_Wg"].rearrange("(c p) e -> p c e", p=P)),
            ]
            for i, name in enumerate(("b1", "bd", "gamma", "beta", "rmean", "rvar", "A", "Dv")):
                loads.append((ssm_col[:, i:i + 1], a["L1_attn_" + name].rearrange("(p a) -> p a", a=1)))
            assert len(loads) == N_SETUP_LOADS
            for dst, src in loads:
                sp.dma_start(dst, src).then_inc(w_loaded, 16)
            for c in range(CH):
                sp.dma_start(ffn_b1[:, c:c + 1], a["L0_ffn_b1"].rearrange("(c p a) -> c p a", p=P, a=1)[c]).then_inc(bd_loaded, 16)
                sp.dma_start(ffn_wd[:, c, :, :], a["L0_ffn_Wd"][:, c * P:(c + 1) * P, :].rearrange("e p d -> p e d")).then_inc(bd_loaded, 16)
            sp.wait_ge(bd_zero, 1)
            for t in range(T):
                sp.dma_start(ffn_bd[t * E8:(t + 1) * E8, t, :], a["L0_ffn_bd"]).then_inc(bd_loaded, 16)
            sp.wait_ge(ids_ready, 1)
            for k in range(2):
                sp.dma_start(idx_dram[k, :].rearrange("(t p) -> t p", p=P), ids_b[:, k, :]).then_inc(idx_stored, 16)
            sp.wait_ge(idx_stored, 32)
            for k in range(2):
                sp.dma_start(idx_all[:, k, :], bcast_rows(idx_dram[k, 0:TH * P], P)).then_inc(idx_loaded, 16)
            sp.dma_start(moe_w1[0:D, :, :], a["L1_ffn_W1"].rearrange("e k n -> k e n")).then_inc(moe_loaded, 16)
            sp.dma_start(moe_w1[D:W65, :, :], a["L1_ffn_b1"].rearrange("(a e) n -> a e n", a=1)).then_inc(moe_loaded, 16)
            sp.dma_start(moe_w2[:, :, :], a["L1_ffn_W2"].rearrange("e k n -> k e n")).then_inc(moe_loaded, 16)
            sp.dma_start(moe_b2[:, :, :].rearrange("p e d -> p (e d)"),
                         bcast_rows(a["L1_ffn_b2"].rearrange("e d -> (e d)"), P)).then_inc(moe_loaded, 16)
            sp.wait_ge(zero_ready, 1)
            per = SLOTS * D // P // 2048
            for k in range(HALVES):
                for i in range(per):
                    sp.dma_start(xs_dram[k][:, :].rearrange("(p r) d -> p (r d)", p=P)[:, i * 2048:(i + 1) * 2048],
                                 zeros).then_inc(zero_stored, 16)
            sp.wait_ge(hot_ready, 2 * PAIRS)
            for k in range(2):
                sp.dma_start(idx_all[:, k, :], bcast_rows(idx_dram[k, TH * P:2 * TH * P], P)).then_inc(idx_loaded, 16)

            for half in range(HALVES):
                src = xs_dram[half][:, :].rearrange("(g p j) d -> g p (j d)", p=P, j=GROUP)
                dst = ys_dram[half][:, :].rearrange("(g p j) d -> g p (j d)", p=P, j=GROUP)
                n = GROUPS // 2
                if half == 0:
                    sp.wait_ge(expert_ready, HALVES)
                sp.wait_ge(scattered[half], 16 * TOP * TH)

                def load(i, u):
                    sp.dma_start(xb[:, u, :, :].rearrange("p j d -> p (j d)"),
                                 src[bass.ds(2 * i + u, 1)].rearrange("a p n -> p (a n)")).then_inc(xb_loaded[u], 16)

                def store(i, u):
                    sp.wait_ge(yb_ready, 2 * i + (half * GROUPS + u + 1))
                    sp.dma_start(dst[bass.ds(2 * i + u, 1)].rearrange("a p n -> p (a n)"),
                                 yb[:, u, :, :].rearrange("p j d -> p (j d)")).then_inc(yb_stored[u], 16)

                for u in range(2):
                    if half:
                        sp.wait_ge(xbt_mm, half * GROUPS - 1 + u)
                    load(0, u)
                with sp.Fori(0, n - 1) as i:
                    for u in range(2):
                        sp.wait_ge(xbt_mm, 2 * i + (half * GROUPS + u + 1))
                        load(i + 1, u)
                    for u in range(2):
                        store(i, u)
                for u in range(2):
                    store(n - 1, u)

            out_v = out.rearrange("b (t p) d -> b p t d", p=P)
            for g in range(SEQS):
                sp.wait_ge(out_ready, g + 1)
                sp.dma_start(out_v[g], h_all[:, g * T:(g + 1) * T, :]).then_inc(out_stored, 16)
            sp.wait_ge(zero_stored, 16 * HALVES * per)
            sp.wait_ge(out_stored, 16 * SEQS)

        @block.gpsimd
        def _(pool):
            pool.memset(ident[:, :], 0.0).then_inc(consts, 1)
            pool.memset(before[:, :], 1.0).then_inc(consts, 1)
            pool.memset(ones[:, :], 1.0).then_inc(consts, 1)
            pool.wait_ge(consts, 3)
            pool.affine_select(out=ident[:, :], in_=ident[:, :], compare_op=ALU.not_equal, fill=1.0,
                               base=0, pattern=[[-1, P]], channel_multiplier=1).then_inc(consts, 1)
            pool.affine_select(out=before[:, :], in_=before[:, :], compare_op=ALU.is_gt, fill=0.0,
                               base=0, pattern=[[1, P]], channel_multiplier=-1).then_inc(consts, 1)
            pool.iota(iota_p[:, :], [[0, 1]], base=0, channel_multiplier=1,
                      allow_small_or_imprecise_dtypes=True).then_inc(consts, 1)
            pool.iota(iota_e[:, :], [[1, EX]], base=0, channel_multiplier=0,
                      allow_small_or_imprecise_dtypes=True).then_inc(consts, 1)
            pool.iota(rank_e8[:, :], [[-1, E8]], base=E8, channel_multiplier=0,
                      allow_small_or_imprecise_dtypes=True).then_inc(consts, 1)
            pool.wait_ge(bn_var, 2)
            pool.tensor_tensor(ssm_bn[:, 5:6], ssm_bn[:, 4:5], ssm_bn[:, 3:4], ALU.pow).then_inc(bn_rstd, 1)
            for half in range(HALVES):
                pool.wait_ge(rows_ready, half + 1)
                pool.wait_ge(xn_saved, 2 * PAIRS * (half + 1))
                if half == 0:
                    pool.wait_ge(zero_stored, 16 * HALVES * (SLOTS * D // P // 2048))
                for t in range(TH):
                    for k in range(TOP):
                        pool.indirect_dma_start(
                            out=xs_dram[half][:, :],
                            out_offset=bass.IndirectOffsetOnAxis(ap=rows[half][:, k, t:t + 1], axis=0),
                            in_=xn_all[:, half * TH + t, :], in_offset=None).then_inc(scattered[half], 16)
            for half in range(HALVES):
                if half == 0:
                    pool.wait_ge(scattered[1], 16 * TOP * TH)
                for u in range(2):
                    pool.wait_ge(yb_stored[u], 16 * (half + 1) * GROUPS // 2 + 16)
                for t in range(TH):
                    for k in range(TOP):
                        pool.indirect_dma_start(
                            out=yg[half][:, k, t, :], out_offset=None, in_=ys_dram[half][:, :],
                            in_offset=bass.IndirectOffsetOnAxis(ap=rows[half][:, k, t:t + 1], axis=0)
                        ).then_inc(gathered[(half * TH + t) // T], 16)

        @block.scalar
        def _(act):
            for i in range(2):
                act.wait_ge(setup_t, 4)
            act.activation(emb_t[:, :], trp[0][:, 0:P], ACT.Copy).then_inc(setup_c, 1)
            act.activation(tok_wt[:, :], trp[0][:, P:P + D], ACT.Copy).then_inc(setup_c, 1)
            act.activation(ssm_w1t[:, :], trp[0][0:D, 2 * P:3 * P], ACT.Copy).then_inc(setup_c, 1)
            act.wait_ge(w_loaded, 16 * N_SETUP_LOADS)
            act.activation(ssm_bn[:, 2:3], ssm_col[:, 6:7], ACT.Exp).then_inc(decay_ready, 1)

            def evacuate(it, half, stage, s):
                for g in range(2):
                    n = (stage * 2 + s) * 2 + g
                    act.wait_ge(tr_ready, count(it, half, TR, n + 1))
                    act.activation(xt[s][:, g * 512:(g + 1) * 512], trp[g][0:D, :], ACT.Copy).then_inc(xt_ready, 1)

            def main(it, half):
                for s in range(2):
                    act.wait_ge(tok_mm, count(it, half, 2, s + 1))
                    act.activation(h[s][:, :, :].rearrange("p t d -> p (t d)"), outp[s][:, :], ACT.Tanh).then_inc(tanh_done, 1)
                for s in range(2):
                    evacuate(it, half, 0, s)
                    for i in range(2 * T):
                        j = s * 2 * T + i
                        act.wait_ge(s_ready, count(it, half, SJ, j + 1))
                        if j >= 4:
                            act.wait_ge(pv_done, count(it, half, SJ, j - 3))
                        act.activation(ering[:, j % 4, :], wide[j % 4][:, :], ACT.Exp, scale=D ** -0.5).then_inc(exp_done, 1)
                for s in range(2):
                    evacuate(it, half, 1, s)
                    for c in range(CH):
                        for g in range(2):
                            q = (s * CH + c) * 2 + g
                            act.wait_ge(h_ready, count(it, half, 8, q + 1))
                            act.activation(ht[:, s, c, g * 512:(g + 1) * 512], wide[q % 4][:, :], ACT.Gelu,
                                           bias=ffn_b1[:, c:c + 1]).then_inc(gelu_done, 1)
                for s in range(2):
                    act.wait_ge(fd_ready, count(it, half, 2, s + 1))
                    act.activation(fe[s][:, :, :], fd[s][:, :, :], ACT.Exp).then_inc(fexp_done, 1)
                    act.wait_ge(selt_mm, count(it, half, 2, s + 1))
                    act.activation(selt[s][:, :], outp[s][0:T * E8, 64:64 + P], ACT.Copy).then_inc(selt_done, 1)
                for s in range(2):
                    evacuate(it, half, 2, s)
                    for g in range(2):
                        act.wait_ge(u_ready, count(it, half, 4, s * 2 + g + 1))
                        act.activation(up[:, s, pad + g * 512:pad + (g + 1) * 512], wide[s * 2 + g][:, :], ACT.Silu,
                                       bias=ssm_col[:, 0:1]).then_inc(silu1_done, 1)
                for s in range(2):
                    act.wait_ge(conv_done, count(it, half, 2, s + 1))
                    act.activation(ysilu[s], yconv[s], ACT.Silu, bias=ssm_bn[:, 1:2], scale=ssm_bn[:, 0:1]).then_inc(silu2_done, 1)
                for s in range(2):
                    evacuate(it, half, 3, s)
                    act.activation(xn_all[:, bass.ds((it * 2 + (half * 2 * PAIRS + s)) * T, T), :], xn[s][:, :, 0:D],
                                   ACT.Copy).then_inc(xn_saved, 1)

            act.wait_ge(setup_done, 1)
            act.wait_ge(bd_loaded, 16 * (2 * CH + T))
            for half in range(HALVES):
                with act.Fori(0, PAIRS) as it:
                    main(it, half)
                for k in range(4):
                    act.wait_ge(cnt_mm, 4 * half + k + 1)
                    bank = (trp + outp)[k]
                    act.activation(cnt[:, 16 * k:16 * (k + 1), 1:TH + 1],
                                   bank[:, :].rearrange("p (e t) -> p e t", t=TH), ACT.Copy).then_inc(cnt_ready, 1)
                act.wait_ge(gdiff_ready, half + 1)
                act.activation(gates[:, half * TH:(half + 1) * TH, 2], gates[:, half * TH:(half + 1) * TH, 2],
                               ACT.Exp).then_inc(gexp_done, 1)
            for half in range(HALVES):
                with act.Fori(0, GROUPS // 2) as i:
                    for u in range(2):
                        act.wait_ge(xbt_mm, 2 * i + (half * GROUPS + u + 1))
                        act.activation(xbt[0:D, u, :], trp[u][0:D, :], ACT.Copy).then_inc(xbt_ready, 1)
                    for u in range(2):
                        act.wait_ge(hbt_mm, 2 * i + (half * GROUPS + u + 1))
                        act.activation(hbt[:, u, :], wide[2 + u][:, :], ACT.Copy).then_inc(hbt_ready, 1)

        @block.tensor
        def _(pe):
            pe.wait_ge(consts, 8)
            pe.wait_ge(w_loaded, 16 * N_SETUP_LOADS)
            pe.transpose(trp[0][:, 0:P], emb[:, :], ident[:, :]).then_inc(setup_t, 1)
            pe.transpose(trp[0][:, P:P + D], tok_w[:, :], ident[0:D, 0:D]).then_inc(setup_t, 1)
            pe.transpose(trp[0][0:D, 2 * P:3 * P], ssm_w1[:, :], ident[:, :]).then_inc(setup_t, 1)
            pe.transpose(trp[1][:, 0:D], ssm_w2[:, :], ident[0:D, 0:D]).then_inc(setup_t, 1)
            pe.wait_ge(setup_c, 2)
            for k in range(2):
                pe.matmul(outp[k][:, 0:D], emb_t[k * D:(k + 1) * D, :], tok_wt[k * D:(k + 1) * D, :],
                          start=True, stop=True).then_inc(table_mm, 1)
            pe.wait_ge(table_ready, 1)
            pe.wait_ge(setup_c, 3)
            pe.wait_ge(setup_done, 1)
            pe.wait_ge(bd_loaded, 16 * (2 * CH + T))

            def transposes(it, half, stage, s):
                pe.wait_ge(xn_ready, count(it, half, 8, stage * 2 + s + 1))
                for g in range(2):
                    n = (stage * 2 + s) * 2 + g
                    if n >= 2:
                        pe.wait_ge(xt_ready, count(it, half, TR, n - 1))
                    alone(pe)
                    for t in range(4):
                        last = pe.transpose(trp[g][0:D, t * P:(t + 1) * P], xn[s][:, g * 4 + t, 0:D], ident[:, :])
                    last.then_inc(tr_ready, 1)

            def xt_there(it, half, stage, s):
                pe.wait_ge(xt_ready, count(it, half, TR, (stage * 2 + s) * 2 + 2))

            def main(it, half):
                for s in range(2):
                    pe.wait_ge(hot_ready, count(it, half, 2, s + 1))
                    for t in range(T):
                        for k in range(2):
                            for part in range(3):
                                last = pe.matmul(outp[s][:, t * D:(t + 1) * D], hot[s][:, k, t * P:(t + 1) * P],
                                                 table_parts[:, part, k, :], start=(k + part == 0), stop=(k + part == 3))
                    last.then_inc(tok_mm, 1)
                for s in range(2):
                    transposes(it, half, 0, s)
                    xt_there(it, half, 0, s)

                    def scores(i):
                        j = s * 2 * T + i
                        if j >= 4:
                            pe.wait_ge(exp_done, count(it, half, SJ, j - 3))
                        m, g = i % T, i // T
                        pe.matmul(wide[j % 4][:, :], xt[s][:, m * P:(m + 1) * P], xt[s][:, g * 512:(g + 1) * 512],
                                  start=True, stop=True).then_inc(s_ready, 1)

                    def weighted(i):
                        j = s * 2 * T + i
                        m, g = i % T, i // T
                        pe.wait_ge(exp_done, count(it, half, SJ, j + 1))
                        if m == 0 and g == 1:
                            pe.wait_ge(ctx_done, count(it, half, 4, s * 2 + 1))
                        for n in range(4):
                            last = pe.matmul(outp[s][:, n * W65:(n + 1) * W65], ering[:, j % 4, n * P:(n + 1) * P],
                                             xn[s][:, m, :], start=(m == 0 and n == 0), stop=(m == T - 1),
                                             skip_group_check=True)
                        last.then_inc(pv_done, 1)

                    lag = 2
                    for i in range(2 * T + lag):
                        if i < 2 * T:
                            scores(i)
                        if i >= lag:
                            weighted(i - lag)
                for s in range(2):
                    transposes(it, half, 1, s)
                    xt_there(it, half, 1, s)
                    for c in range(CH):
                        for g in range(2):
                            q = (s * CH + c) * 2 + g
                            if q >= 4:
                                pe.wait_ge(gelu_done, count(it, half, 8, q - 3))
                            pe.matmul(wide[q % 4][:, :], ffn_w1[:, c * P:(c + 1) * P], xt[s][:, g * 512:(g + 1) * 512],
                                      start=True, stop=True).then_inc(h_ready, 1)
                pe.wait_ge(gelu_done, count(it, half, 8, 8))
                for s in range(2):
                    for t in range(T):
                        for c in range(CH):
                            last = pe.matmul(outp[s][:, t * E8:(t + 1) * E8], ht[:, s, c, t * P:(t + 1) * P],
                                             ffn_wg[:, c, :], start=(c == 0), stop=(c == CH - 1))
                    last.then_inc(flog_ready, 1)
                for s in range(2):
                    for t in range(T):
                        q = s * T + t
                        if q >= 4:
                            pe.wait_ge(d_done, count(it, half, 2 * T, q - 3))
                        for c in range(CH):
                            last = pe.matmul(wide[q % 4][:, :], ht[:, s, c, t * P:(t + 1) * P],
                                             ffn_wd[:, c, :, :].rearrange("p e d -> p (e d)"), start=(c == 0), stop=(c == CH - 1))
                        last.then_inc(d_ready, 1)
                    pe.wait_ge(selp_ready, count(it, half, 2, s + 1))
                    alone(pe)
                    pe.transpose(outp[s][0:T * E8, 64:64 + P], selp[s][:, :, :].rearrange("p t e -> p (t e)"), ident[:, :]).then_inc(selt_mm, 1)
                    pe.wait_ge(selt_done, count(it, half, 2, s + 1))
                    pe.matmul(outp[s][:, :], selt[s][:, :], ffn_bd[:, :, :].rearrange("p t d -> p (t d)"),
                              start=True, stop=True).then_inc(bd_ready, 1)
                for s in range(2):
                    transposes(it, half, 2, s)
                    xt_there(it, half, 2, s)
                    if s == 0:
                        pe.wait_ge(d_done, count(it, half, 2 * T, 2 * T))
                    for g in range(2):
                        pe.matmul(wide[s * 2 + g][:, :], ssm_w1t[:, :], xt[s][:, g * 512:(g + 1) * 512],
                                  start=True, stop=True).then_inc(u_ready, 1)
                for s in range(2):
                    pe.wait_ge(scan_done, count(it, half, 2, s + 1))
                    for t in range(T):
                        pe.matmul(outp[s][:, t * D:(t + 1) * D], gst[:, s, t * P:(t + 1) * P], ssm_w2bc[:, :],
                                  start=True, stop=False)
                        last = pe.matmul(outp[s][:, t * D:(t + 1) * D], ysilu[s][:, t * P:(t + 1) * P], ssm_w2d[:, :],
                                         start=False, stop=True)
                    last.then_inc(mout_ready, 1)
                for s in range(2):
                    transposes(it, half, 3, s)
                    xt_there(it, half, 3, s)
                    for t in range(T):
                        last = pe.matmul(outp[s][:, t * EX:(t + 1) * EX], xt[s][:, t * P:(t + 1) * P], moe_wr[:, :],
                                         start=True, stop=True)
                    last.then_inc(rlog_ready, 1)

            for half in range(HALVES):
                with pe.Fori(0, PAIRS) as it:
                    main(it, half)
                pe.wait_ge(picks_ready, half + 1)
                for k in range(4):
                    pe.matmul((trp + outp)[k][:, :], ones[:, :],
                              picks[:, :, 16 * k:16 * (k + 1)].rearrange("p t e -> p e t"),
                              start=True, stop=True).then_inc(cnt_mm, 1)
                for k in range(4):
                    pe.matmul(wide[k][:, :], before[:, :], picks[:, 8 * k:8 * (k + 1), :].rearrange("p t e -> p (t e)"),
                              start=True, stop=True).then_inc(place_mm, 1)
                pe.wait_ge(eb_ready, half + 1)
                pe.matmul(outp[0][0:1, 0:BLOCKS], eb[:, :], ident[:, 0:BLOCKS], start=True, stop=True).then_inc(expert_mm, 1)

            pe.wait_ge(expert_ready, HALVES)
            pe.wait_ge(moe_loaded, 64)
            pe.wait_ge(pad_ready, 1)
            for half in range(HALVES):
                with pe.Fori(0, GROUPS // 2) as i:
                    for u in range(2):
                        pe.wait_ge(xb_loaded[u], 16 * i + 16 * (half * GROUPS // 2 + 1))
                        alone(pe)
                        for j in range(GROUP):
                            last = pe.transpose(trp[u][0:D, j * P:(j + 1) * P], xb[:, u, j, :], ident[:, :])
                        last.then_inc(xbt_mm, 1)
                    for u in range(2):
                        es = [pe.value_load(expert[half][0:1, bass.ds(i * 2 * GROUP + (u * GROUP + j), 1)], min_val=0, max_val=EX - 1)
                              for j in range(GROUP)]
                        pe.wait_ge(xbt_ready, 2 * i + (half * GROUPS + u + 1))
                        for j, e in enumerate(es):
                            last = pe.matmul(wide[u][:, j * P:(j + 1) * P], xbt[:, u, j * P:(j + 1) * P],
                                             moe_w1[:, bass.ds(e, 1), :].rearrange("p a n -> p (a n)"), start=True, stop=True)
                        last.then_inc(hb_mm, 1)
                    for u in range(2):
                        pe.wait_ge(hb_ready, 2 * i + (half * GROUPS + u + 1))
                        for j in range(GROUP):
                            last = pe.transpose(wide[2 + u][:, j * P:(j + 1) * P], hb[:, u, j * P:(j + 1) * P], ident[:, :])
                        last.then_inc(hbt_mm, 1)
                    for u in range(2):
                        es = [pe.value_load(expert[half][0:1, bass.ds(i * 2 * GROUP + (u * GROUP + j), 1)], min_val=0, max_val=EX - 1)
                              for j in range(GROUP)]
                        pe.wait_ge(hbt_ready, 2 * i + (half * GROUPS + u + 1))
                        for j, e in enumerate(es):
                            last = pe.matmul(outp[u][:, j * D:(j + 1) * D], hbt[:, u, j * P:(j + 1) * P],
                                             moe_w2[:, bass.ds(e, 1), :].rearrange("p a n -> p (a n)"), start=True, stop=True)
                        last.then_inc(yb_mm, 1)

        @block.vector
        def _(dve):
            at = [0]
            base = [None]

            def step(ins):
                at[0] += 1
                ins.then_inc(dve_step, 1)
                dve.wait_ge(dve_step, at[0] if base[0] is None else base[0] + at[0])

            def looped(n, per, body):
                start = at[0]
                with dve.Fori(0, n) as it:
                    base[0] = it * per
                    body(it)
                    base[0] = None
                assert at[0] - start == per, at[0] - start
                at[0] = start + n * per

            step(dve.memset(ffn_bd[:, :, :], 0.0))
            dve.memset(zeros, 0.0).then_inc(zero_ready, 1)
            dve.sem_inc(bd_zero, 1)
            for s in range(2):
                step(dve.memset(xn[s][:, :, D:W65], 1.0))
            dve.wait_ge(ids_loaded, 16)
            step(dve.tensor_scalar(ids_i[:, 0, :], ids[:, :], 7, None, ALU.arith_shift_right))
            step(dve.tensor_scalar(ids_i[:, 1, :], ids[:, :], VOCAB - 1, None, ALU.bitwise_and))
            step(dve.tensor_copy(ids_f[:, 0, :], ids_i[:, 0, :]))
            step(dve.tensor_scalar(ids_f[:, 1, :], ids_f[:, 0, :], 0.0, float(VOCAB), ALU.is_lt, ALU.mult))
            step(dve.tensor_tensor(ids_f[:, 2, :], ids_f[:, 0, :], ids_f[:, 1, :], ALU.add))
            step(dve.tensor_scalar(ids_b[:, 0, :], ids_f[:, 2, :], 0.0, float(VOCAB - 1), ALU.max, ALU.min))
            dve.tensor_copy(ids_b[:, 1, :], ids_i[:, 1, :]).then_inc(ids_ready, 1)
            dve.wait_ge(w_loaded, 16 * N_SETUP_LOADS)
            dve.memset(ssm_bn[:, 3:4], -0.5).then_inc(bn_var, 1)
            dve.tensor_scalar(ssm_bn[:, 4:5], ssm_col[:, 5:6], BN_EPS, None, ALU.add).then_inc(bn_var, 1)
            dve.wait_ge(bn_rstd, 1)
            step(dve.tensor_tensor(ssm_bn[:, 0:1], ssm_bn[:, 5:6], ssm_col[:, 2:3], ALU.mult))
            step(dve.tensor_tensor(ssm_bn[:, 4:5], ssm_col[:, 1:2], ssm_col[:, 4:5], ALU.subtract))
            step(dve.tensor_tensor(ssm_bn[:, 4:5], ssm_bn[:, 4:5], ssm_bn[:, 0:1], ALU.mult))
            step(dve.tensor_tensor(ssm_bn[:, 1:2], ssm_bn[:, 4:5], ssm_col[:, 3:4], ALU.add))
            step(dve.tensor_tensor(ssm_bc[:, 0, :], ssm_bc[:, 0, :], ssm_bc[:, 1, :], ALU.mult))
            step(dve.tensor_reduce(ssm_bn[:, 3:4], ssm_bc[:, 0, :], AX, ALU.add))
            dve.wait_ge(setup_t, 4)
            step(dve.tensor_scalar(ssm_w2bc[:, :], trp[1][:, 0:D], ssm_bn[:, 3:4], None, ALU.mult))
            step(dve.tensor_scalar(ssm_w2d[:, :], trp[1][:, 0:D], ssm_col[:, 7:8], None, ALU.mult))
            dve.wait_ge(table_mm, 2)
            step(dve.tensor_copy(table[:, 0, :], outp[0][:, 0:D]))
            step(dve.tensor_tensor(table[:, 1, :], outp[1][:, 0:D], tok_b[:, :], ALU.add))
            for part in range(3):
                step(dve.tensor_copy(table_parts[:, part, :, :], table[:, :, :]))
                if part < 2:
                    step(dve.tensor_tensor(table[:, :, :], table[:, :, :], table_parts[:, part, :, :], ALU.subtract))
            dve.sem_inc(table_ready, 1)
            dve.wait_ge(decay_ready, 1)
            dve.wait_ge(consts, 8)
            dve.sem_inc(setup_done, 2)

            def bc(ap, shape):
                return ap.to_broadcast(shape)

            SH = [P, T, D]

            def layernorm(src, s):
                alone(dve)
                step(dve.tensor_reduce(stat[:, 0, :], src, AX, ALU.add))
                step(dve.tensor_scalar(stat[:, 0, :], stat[:, 0, :], 1.0 / D, None, ALU.mult))
                step(dve.tensor_tensor(xc[:, :, :], src, bc(stat[:, 0, :].unsqueeze(2), SH), ALU.subtract))
                step(dve.tensor_tensor(sq[:, :, :], xc[:, :, :], xc[:, :, :], ALU.mult))
                step(dve.tensor_reduce(stat[:, 1, :], sq[:, :, :], AX, ALU.add))
                step(dve.tensor_scalar(stat[:, 1, :], stat[:, 1, :], 1.0 / D, LN_EPS, ALU.mult, ALU.add))
                step(dve.tensor_scalar(stat_i[:, :], stat[:, 1, :].bitcast(I32), 1, None, ALU.arith_shift_right))
                step(dve.tensor_scalar(stat[:, 2, :].bitcast(I32), stat_i[:, :], -1.0, float(RSQRT_SEED), ALU.mult, ALU.add))
                for _ in range(3):
                    step(dve.scalar_tensor_tensor(stat[:, 3, :], stat[:, 2, :], -0.5, stat[:, 2, :], ALU.mult, ALU.mult))
                    step(dve.tensor_tensor(stat[:, 3, :], stat[:, 3, :], stat[:, 1, :], ALU.mult))
                    step(dve.scalar_tensor_tensor(stat[:, 2, :], stat[:, 3, :], 1.5, stat[:, 2, :], ALU.add, ALU.mult))
                step(dve.tensor_tensor(xn[s][:, :, 0:D], xc[:, :, :], bc(stat[:, 2, :].unsqueeze(2), SH), ALU.mult))
                dve.sem_inc(xn_ready, 1)

            def main(it, half):
                for s in range(2):
                    step(dve.tensor_scalar(hot[s][:, :, :], idx_all[:, :, bass.ds((it * 2 + s) * SEQ, SEQ)], iota_p[:, 0:1], None, ALU.is_equal))
                    dve.sem_inc(hot_ready, 1)
                for s in range(2):
                    dve.wait_ge(tanh_done, count(it, half, 2, s + 1))
                    layernorm(h[s][:, :, :], s)
                for s in range(2):
                    for g in range(2):
                        dve.wait_ge(pv_done, count(it, half, SJ, s * 2 * T + (g + 1) * T))
                        o = outp[s][:, 0:4 * W65].rearrange("p (t d) -> p t d", d=W65)
                        step(dve.reciprocal(stat[:, 4, 0:4], o[:, :, D]))
                        step(dve.tensor_tensor(acc[:, 0:4, :], o[:, :, 0:D], bc(stat[:, 4, 0:4].unsqueeze(2), [P, 4, D]), ALU.mult))
                        dve.sem_inc(ctx_done, 1)
                        step(dve.tensor_tensor(h[s][:, 4 * g:4 * g + 4, :], h[s][:, 4 * g:4 * g + 4, :], acc[:, 0:4, :], ALU.add))
                    layernorm(h[s][:, :, :], s)
                G = [P, T, E8]
                for s in range(2):
                    dve.wait_ge(flog_ready, count(it, half, 2, s + 1))
                    lo = outp[s][:, 0:T * E8].rearrange("p (t e) -> p t e", e=E8)
                    step(dve.tensor_tensor(gate[:, 0, :, :], lo, bc(ffn_bg[:, :].unsqueeze(1), G), ALU.add))
                    step(dve.tensor_reduce(gate1[:, 0, :], gate[:, 0, :, :], AX, ALU.max))
                    step(dve.tensor_tensor(fd[s][:, :, :], gate[:, 0, :, :], bc(gate1[:, 0, :].unsqueeze(2), G), ALU.subtract))
                    dve.sem_inc(fd_ready, 1)
                    step(dve.tensor_scalar(gate[:, 1, :, :], fd[s][:, :, :], 0.0, None, ALU.is_equal))
                    step(dve.tensor_tensor(gate[:, 1, :, :], gate[:, 1, :, :], bc(rank_e8[:, :].unsqueeze(1), G), ALU.mult))
                    step(dve.tensor_reduce(gate1[:, 1, :], gate[:, 1, :, :], AX, ALU.max))
                    step(dve.tensor_tensor(gate[:, 2, :, :], gate[:, 1, :, :], bc(gate1[:, 1, :].unsqueeze(2), G), ALU.is_equal))
                    dve.wait_ge(fexp_done, count(it, half, 2, s + 1))
                    step(dve.tensor_reduce(gate1[:, 2, :], fe[s][:, :, :], AX, ALU.add))
                    step(dve.reciprocal(gate1[:, 3, :], gate1[:, 2, :]))
                    step(dve.tensor_tensor(selp[s][:, :, :], gate[:, 2, :, :], bc(gate1[:, 3, :].unsqueeze(2), G), ALU.mult))
                    dve.sem_inc(selp_ready, 1)
                    for t in range(T):
                        dve.wait_ge(d_ready, count(it, half, 2 * T, s * T + t + 1))
                        step(dve.tensor_tensor(dtmp[:, t % 2, :, :], wide[t % 4][:, :].rearrange("p (e d) -> p e d", d=D),
                                               bc(selp[s][:, t, :].unsqueeze(2), [P, E8, D]), ALU.mult))
                        dve.sem_inc(d_done, 1)
                        step(dve.tensor_reduce(acc[:, t, :], dtmp[:, t % 2, :, :].rearrange("p e d -> p d e"), AX, ALU.add))
                    step(dve.tensor_tensor(h[s][:, :, :], h[s][:, :, :], acc[:, :, :], ALU.add))
                    dve.wait_ge(bd_ready, count(it, half, 2, s + 1))
                    step(dve.tensor_tensor(h[s][:, :, :], outp[s][:, :].rearrange("p (t d) -> p t d", d=D), h[s][:, :, :], ALU.add))
                    layernorm(h[s][:, :, :], s)
                for s in range(2):
                    dve.wait_ge(silu1_done, count(it, half, 4, 2 * s + 2))
                    step(dve.tensor_scalar(yconv[s], up[:, s, 0:SEQ], ssm_taps[:, 0:1], None, ALU.mult))
                    for k in range(1, TAPS):
                        step(dve.scalar_tensor_tensor(yconv[s], up[:, s, k:k + SEQ], ssm_taps[:, k:k + 1], yconv[s], ALU.mult, ALU.add))
                    dve.sem_inc(conv_done, 1)
                for s in range(2):
                    dve.wait_ge(silu2_done, count(it, half, 2, s + 1))
                    step(dve.tensor_tensor_scan(gst[:, s, 0:SEQ], bc(ssm_bn[:, 2:3], [P, SEQ]), ysilu[s], 0.0, ALU.mult, ALU.add))
                    dve.sem_inc(scan_done, 1)
                for s in range(2):
                    tiles = bass.ds((it * 2 + (half * 2 * PAIRS + s)) * T, T)
                    dve.wait_ge(mout_ready, count(it, half, 2, s + 1))
                    step(dve.tensor_tensor(h[s][:, :, :], outp[s][:, :].rearrange("p (t d) -> p t d", d=D), h[s][:, :, :], ALU.add))
                    step(dve.tensor_tensor(h_all[:, tiles, :], h[s][:, :, :], bc(ssm_b2[:, :].unsqueeze(1), SH), ALU.add))
                    layernorm(h_all[:, tiles, :], s)
                for s in range(2):
                    tiles = bass.ds((it * 2 + (half * 2 * PAIRS + s)) * T, T)
                    dve.wait_ge(rlog_ready, count(it, half, 2, s + 1))
                    step(dve.tensor_tensor(lg[s][:, :, :], outp[s][:, :].rearrange("p (t e) -> p t e", e=EX),
                                           bc(moe_br[:, :].unsqueeze(1), [P, T, EX]), ALU.add))
                    for t in range(T):
                        alone(dve)
                        step(dve.max(v8[s][:, t, :], lg[s][:, t, :]))
                        alone(dve)
                        step(dve.max_index(i8[s][:, t, :], v8[s][:, t, :], lg[s][:, t, :]))
                    step(dve.tensor_copy(top_val[:, tiles, :], v8[s][:, :, 0:TOP]))
                    step(dve.tensor_copy(top_idx[:, tiles, :], i8[s][:, :, 0:TOP]))

            dve.wait_ge(bd_loaded, 16 * (2 * CH + T))
            dve.wait_ge(zero_stored, 16 * HALVES * (SLOTS * D // P // 2048))
            for half in range(HALVES):
                dve.wait_ge(idx_loaded, 32 * (half + 1))
                for s in range(2):
                    step(dve.memset(up[:, s, 0:pad], 0.0))
                    step(dve.memset(up[:, s, pad + SEQ:2 * pad + SEQ], 0.0))
                looped(PAIRS, DVE_MAIN, lambda it, half=half: main(it, half))
                tiles = slice(half * TH, (half + 1) * TH)
                OH = [P, TH, EX]
                for k in range(TOP):
                    step(dve.tensor_tensor(pick[k], bc(iota_e[:, :].unsqueeze(1), OH),
                                           bc(top_idx[:, tiles, k].unsqueeze(2), OH), ALU.is_equal))
                step(dve.tensor_tensor(picks, pick[0], pick[1], ALU.add))
                dve.sem_inc(picks_ready, 1)
                step(dve.tensor_tensor(gates[:, tiles, 2], top_val[:, tiles, 1], top_val[:, tiles, 0], ALU.subtract))
                dve.sem_inc(gdiff_ready, 1)
                step(dve.memset(seg_keep[:, :, :], 1.0))
                step(dve.memset(seg_keep[:, :, 0:1], 0.0))
                step(dve.memset(cnt[:, :, 0:1], 0.0))
                dve.wait_ge(cnt_ready, 4 * (half + 1))
                step(dve.tensor_tensor_scan(cum[:, :, :].rearrange("p e t -> p (e t)"), seg_keep[:, :, :].rearrange("p e t -> p (e t)"),
                                            cnt[:, :, :].rearrange("p e t -> p (e t)"), 0.0, ALU.mult, ALU.add))
                step(dve.tensor_scalar(nb_i[:, :], cum[:, :, TH], float(P - 1), None, ALU.add))
                step(dve.tensor_scalar(nb_i[:, :], nb_i[:, :], 7, None, ALU.arith_shift_right))
                step(dve.tensor_copy(nb[:, 0, :], nb_i[:, :]))
                step(dve.tensor_tensor_scan(nb[:, 1, :], bc(seg_keep[:, 0, 1:2], [P, EX]), nb[:, 0, :], 0.0, ALU.mult, ALU.add))
                step(dve.tensor_tensor(nb[:, 2, :], nb[:, 1, :], nb[:, 0, :], ALU.subtract))
                step(dve.tensor_scalar(nb[:, 4, :], nb[:, 2, :], iota_p[:, 0:1], None, ALU.is_le))
                step(dve.tensor_reduce(eb[:, :], nb[:, 4, :], AX, ALU.add))
                dve.sem_inc(eb_ready, 1)
                step(dve.tensor_scalar(nb[:, 3, :], nb[:, 2, :], float(P), None, ALU.mult))
                for k in range(4):
                    dve.wait_ge(place_mm, 4 * half + k + 1)
                    step(dve.tensor_tensor(place[:, 8 * k:8 * (k + 1), :], wide[k][:, :].rearrange("p (t e) -> p t e", e=EX),
                                           cum[:, :, 8 * k:8 * (k + 1)].rearrange("p e t -> p t e"), ALU.add))
                step(dve.tensor_tensor(place, place, bc(nb[:, 3, :].unsqueeze(1), OH), ALU.add))
                for k in range(TOP):
                    step(dve.tensor_tensor(prod, place, pick[k], ALU.mult))
                    step(dve.tensor_reduce(slot_f[:, k, :], prod, AX, ALU.add))
                step(dve.tensor_copy(slot_i[:, 0, :, :], slot_f[:, :, :]))
                step(dve.tensor_scalar(slot_i[:, 1, :, :], slot_i[:, 0, :, :], ~(GROUP * P - 1), None, ALU.bitwise_and))
                step(dve.tensor_scalar(slot_i[:, 2, :, :], slot_i[:, 0, :, :], P - 1, 2, ALU.bitwise_and, ALU.logical_shift_left))
                step(dve.tensor_scalar(slot_i[:, 3, :, :], slot_i[:, 0, :, :], 7, GROUP - 1, ALU.logical_shift_right, ALU.bitwise_and))
                step(dve.tensor_tensor(slot_i[:, 1, :, :], slot_i[:, 1, :, :], slot_i[:, 2, :, :], ALU.bitwise_or))
                step(dve.tensor_tensor(rows[half][:, :, :], slot_i[:, 1, :, :], slot_i[:, 3, :, :], ALU.bitwise_or))
                dve.sem_inc(rows_ready, 1)
                dve.wait_ge(gexp_done, half + 1)
                step(dve.tensor_scalar(gates[:, tiles, 0], gates[:, tiles, 2], 1.0, None, ALU.add))
                step(dve.reciprocal(gates[:, tiles, 0], gates[:, tiles, 0]))
                step(dve.tensor_tensor(gates[:, tiles, 1], gates[:, tiles, 2], gates[:, tiles, 0], ALU.mult))
                dve.wait_ge(expert_mm, half + 1)
                step(dve.tensor_scalar(expert[half][:, :], outp[0][0:1, 0:BLOCKS], -1.0, None, ALU.add))
                dve.sem_inc(expert_ready, 1)

            dve.memset(xbt[D:W65, :, :], 1.0).then_inc(pad_ready, 1)
            for u in range(2):
                dve.sem_inc(yb_stored[u], 16)
            dve.wait_ge(moe_loaded, 64)
            for half in range(HALVES):
                with dve.Fori(0, GROUPS // 2) as i:
                    for u in range(2):
                        dve.wait_ge(hb_mm, 2 * i + (half * GROUPS + u + 1))
                        dve.tensor_scalar(hb[:, u, :], wide[u][:, :], 0.0, None, ALU.max).then_inc(hb_ready, 1)
                    for u in range(2):
                        es = [dve.value_load(expert[half][0:1, bass.ds(i * 2 * GROUP + (u * GROUP + j), 1)], min_val=0, max_val=EX - 1)
                              for j in range(GROUP)]
                        dve.wait_ge(yb_mm, 2 * i + (half * GROUPS + u + 1))
                        dve.wait_ge(yb_stored[u], 16 * i + 16 * (half * GROUPS // 2 + 1))
                        for j, e in enumerate(es):
                            last = dve.tensor_tensor(yb[:, u, j, :], outp[u][:, j * D:(j + 1) * D],
                                                     moe_b2[:, bass.ds(e, 1), :].rearrange("p a n -> p (a n)"), ALU.add)
                        last.then_inc(yb_ready, 1)
            for g in range(SEQS):
                half, t0 = g * T // TH, g * T % TH
                tiles = slice(g * T, (g + 1) * T)
                dve.wait_ge(gathered[g], 16 * TOP * T)
                for k in range(TOP):
                    y = yg[half][:, k, t0:t0 + T, :]
                    step(dve.tensor_tensor(y, y, bc(gates[:, tiles, k].unsqueeze(2), SH), ALU.mult))
                    step(dve.tensor_tensor(h_all[:, tiles, :], h_all[:, tiles, :], y, ALU.add))
                dve.sem_inc(out_ready, 1)


DVE_MAIN = 268


def kernel(**inputs):
    import numpy as _np
    import concourse.bacc as _bacc
    from concourse import mybir as _mybir
    from concourse.bass_utils import run_bass_kernel_spmd as _run

    nc = _bacc.Bacc("TRN2", target_bir_lowering=False, num_devices=1)
    arrays, handles = {}, {}
    for name, v in inputs.items():
        v = _np.ascontiguousarray(v)
        arrays[f"in_{name}"] = v
        handles[name] = nc.dram_tensor(f"in_{name}", v.shape, _mybir.dt.from_np(v.dtype), kind="ExternalInput").ap()
    result = nc.dram_tensor("out_0", (SEQS, SEQ, D), F32, kind="ExternalOutput").ap()
    lm_tower(nc, handles, result)
    r = _run(nc, [arrays], core_ids=[0])
    return r.results[0]["out_0"]
```

```python
from contextlib import ExitStack

import concourse.bass as bass
from concourse import mybir

ALU = mybir.AluOpType
ACT = mybir.ActivationFunctionType
AX = mybir.AxisListType.X
F32 = mybir.dt.float32
BF16 = mybir.dt.bfloat16
F16 = mybir.dt.float16
I32 = mybir.dt.int32
U32 = mybir.dt.uint32

P = 128
D = 64
SEQS, SEQ = 8, 1024
T = SEQ // P
HALVES = 2
PAIRS = SEQS // 2 // HALVES
TH = SEQS * T // HALVES
VOCAB = 128
HID = 256
CH = HID // P
E8 = 8
TAPS = 5
STATE = 8
EX = 64
HID2 = 128
TOP = 2
LN_EPS = 1e-5
BN_EPS = 1e-5
BLOCKS = TH * P * TOP // P + EX
GROUP = 4
GROUPS = BLOCKS // GROUP
SLOTS = BLOCKS * P
W65 = D + 1
PARTS = 3
EX_BITS = 6
STAGE_E = 16
RSQRT_SEED = 0x5F3759DF


def lm_tower(nc, a, out):
    ctx = ExitStack()
    with ctx:
        def sb(name, shape, dt=F32):
            return ctx.enter_context(nc.sbuf_tensor(name, shape, dt))

        def sem(name):
            return ctx.enter_context(nc.semaphore(name))

        idx_dram = nc.dram_tensor("idx_dram", [2, SEQS * SEQ], BF16)
        xs_dram = [nc.dram_tensor(f"xs_dram{h}", [SLOTS, 2 * D], F16) for h in range(HALVES)]
        ys_dram = [nc.dram_tensor(f"ys_dram{h}", [SLOTS, D], F32) for h in range(HALVES)]

        table_parts = sb("table_parts", [VOCAB, 3, 2, D], BF16)
        ffn_w1 = sb("ffn_w1", [P, PARTS, HID], BF16)
        ffn_b1 = sb("ffn_b1", [P, CH])
        ffn_wg = sb("ffn_wg", [P, CH, E8])
        ffn_bg = sb("ffn_bg", [P, E8])
        ffn_wd = sb("ffn_wd", [P, CH, E8, D])
        ffn_bd = sb("ffn_bd", [T * E8, T, D])
        ssm_w1t = sb("ssm_w1t", [P, PARTS, P], BF16)
        ssm_col = sb("ssm_col", [P, 8])
        ssm_taps = sb("ssm_taps", [P, TAPS])
        ssm_bc = sb("ssm_bc", [P, 2, STATE])
        ssm_bn = sb("ssm_bn", [P, 6])
        ssm_w2bc = sb("ssm_w2bc", [P, D])
        ssm_w2d = sb("ssm_w2d", [P, D])
        ssm_b2 = sb("ssm_b2", [P, D])
        moe_wr = sb("moe_wr", [P, PARTS, EX], BF16)
        moe_br = sb("moe_br", [P, EX])
        moe_w1 = sb("moe_w1", [P, PARTS, EX, HID2], BF16)
        moe_b1 = sb("moe_b1", [HID2, EX])
        moe_w2 = sb("moe_w2", [HID2, EX, D])
        ident = sb("ident", [P, P])
        ident16 = sb("ident16", [P, P], F16)
        before = sb("before", [P, P], BF16)
        ones = sb("ones", [P, P], BF16)
        iota_p = sb("iota_p", [P, 1])
        iota_e = sb("iota_e", [P, EX])
        rank_e8 = sb("rank_e8", [P, E8])

        idx_all = sb("idx_all", [P, 2, TH * P], BF16)

        h_all = sb("h_all", [P, HALVES * TH, D])
        xn_all = sb("xn_all", [P, HALVES * TH, 2 * D], F16)
        top_val = sb("top_val", [P, HALVES * TH, TOP])
        top_idx = sb("top_idx", [P, HALVES * TH, TOP])

        hots = sb("hots", [P, 2, 2, SEQ], BF16)
        hot = [hots[:, s, :, :] for s in range(2)]
        h = [sb(f"h{s}", [P, T, D]) for s in range(2)]
        xca = sb("xca", [P, EX * (TH + 1) // 2])
        xc, acc = (xca[:, k * T * D:(k + 1) * T * D].rearrange("p (t d) -> p t d", d=D) for k in range(2))
        seg_keep = xca[:, :].bitcast(BF16).rearrange("p (e t) -> p e t", e=EX)
        stat = sb("stat", [P, 6, T])
        stat_i = sb("stat_i", [P, T], I32)
        xn = [sb(f"xn{s}", [P, T, W65]) for s in range(2)]
        xs = [sb(f"xs{s}", [P, T, 4, D], F16) for s in range(2)]
        xt = [sb(f"xt{s}", [P, SEQ], F16) for s in range(2)]
        xt_high, xt_low = ([hots[:, s, k, :].bitcast(F16) for s in range(2)] for k in range(2))
        ering = sb("ering", [P, 4, 512])
        ht = sb("ht", [P, 2, CH, SEQ])
        dtmp = ering[:, 0:2, :].rearrange("p a (e d) -> p a e d", d=D)
        gate = sb("gate", [P, 8, T, E8])
        gate1 = sb("gate1", [P, 4, T])
        selp = [sb(f"selp{s}", [P, T, E8]) for s in range(2)]
        fd = [sb(f"fd{s}", [P, T, E8]) for s in range(2)]
        fe = [sb(f"fe{s}", [P, T, E8]) for s in range(2)]
        selt = [sb(f"selt{s}", [T * E8, P]) for s in range(2)]
        pad = TAPS // 2
        up = sb("up", [P, 2, EX * (TH + 1) // 2])
        gst = sb("gst", [P, 2, EX * (TH + 1) // 2])
        lg = [up[:, s, pad:pad + T * EX].rearrange("p (t e) -> p t e", e=EX) for s in range(2)]
        v8 = [sb(f"v8{s}", [P, T, 8]) for s in range(2)]
        i8 = [sb(f"i8{s}", [P, T, 8], U32) for s in range(2)]
        used = [0]

        def early(rows_, cols, dt=F32):
            v = gst[0:rows_, used[0] // (EX * (TH + 1) // 2), used[0] % (EX * (TH + 1) // 2):][:, 0:cols]
            used[0] += cols
            return v if dt == F32 else v.bitcast(dt)

        emb, emb_t, tok_w = early(VOCAB, 2 * D), early(2 * D, VOCAB), early(D, 2 * D)
        tok_b, tok_wt, ssm_w2 = early(P, D), early(2 * D, D), early(D, P)
        ssm_w1 = early(P, 2 * D)
        table = early(VOCAB, 2 * D).rearrange("p (k d) -> p k d", k=2)
        ids = early(SEQS * T, P, I32)
        used[0] = EX * (TH + 1) // 2
        ids_i = early(SEQS * T, 2 * P, I32).rearrange("p (k n) -> p k n", k=2)
        ids_f = early(SEQS * T, 3 * P).rearrange("p (k n) -> p k n", k=3)
        ids_b = early(SEQS * T, P, BF16).rearrange("p (k n) -> p k n", k=2)
        ffn_w1f = ering[:, 0, 0:HID]
        moe_wrf = ering[:, 1, 0:EX]
        ssm_w1f = ering[:, 2, 0:P]
        moe_b1r = ering[0:EX, 3, 0:HID2]
        moe_w1f = h_all[:, TH:, :].rearrange("p t d -> p (t d)")[:, 0:STAGE_E * HID2]
        yconv = [ht[:, s, 0, :] for s in range(2)]
        ysilu = [ht[:, s, 1, :] for s in range(2)]

        pick = [ht[:, k, 0, :].bitcast(BF16).rearrange("p (t e) -> p t e", e=EX) for k in range(TOP)]
        picks = ht[:, 0, 1, :].bitcast(BF16).rearrange("p (t e) -> p t e", e=EX)
        place = ering[:, :, :].rearrange("p a b -> p (a b)").rearrange("p (t e) -> p t e", e=EX)
        cnt = up[:, :, :].rearrange("p a b -> p (a b)").rearrange("p (e t) -> p e t", e=EX)
        cum = gst[:, :, :].rearrange("p a b -> p (a b)").rearrange("p (e t) -> p e t", e=EX)
        prod = hots[:, :, :, :].rearrange("p a b c -> p (a b c)").bitcast(F32).rearrange("p (t e) -> p t e", e=EX)
        nb = gate[:, 0:5, :, :].rearrange("p k t e -> p k (t e)")
        nb_i = sb("nb_i", [P, EX], I32)
        eb = sb("eb", [P, 1])
        slot_f = sb("slot_f", [P, TOP, TH])
        slot_i = sb("slot_i", [P, 4, TOP, TH], I32)
        rows = [sb(f"rows{k}", [P, TOP, TH], I32) for k in range(HALVES)]
        expert = [sb(f"expert{k}", [1, GROUPS], I32) for k in range(HALVES)]
        expert_f = sb("expert_f", [1, BLOCKS])
        gates = sb("gates", [P, HALVES * TH, 3])

        xb = ering[:, 2, :].bitcast(F16).rearrange("p (u j d) -> p u j d", u=2, d=2 * D)
        xbt = ering[:, 0:2, 0:GROUP * P // 2].bitcast(F16)
        hbt = ht[:, 1, :, 0:GROUP * P]
        moe_b2 = idx_all[:, :, :].rearrange("p a b -> p (a b)").bitcast(F32).rearrange("p (e d) -> p e d", d=D)
        yb = ering[:, 3, :].rearrange("p (u j d) -> p u j d", u=2, d=D)
        yg = [xn_all[:, :, :].rearrange("p t d -> p (t d)").bitcast(F32).rearrange("p (k t d) -> p k t d", k=TOP, d=D),
              idx_all[:, :, :].rearrange("p a b -> p (a b)").bitcast(F32).rearrange("p (k t d) -> p k t d", k=TOP, d=D)]
        zeros = xn_all[:, TH:, :].rearrange("p t d -> p (t d)").bitcast(F32)

        wide = [ctx.enter_context(nc.psum_tensor(f"wide{i}", [P, 512], F32)) for i in range(4)]
        trp = [ctx.enter_context(nc.psum_tensor(f"trp{i}", [P, 512], F32)) for i in range(2)]
        outp = [ctx.enter_context(nc.psum_tensor(f"outp{i}", [P, 512], F32)) for i in range(2)]

        ids_loaded = sem("ids_loaded")
        w_loaded = sem("w_loaded")
        bd_loaded = sem("bd_loaded")
        moe_loaded = sem("moe_loaded")
        consts = sem("consts")
        seg_done = sem("seg_done")
        bd_zero = sem("bd_zero")
        zero_ready = sem("zero_ready")
        zero_stored = sem("zero_stored")
        ids_ready = sem("ids_ready")
        idx_stored = sem("idx_stored")
        idx_loaded = sem("idx_loaded")
        setup_t = sem("setup_t")
        setup_c = sem("setup_c")
        table_mm = sem("table_mm")
        table_ready = sem("table_ready")
        bn_var = sem("bn_var")
        bn_rstd = sem("bn_rstd")
        decay_ready = sem("decay_ready")
        setup_done = sem("setup_done")
        hot_ready, xn_ready, ctx_done = sem("hot_ready"), sem("xn_ready"), sem("ctx_done")
        fd_ready, selp_ready, d_done = sem("fd_ready"), sem("selp_ready"), sem("d_done")
        conv_done, scan_done = sem("conv_done"), sem("scan_done")
        tok_mm, tr_ready, s_ready, pv_done = sem("tok_mm"), sem("tr_ready"), sem("s_ready"), sem("pv_done")
        h_ready, flog_ready, d_ready = sem("h_ready"), sem("flog_ready"), sem("d_ready")
        selt_mm, bd_ready, u_ready = sem("selt_mm"), sem("bd_ready"), sem("u_ready")
        mout_ready, rlog_ready = sem("mout_ready"), sem("rlog_ready")
        tanh_done, xt_ready, exp_done = sem("tanh_done"), sem("xt_ready"), sem("exp_done")
        gelu_done, fexp_done, selt_done = sem("gelu_done"), sem("fexp_done"), sem("selt_done")
        silu1_done, silu2_done, xn_saved = sem("silu1_done"), sem("silu2_done"), sem("xn_saved")
        dve_step, waits_passed = sem("dve_step"), sem("waits_passed")
        picks_ready, place_mm, cnt_mm, cnt_ready = sem("picks_ready"), sem("place_mm"), sem("cnt_mm"), sem("cnt_ready")
        eb_ready, expert_mm, expert_ready, rows_ready = sem("eb_ready"), sem("expert_mm"), sem("expert_ready"), sem("rows_ready")
        gdiff_ready, gexp_done = sem("gdiff_ready"), sem("gexp_done")
        scattered = [sem(f"scattered{k}") for k in range(HALVES)]
        gathered = [sem(f"gathered{k}") for k in range(HALVES * TH // T)]
        xb_loaded = [sem(f"xb_loaded{u}") for u in range(2)]
        yb_stored = [sem(f"yb_stored{u}") for u in range(2)]
        xbt_mm, xbt_ready, hb_mm, hb_ready = sem("xbt_mm"), sem("xbt_ready"), sem("hb_mm"), sem("hb_ready")
        yb_mm, yb_ready = sem("yb_mm"), sem("yb_ready")
        w1_loaded, w1_split, b2_loaded, split_step = sem("w1_loaded"), sem("w1_split"), sem("b2_loaded"), sem("split_step")
        out_ready, out_stored = sem("out_ready"), sem("out_stored")

        N_SETUP_LOADS = 27
        LN = ("attention", "experts8", "ssm", "router")
        TR = 2 * (3 + len(LN) - 1)
        SJ = 2 * 2 * T

        def count(it, half, n, k):
            return it * n + (half * PAIRS * n + k)

        def tr_index(stage, s):
            return 3 * s if stage == 0 else 6 + 2 * (stage - 1) + s

        def row(v):
            return v.rearrange("(a n) -> a n", a=1)

        def bcast_rows(v, n):
            return row(v).to_broadcast([n, v.shape[0]])

        class Group:
            def __init__(self, i, n):
                self.i, self.n = i, n

            def __add__(self, k):
                return self.n + k if self.i is None else 2 * self.i + (self.n + k)

        def parity(g):
            return g.n % 2

        def experts(eng, half, g):
            at = slice(g.n, g.n + 1) if g.i is None else bass.ds(g.i * 2 + g.n, 1)
            packed = eng.value_load(expert[half][0:1, at])
            return [eng.snap((packed >> (EX_BITS * j)) & (EX - 1)) for j in range(GROUP)]

        def pipeline(eng, *steps):
            ahead = len(steps) - 1
            for n in range(-ahead, 0):
                for k, f in enumerate(steps):
                    if n + ahead - k >= 0:
                        f(Group(None, n + ahead - k))
            rounds = (GROUPS - ahead) // 2
            with eng.Fori(0, rounds) as i:
                for n in range(2):
                    for k, f in enumerate(steps):
                        f(Group(i, n + ahead - k))
            for n in range(2 * rounds, GROUPS):
                for k, f in enumerate(steps):
                    if n + ahead - k < GROUPS:
                        f(Group(None, n + ahead - k))

        def alone(eng):
            eng.sem_inc(waits_passed, 1)

        block = ctx.enter_context(nc.Block())

        @block.sync
        def _(sp):
            sp.dma_start(ids[:, :], a["x"].rearrange("b (t p) -> (b t) p", p=P)).then_inc(ids_loaded, 16)
            loads = [
                (emb[:, 0:D], a["L0_tok_emb1"]), (emb[:, D:2 * D], a["L0_tok_emb2"]),
                (tok_w[:, :], a["L0_tok_W"]), (tok_b[:, :], bcast_rows(a["L0_tok_b"], P)),
                (ffn_w1f[0:D, :], a["L0_ffn_W1"]), (ffn_w1f[D:P, :], a["L0_ffn_W1"]), (ffn_bg[:, :], bcast_rows(a["L0_ffn_bg"], P)),
                (ssm_w1[:, 0:D], a["L1_attn_w1"]), (ssm_w1[:, D:2 * D], a["L1_attn_w1"]), (ssm_w2[:, :], a["L1_attn_w2"]),
                (ssm_b2[:, :], bcast_rows(a["L1_attn_b2"], P)),
                (ssm_taps[:, :], a["L1_attn_wd"].rearrange("e a k -> e (a k)")),
                (ssm_bc[:, 0, :], a["L1_attn_Bm"]), (ssm_bc[:, 1, :], a["L1_attn_Cm"]),
                (moe_wrf[0:D, :], a["L1_ffn_Wr"]), (moe_wrf[D:P, :], a["L1_ffn_Wr"]), (moe_b1r, a["L1_ffn_b1"]), (moe_br[:, :], bcast_rows(a["L1_ffn_br"], P)),
                (ffn_wg[:, :, :], a["L0_ffn_Wg"].rearrange("(c p) e -> p c e", p=P)),
            ]
            for i, name in enumerate(("b1", "bd", "gamma", "beta", "rmean", "rvar", "A", "Dv")):
                loads.append((ssm_col[:, i:i + 1], a["L1_attn_" + name].rearrange("(p a) -> p a", a=1)))
            assert len(loads) == N_SETUP_LOADS
            for dst, src in loads:
                sp.dma_start(dst, src).then_inc(w_loaded, 16)
            for c in range(CH):
                sp.dma_start(ffn_b1[:, c:c + 1], a["L0_ffn_b1"].rearrange("(c p a) -> c p a", p=P, a=1)[c]).then_inc(bd_loaded, 16)
                sp.dma_start(ffn_wd[:, c, :, :], a["L0_ffn_Wd"][:, c * P:(c + 1) * P, :].rearrange("e p d -> p e d")).then_inc(bd_loaded, 16)
            sp.wait_ge(bd_zero, 1)
            for t in range(T):
                sp.dma_start(ffn_bd[t * E8:(t + 1) * E8, t, :], a["L0_ffn_bd"]).then_inc(bd_loaded, 16)
            sp.wait_ge(ids_ready, 1)
            for k in range(2):
                sp.dma_start(idx_dram[k, :].rearrange("(t p) -> t p", p=P), ids_b[:, k, :]).then_inc(idx_stored, 16)
            sp.wait_ge(idx_stored, 32)
            for k in range(2):
                sp.dma_start(idx_all[:, k, :], bcast_rows(idx_dram[k, 0:TH * P], P)).then_inc(idx_loaded, 16)
            sp.wait_ge(zero_ready, 1)
            zero_cols = TH * D
            per = SLOTS * D // P // zero_cols
            for k in range(HALVES):
                for i in range(per):
                    sp.dma_start(xs_dram[k][:, :].bitcast(F32).rearrange("(p r) d -> p (r d)", p=P)[:, i * zero_cols:(i + 1) * zero_cols],
                                 zeros).then_inc(zero_stored, 16)
            sp.dma_start(moe_w2[:, :, :], a["L1_ffn_W2"].rearrange("e k n -> k e n")).then_inc(moe_loaded, 16)
            for c in range(EX // STAGE_E):
                if c:
                    sp.wait_ge(w1_split, c)
                w = a["L1_ffn_W1"][c * STAGE_E:(c + 1) * STAGE_E].rearrange("e k n -> k e n")
                for k in range(2):
                    sp.dma_start(moe_w1f[k * D:(k + 1) * D, :].rearrange("p (e n) -> p e n", n=HID2), w).then_inc(w1_loaded, 16)
            sp.wait_ge(hot_ready, 2 * PAIRS)
            for k in range(2):
                sp.dma_start(idx_all[:, k, :], bcast_rows(idx_dram[k, TH * P:2 * TH * P], P)).then_inc(idx_loaded, 16)

            sp.wait_ge(hot_ready, 2 * PAIRS * HALVES)
            sp.dma_start(moe_b2.rearrange("p e d -> p (e d)"),
                         bcast_rows(a["L1_ffn_b2"].rearrange("e d -> (e d)"), P)).then_inc(b2_loaded, 16)

            for half in range(HALVES):
                src = xs_dram[half][:, :].rearrange("(g p j) d -> g p (j d)", p=P, j=GROUP)
                dst = ys_dram[half][:, :].rearrange("(g p j) d -> g p (j d)", p=P, j=GROUP)
                n = GROUPS // 2
                if half == 0:
                    sp.wait_ge(expert_ready, HALVES)
                sp.wait_ge(scattered[half], 16 * TOP * TH)

                def load(i, u):
                    sp.dma_start(xb[:, u, :, :].rearrange("p j d -> p (j d)"),
                                 src[bass.ds(2 * i + u, 1)].rearrange("a p n -> p (a n)")).then_inc(xb_loaded[u], 16)

                def store(i, u, back=0):
                    sp.wait_ge(yb_ready, 2 * i + (half * GROUPS + u + 3 - 2 * back))
                    sp.dma_start(dst[bass.ds(2 * i + (u - 2 * back), 1)].rearrange("a p n -> p (a n)"),
                                 yb[:, u, :, :].rearrange("p j d -> p (j d)")).then_inc(yb_stored[u], 16)

                for u in range(2):
                    if half:
                        sp.wait_ge(xbt_mm, half * GROUPS - 1 + u)
                    load(0, u)
                for u in range(2):
                    sp.wait_ge(xbt_mm, half * GROUPS + u + 1)
                    load(1, u)
                with sp.Fori(1, n - 1) as i:
                    for u in range(2):
                        sp.wait_ge(xbt_mm, 2 * i + (half * GROUPS + u + 1))
                        load(i + 1, u)
                        store(i, u, back=1)
                for i in (n - 2, n - 1):
                    for u in range(2):
                        store(i, u)

            out_v = out.rearrange("b (t p) d -> b p t d", p=P)
            for g in range(SEQS):
                sp.wait_ge(out_ready, g + 1)
                sp.dma_start(out_v[g], h_all[:, g * T:(g + 1) * T, :]).then_inc(out_stored, 16)
            sp.wait_ge(zero_stored, 16 * HALVES * per)
            sp.wait_ge(out_stored, 16 * SEQS)

        @block.gpsimd
        def _(pool):
            pool.memset(ident[:, :], 0.0).then_inc(consts, 1)
            pool.memset(before[:, :], 1.0).then_inc(consts, 1)
            pool.memset(ones[:, :], 1.0).then_inc(consts, 1)
            pool.wait_ge(consts, 3)
            pool.affine_select(out=ident[:, :], in_=ident[:, :], compare_op=ALU.not_equal, fill=1.0,
                               base=0, pattern=[[-1, P]], channel_multiplier=1).then_inc(consts, 1)
            pool.affine_select(out=before[:, :], in_=before[:, :], compare_op=ALU.is_gt, fill=0.0,
                               base=0, pattern=[[1, P]], channel_multiplier=-1).then_inc(consts, 1)
            pool.iota(iota_p[:, :], [[0, 1]], base=0, channel_multiplier=1,
                      allow_small_or_imprecise_dtypes=True).then_inc(consts, 1)
            pool.iota(iota_e[:, :], [[1, EX]], base=0, channel_multiplier=0,
                      allow_small_or_imprecise_dtypes=True).then_inc(consts, 1)
            pool.iota(rank_e8[:, :], [[-1, E8]], base=E8, channel_multiplier=0,
                      allow_small_or_imprecise_dtypes=True).then_inc(consts, 1)
            pool.wait_ge(consts, 8)
            pool.tensor_copy(ident16[:, :], ident[:, :]).then_inc(consts, 1)
            pool.wait_ge(bn_var, 2)
            pool.tensor_tensor(ssm_bn[:, 5:6], ssm_bn[:, 4:5], ssm_bn[:, 3:4], ALU.pow).then_inc(bn_rstd, 1)
            at = 0
            for c in range(EX // STAGE_E):
                pool.wait_ge(w1_loaded, 32 * (c + 1))
                for part in range(PARTS):
                    dst = moe_w1[:, part, c * STAGE_E:(c + 1) * STAGE_E, :].rearrange("p e n -> p (e n)")
                    pool.tensor_copy(dst, moe_w1f).then_inc(split_step, 1)
                    at += 1
                    pool.wait_ge(split_step, at)
                    if part < PARTS - 1:
                        pool.tensor_tensor(moe_w1f, moe_w1f, dst, ALU.subtract).then_inc(split_step, 1)
                        at += 1
                        pool.wait_ge(split_step, at)
                pool.sem_inc(w1_split, 1)
            for half in range(HALVES):
                pool.wait_ge(rows_ready, half + 1)
                pool.wait_ge(xn_saved, 2 * PAIRS * (half + 1))
                if half == 0:
                    pool.wait_ge(zero_stored, 16 * HALVES * (SLOTS * D // P // (TH * D)))
                for t in range(TH):
                    for k in range(TOP):
                        pool.indirect_dma_start(
                            out=xs_dram[half][:, :],
                            out_offset=bass.IndirectOffsetOnAxis(ap=rows[half][:, k, t:t + 1], axis=0),
                            in_=xn_all[:, half * TH + t, :], in_offset=None).then_inc(scattered[half], 16)
            for half in range(HALVES):
                if half == 0:
                    pool.wait_ge(scattered[1], 16 * TOP * TH)
                for u in range(2):
                    pool.wait_ge(yb_stored[u], 16 * (half + 1) * GROUPS // 2 + 16)
                for t in range(TH):
                    for k in range(TOP):
                        pool.indirect_dma_start(
                            out=yg[half][:, k, t, :], out_offset=None, in_=ys_dram[half][:, :],
                            in_offset=bass.IndirectOffsetOnAxis(ap=rows[half][:, k, t:t + 1], axis=0)
                        ).then_inc(gathered[(half * TH + t) // T], 16)

        @block.scalar
        def _(act):
            act.wait_ge(setup_t, 5)
            act.activation(emb_t[:, :], trp[0][:, 0:P], ACT.Copy).then_inc(setup_c, 1)
            act.activation(tok_wt[:, :], trp[0][:, P:P + D], ACT.Copy).then_inc(setup_c, 1)
            act.activation(ssm_w1f, trp[0][:, 2 * P:3 * P], ACT.Copy).then_inc(setup_c, 1)
            act.activation(moe_b1[:, :], trp[0][:, 3 * P:3 * P + EX], ACT.Copy).then_inc(setup_c, 1)
            act.wait_ge(w_loaded, 16 * N_SETUP_LOADS)
            act.activation(ssm_bn[:, 2:3], ssm_col[:, 6:7], ACT.Exp).then_inc(decay_ready, 1)

            def evacuate(it, half, stage, s):
                for k, dst in enumerate((xt, xt_high, xt_low) if stage == 0 else (xt,)):
                    n = tr_index(stage, s) + k
                    act.wait_ge(tr_ready, count(it, half, TR, n + 1))
                    act.activation(dst[s][:, :], trp[n % 2][:, :].bitcast(F16), ACT.Copy).then_inc(xt_ready, 1)

            def main(it, half):
                for s in range(2):
                    act.wait_ge(tok_mm, count(it, half, 2, s + 1))
                    act.activation(h[s][:, :, :].rearrange("p t d -> p (t d)"), outp[s][:, :], ACT.Tanh).then_inc(tanh_done, 1)
                for s in range(2):
                    evacuate(it, half, 0, s)
                    for i in range(2 * T):
                        j = s * 2 * T + i
                        act.wait_ge(s_ready, count(it, half, SJ, j + 1))
                        if j >= 4:
                            act.wait_ge(pv_done, count(it, half, SJ, j - 3))
                        act.activation(ering[:, j % 4, :], wide[j % 4][:, :], ACT.Exp, scale=D ** -0.5).then_inc(exp_done, 1)
                for s in range(2):
                    evacuate(it, half, 1, s)
                    for c in range(CH):
                        for g in range(2):
                            q = (s * CH + c) * 2 + g
                            act.wait_ge(h_ready, count(it, half, 8, q + 1))
                            act.activation(ht[:, s, c, g * 512:(g + 1) * 512], wide[q % 4][:, :], ACT.Gelu,
                                           bias=ffn_b1[:, c:c + 1]).then_inc(gelu_done, 1)
                for s in range(2):
                    act.wait_ge(fd_ready, count(it, half, 2, s + 1))
                    act.activation(fe[s][:, :, :], fd[s][:, :, :], ACT.Exp).then_inc(fexp_done, 1)
                    act.wait_ge(selt_mm, count(it, half, 2, s + 1))
                    act.activation(selt[s][:, :], outp[s][0:T * E8, 64:64 + P], ACT.Copy).then_inc(selt_done, 1)
                for s in range(2):
                    evacuate(it, half, 2, s)
                    for g in range(2):
                        act.wait_ge(u_ready, count(it, half, 4, s * 2 + g + 1))
                        act.activation(up[:, s, pad + g * 512:pad + (g + 1) * 512], wide[s * 2 + g][:, :], ACT.Silu,
                                       bias=ssm_col[:, 0:1]).then_inc(silu1_done, 1)
                for s in range(2):
                    act.wait_ge(conv_done, count(it, half, 2, s + 1))
                    act.activation(ysilu[s], yconv[s], ACT.Silu, bias=ssm_bn[:, 1:2], scale=ssm_bn[:, 0:1]).then_inc(silu2_done, 1)
                for s in range(2):
                    evacuate(it, half, 3, s)
                    act.activation(xn_all[:, bass.ds((it * 2 + (half * 2 * PAIRS + s)) * T, T), :], xs[s][:, :, 1:3, :].rearrange("p t k d -> p t (k d)"),
                                   ACT.Copy).then_inc(xn_saved, 1)

            act.wait_ge(setup_done, 1)
            act.wait_ge(bd_loaded, 16 * (2 * CH + T))
            for half in range(HALVES):
                with act.Fori(0, PAIRS) as it:
                    main(it, half)
                for k in range(4):
                    act.wait_ge(cnt_mm, 4 * half + k + 1)
                    bank = (trp + outp)[k]
                    act.activation(cnt[:, 16 * k:16 * (k + 1), 1:TH + 1],
                                   bank[:, :].rearrange("p (e t) -> p e t", t=TH), ACT.Copy).then_inc(cnt_ready, 1)
                act.wait_ge(gdiff_ready, half + 1)
                act.activation(gates[:, half * TH:(half + 1) * TH, 2], gates[:, half * TH:(half + 1) * TH, 2],
                               ACT.Exp).then_inc(gexp_done, 1)
            for half in range(HALVES):
                def turned(g):
                    u = parity(g)
                    act.wait_ge(xbt_mm, g + (half * GROUPS + 1))
                    act.activation(xbt[:, u, :], trp[u][:, 0:GROUP * P // 2].bitcast(F16), ACT.Copy).then_inc(xbt_ready, 1)

                def hidden(g):
                    u = parity(g)
                    es = experts(act, half, g)
                    act.wait_ge(hb_mm, g + (half * GROUPS + 1))
                    for j, e in enumerate(es):
                        last = act.activation(hbt[:, u, j * P:(j + 1) * P], wide[u][:, j * P:(j + 1) * P], ACT.Relu,
                                              bias=moe_b1[:, bass.ds(e, 1)])
                    last.then_inc(hb_ready, 1)

                pipeline(act, turned, hidden)

        @block.tensor
        def _(pe):
            pe.wait_ge(consts, 9)
            pe.wait_ge(w_loaded, 16 * N_SETUP_LOADS)
            pe.transpose(trp[0][:, 0:P], emb[:, :], ident[:, :]).then_inc(setup_t, 1)
            pe.transpose(trp[0][:, P:P + D], tok_w[:, :], ident[0:D, 0:D]).then_inc(setup_t, 1)
            pe.transpose(trp[0][:, 2 * P:3 * P], ssm_w1[:, :], ident[:, :]).then_inc(setup_t, 1)
            pe.transpose(trp[1][:, 0:D], ssm_w2[:, :], ident[0:D, 0:D]).then_inc(setup_t, 1)
            pe.transpose(trp[0][:, 3 * P:3 * P + EX], moe_b1r, ident[0:EX, 0:EX]).then_inc(setup_t, 1)
            pe.wait_ge(setup_c, 2)
            for k in range(2):
                pe.matmul(outp[k][:, 0:D], emb_t[k * D:(k + 1) * D, :], tok_wt[k * D:(k + 1) * D, :],
                          start=True, stop=True).then_inc(table_mm, 1)
            pe.wait_ge(table_ready, 1)
            pe.wait_ge(setup_c, 4)
            pe.wait_ge(setup_done, 1)
            pe.wait_ge(bd_loaded, 16 * (2 * CH + T))

            def transposes(it, half, stage, s):
                pe.wait_ge(xn_ready, count(it, half, 8, stage * 2 + s + 1))
                for k in range(3 if stage == 0 else 1):
                    n = tr_index(stage, s) + k
                    if n >= 2:
                        pe.wait_ge(xt_ready, count(it, half, TR, n - 1))
                    alone(pe)
                    for t in range(T):
                        first = (1, 0, 2)[k]
                        rows_ = xs[s][:, t, first:first + 2, :].rearrange("p k d -> p (k d)")
                        last = pe.transpose(trp[n % 2][:, :].bitcast(F16)[:, t * P:(t + 1) * P], rows_, ident16[:, :])
                    last.then_inc(tr_ready, 1)

            def xt_there(it, half, stage, s):
                pe.wait_ge(xt_ready, count(it, half, TR, tr_index(stage, s) + (3 if stage == 0 else 1)))

            def by_parts(out_, weights, moving, weights_move=False):
                for part in range(PARTS):
                    w = weights(part)
                    last = pe.matmul(out_, moving if weights_move else w, w if weights_move else moving,
                                     start=(part == 0), stop=(part == PARTS - 1))
                return last

            def main(it, half):
                for s in range(2):
                    pe.wait_ge(hot_ready, count(it, half, 2, s + 1))
                    for t in range(T):
                        for k in range(2):
                            for part in range(3):
                                last = pe.matmul(outp[s][:, t * D:(t + 1) * D], hot[s][:, k, t * P:(t + 1) * P],
                                                 table_parts[:, part, k, :], start=(k + part == 0), stop=(k + part == 3))
                    last.then_inc(tok_mm, 1)
                for s in range(2):
                    transposes(it, half, 0, s)
                    xt_there(it, half, 0, s)

                    def scores(i):
                        j = s * 2 * T + i
                        if j >= 4:
                            pe.wait_ge(exp_done, count(it, half, SJ, j - 3))
                        m, g = i % T, i // T
                        pe.matmul(wide[j % 4][:, :], xt[s][:, m * P:(m + 1) * P], xt_high[s][:, g * 512:(g + 1) * 512],
                                  start=True, stop=False)
                        pe.matmul(wide[j % 4][:, :], xt[s][:, m * P:(m + 1) * P], xt_low[s][:, g * 512:(g + 1) * 512],
                                  start=False, stop=True).then_inc(s_ready, 1)

                    def weighted(i):
                        j = s * 2 * T + i
                        m, g = i % T, i // T
                        pe.wait_ge(exp_done, count(it, half, SJ, j + 1))
                        if m == 0 and g == 1:
                            pe.wait_ge(ctx_done, count(it, half, 4, s * 2 + 1))
                        for n in range(4):
                            last = pe.matmul(outp[s][:, n * W65:(n + 1) * W65], ering[:, j % 4, n * P:(n + 1) * P],
                                             xn[s][:, m, :], start=(m == 0 and n == 0), stop=(m == T - 1),
                                             skip_group_check=True)
                        last.then_inc(pv_done, 1)

                    lag = 2
                    for i in range(2 * T + lag):
                        if i < 2 * T:
                            scores(i)
                        if i >= lag:
                            weighted(i - lag)
                for s in range(2):
                    transposes(it, half, 1, s)
                    xt_there(it, half, 1, s)
                    for c in range(CH):
                        for g in range(2):
                            q = (s * CH + c) * 2 + g
                            if q >= 4:
                                pe.wait_ge(gelu_done, count(it, half, 8, q - 3))
                            by_parts(wide[q % 4][:, :], lambda part: ffn_w1[:, part, c * P:(c + 1) * P],
                                     xt[s][:, g * 512:(g + 1) * 512]).then_inc(h_ready, 1)
                pe.wait_ge(gelu_done, count(it, half, 8, 8))
                for s in range(2):
                    for t in range(T):
                        for c in range(CH):
                            last = pe.matmul(outp[s][:, t * E8:(t + 1) * E8], ht[:, s, c, t * P:(t + 1) * P],
                                             ffn_wg[:, c, :], start=(c == 0), stop=(c == CH - 1))
                    last.then_inc(flog_ready, 1)
                for s in range(2):
                    for t in range(T):
                        q = s * T + t
                        if q >= 4:
                            pe.wait_ge(d_done, count(it, half, 2 * T, q - 3))
                        for c in range(CH):
                            last = pe.matmul(wide[q % 4][:, :], ht[:, s, c, t * P:(t + 1) * P],
                                             ffn_wd[:, c, :, :].rearrange("p e d -> p (e d)"), start=(c == 0), stop=(c == CH - 1))
                        last.then_inc(d_ready, 1)
                    pe.wait_ge(selp_ready, count(it, half, 2, s + 1))
                    alone(pe)
                    pe.transpose(outp[s][0:T * E8, 64:64 + P], selp[s][:, :, :].rearrange("p t e -> p (t e)"), ident[:, :]).then_inc(selt_mm, 1)
                    pe.wait_ge(selt_done, count(it, half, 2, s + 1))
                    pe.matmul(outp[s][:, :], selt[s][:, :], ffn_bd[:, :, :].rearrange("p t d -> p (t d)"),
                              start=True, stop=True).then_inc(bd_ready, 1)
                for s in range(2):
                    transposes(it, half, 2, s)
                    xt_there(it, half, 2, s)
                    if s == 0:
                        pe.wait_ge(d_done, count(it, half, 2 * T, 2 * T))
                    for g in range(2):
                        by_parts(wide[s * 2 + g][:, :], lambda part: ssm_w1t[:, part, :],
                                 xt[s][:, g * 512:(g + 1) * 512]).then_inc(u_ready, 1)
                for s in range(2):
                    pe.wait_ge(scan_done, count(it, half, 2, s + 1))
                    for t in range(T):
                        pe.matmul(outp[s][:, t * D:(t + 1) * D], gst[:, s, t * P:(t + 1) * P], ssm_w2bc[:, :],
                                  start=True, stop=False)
                        last = pe.matmul(outp[s][:, t * D:(t + 1) * D], ysilu[s][:, t * P:(t + 1) * P], ssm_w2d[:, :],
                                         start=False, stop=True)
                    last.then_inc(mout_ready, 1)
                for s in range(2):
                    transposes(it, half, 3, s)
                    xt_there(it, half, 3, s)
                    for t in range(T):
                        last = by_parts(outp[s][:, t * EX:(t + 1) * EX], lambda part: moe_wr[:, part, :],
                                        xt[s][:, t * P:(t + 1) * P], weights_move=True)
                    last.then_inc(rlog_ready, 1)

            for half in range(HALVES):
                with pe.Fori(0, PAIRS) as it:
                    main(it, half)
                pe.wait_ge(picks_ready, half + 1)
                for k in range(4):
                    pe.matmul((trp + outp)[k][:, :], ones[:, :],
                              picks[:, :, 16 * k:16 * (k + 1)].rearrange("p t e -> p e t"),
                              start=True, stop=True).then_inc(cnt_mm, 1)
                for k in range(4):
                    pe.matmul(wide[k][:, :], before[:, :], picks[:, 8 * k:8 * (k + 1), :].rearrange("p t e -> p (t e)"),
                              start=True, stop=True).then_inc(place_mm, 1)
                pe.wait_ge(eb_ready, half + 1)
                pe.matmul(outp[0][0:1, 0:BLOCKS], eb[:, :], ident[:, 0:BLOCKS], start=True, stop=True).then_inc(expert_mm, 1)

            pe.wait_ge(expert_ready, HALVES)
            pe.wait_ge(moe_loaded, 16)
            pe.wait_ge(w1_split, EX // STAGE_E)
            for half in range(HALVES):
                before_ = half * GROUPS

                def turn(g):
                    u = parity(g)
                    if g.i is None:
                        pe.wait_ge(xb_loaded[u], 16 * (before_ // 2 + g.n // 2 + 1))
                    else:
                        pe.wait_ge(xb_loaded[u], 16 * g.i + 16 * (before_ // 2 + g.n // 2 + 1))
                    alone(pe)
                    for j in range(GROUP):
                        last = pe.transpose(trp[u][:, 0:GROUP * P // 2].bitcast(F16)[:, j * P:(j + 1) * P], xb[:, u, j, :], ident16[:, :])
                    last.then_inc(xbt_mm, 1)

                def up_projection(g):
                    u = parity(g)
                    es = experts(pe, half, g)
                    pe.wait_ge(xbt_ready, g + (before_ + 1))
                    for j, e in enumerate(es):
                        last = by_parts(wide[u][:, j * P:(j + 1) * P],
                                        lambda part: moe_w1[:, part, bass.ds(e, 1), :].rearrange("p a n -> p (a n)"),
                                        xbt[:, u, j * P:(j + 1) * P])
                    last.then_inc(hb_mm, 1)

                def down_projection(g):
                    u = parity(g)
                    es = experts(pe, half, g)
                    pe.wait_ge(hb_ready, g + (before_ + 1))
                    pe.wait_ge(yb_ready, g + (before_ + 1))
                    for j, e in enumerate(es):
                        last = pe.matmul(outp[u][:, j * D:(j + 1) * D], hbt[:, u, j * P:(j + 1) * P],
                                         moe_w2[:, bass.ds(e, 1), :].rearrange("p a n -> p (a n)"), start=True, stop=True)
                    last.then_inc(yb_mm, 1)

                pipeline(pe, turn, up_projection, down_projection)

        @block.vector
        def _(dve):
            at = [0]
            base = [None]

            def step(ins):
                at[0] += 1
                ins.then_inc(dve_step, 1)
                dve.wait_ge(dve_step, at[0] if base[0] is None else base[0] + at[0])

            def looped(n, per, body):
                start = at[0]
                with dve.Fori(0, n) as it:
                    base[0] = it * per
                    body(it)
                    base[0] = None
                assert at[0] - start == per, at[0] - start
                at[0] = start + n * per

            step(dve.memset(ffn_bd[:, :, :], 0.0))
            dve.sem_inc(bd_zero, 1)
            step(dve.memset(zeros, 0.0))
            dve.sem_inc(zero_ready, 1)
            for s in range(2):
                step(dve.memset(xn[s][:, :, D:W65], 1.0))
            dve.wait_ge(ids_loaded, 16)
            step(dve.tensor_scalar(ids_i[:, 0, :], ids[:, :], 7, None, ALU.arith_shift_right))
            step(dve.tensor_scalar(ids_i[:, 1, :], ids[:, :], VOCAB - 1, None, ALU.bitwise_and))
            step(dve.tensor_copy(ids_f[:, 0, :], ids_i[:, 0, :]))
            step(dve.tensor_scalar(ids_f[:, 1, :], ids_f[:, 0, :], 0.0, float(VOCAB), ALU.is_lt, ALU.mult))
            step(dve.tensor_tensor(ids_f[:, 2, :], ids_f[:, 0, :], ids_f[:, 1, :], ALU.add))
            step(dve.tensor_scalar(ids_b[:, 0, :], ids_f[:, 2, :], 0.0, float(VOCAB - 1), ALU.max, ALU.min))
            dve.tensor_copy(ids_b[:, 1, :], ids_i[:, 1, :]).then_inc(ids_ready, 1)
            dve.wait_ge(w_loaded, 16 * N_SETUP_LOADS)
            dve.memset(ssm_bn[:, 3:4], -0.5).then_inc(bn_var, 1)
            dve.tensor_scalar(ssm_bn[:, 4:5], ssm_col[:, 5:6], BN_EPS, None, ALU.add).then_inc(bn_var, 1)
            dve.wait_ge(bn_rstd, 1)
            step(dve.tensor_tensor(ssm_bn[:, 0:1], ssm_bn[:, 5:6], ssm_col[:, 2:3], ALU.mult))
            step(dve.tensor_tensor(ssm_bn[:, 4:5], ssm_col[:, 1:2], ssm_col[:, 4:5], ALU.subtract))
            step(dve.tensor_tensor(ssm_bn[:, 4:5], ssm_bn[:, 4:5], ssm_bn[:, 0:1], ALU.mult))
            step(dve.tensor_tensor(ssm_bn[:, 1:2], ssm_bn[:, 4:5], ssm_col[:, 3:4], ALU.add))
            step(dve.tensor_tensor(ssm_bc[:, 0, :], ssm_bc[:, 0, :], ssm_bc[:, 1, :], ALU.mult))
            step(dve.tensor_reduce(ssm_bn[:, 3:4], ssm_bc[:, 0, :], AX, ALU.add))
            dve.wait_ge(setup_t, 5)
            step(dve.tensor_scalar(ssm_w2bc[:, :], trp[1][:, 0:D], ssm_bn[:, 3:4], None, ALU.mult))
            step(dve.tensor_scalar(ssm_w2d[:, :], trp[1][:, 0:D], ssm_col[:, 7:8], None, ALU.mult))
            dve.wait_ge(table_mm, 2)
            step(dve.tensor_copy(table[:, 0, :], outp[0][:, 0:D]))
            step(dve.tensor_tensor(table[:, 1, :], outp[1][:, 0:D], tok_b[:, :], ALU.add))
            for part in range(3):
                step(dve.tensor_copy(table_parts[:, part, :, :], table[:, :, :]))
                if part < 2:
                    step(dve.tensor_tensor(table[:, :, :], table[:, :, :], table_parts[:, part, :, :], ALU.subtract))
            dve.sem_inc(table_ready, 1)
            dve.wait_ge(setup_c, 4)
            for src, parts in ((ffn_w1f, ffn_w1), (ssm_w1f, ssm_w1t), (moe_wrf, moe_wr)):
                for part in range(PARTS):
                    step(dve.tensor_copy(parts[:, part, :], src))
                    if part < PARTS - 1:
                        step(dve.tensor_tensor(src, src, parts[:, part, :], ALU.subtract))
            dve.wait_ge(decay_ready, 1)
            dve.wait_ge(consts, 9)
            dve.sem_inc(setup_done, 2)

            def bc(ap, shape):
                return ap.to_broadcast(shape)

            SH = [P, T, D]

            def layernorm(src, s):
                alone(dve)
                step(dve.tensor_reduce(stat[:, 0, :], src, AX, ALU.add))
                step(dve.tensor_scalar(stat[:, 0, :], stat[:, 0, :], 1.0 / D, None, ALU.mult))
                step(dve.tensor_tensor(xc[:, :, :], src, bc(stat[:, 0, :].unsqueeze(2), SH), ALU.subtract))
                step(dve.tensor_tensor(xn[s][:, :, 0:D], xc[:, :, :], xc[:, :, :], ALU.mult))
                step(dve.tensor_reduce(stat[:, 1, :], xn[s][:, :, 0:D], AX, ALU.add))
                step(dve.tensor_scalar(stat[:, 1, :], stat[:, 1, :], 1.0 / D, LN_EPS, ALU.mult, ALU.add))
                step(dve.tensor_scalar(stat_i[:, :], stat[:, 1, :].bitcast(I32), 1, None, ALU.arith_shift_right))
                step(dve.tensor_scalar(stat[:, 2, :].bitcast(I32), stat_i[:, :], -1.0, float(RSQRT_SEED), ALU.mult, ALU.add))
                for _ in range(3):
                    step(dve.scalar_tensor_tensor(stat[:, 3, :], stat[:, 2, :], -0.5, stat[:, 2, :], ALU.mult, ALU.mult))
                    step(dve.tensor_tensor(stat[:, 3, :], stat[:, 3, :], stat[:, 1, :], ALU.mult))
                    step(dve.scalar_tensor_tensor(stat[:, 2, :], stat[:, 3, :], 1.5, stat[:, 2, :], ALU.add, ALU.mult))
                step(dve.tensor_tensor(xn[s][:, :, 0:D], xc[:, :, :], bc(stat[:, 2, :].unsqueeze(2), SH), ALU.mult))

            def split(stage, s):
                step(dve.tensor_copy(xs[s][:, :, 1, :], xn[s][:, :, 0:D]))
                step(dve.tensor_tensor(xs[s][:, :, 2, :], xn[s][:, :, 0:D], xs[s][:, :, 1, :], ALU.subtract))
                if stage == 0:
                    step(dve.tensor_copy(xs[s][:, :, 0, :], xs[s][:, :, 1, :]))
                    step(dve.tensor_copy(xs[s][:, :, 3, :], xs[s][:, :, 2, :]))
                dve.sem_inc(xn_ready, 1)

            def main(it, half):
                for s in range(2):
                    step(dve.tensor_scalar(hot[s][:, :, :], idx_all[:, :, bass.ds((it * 2 + s) * SEQ, SEQ)], iota_p[:, 0:1], None, ALU.is_equal))
                    dve.sem_inc(hot_ready, 1)
                for s in range(2):
                    dve.wait_ge(tanh_done, count(it, half, 2, s + 1))
                    layernorm(h[s][:, :, :], s)
                    split(0, s)
                for s in range(2):
                    for g in range(2):
                        dve.wait_ge(pv_done, count(it, half, SJ, s * 2 * T + (g + 1) * T))
                        o = outp[s][:, 0:4 * W65].rearrange("p (t d) -> p t d", d=W65)
                        step(dve.reciprocal(stat[:, 4, 0:4], o[:, :, D]))
                        step(dve.tensor_tensor(acc[:, 0:4, :], o[:, :, 0:D], bc(stat[:, 4, 0:4].unsqueeze(2), [P, 4, D]), ALU.mult))
                        dve.sem_inc(ctx_done, 1)
                        step(dve.tensor_tensor(h[s][:, 4 * g:4 * g + 4, :], h[s][:, 4 * g:4 * g + 4, :], acc[:, 0:4, :], ALU.add))
                    layernorm(h[s][:, :, :], s)
                    split(1, s)
                G = [P, T, E8]
                for s in range(2):
                    dve.wait_ge(flog_ready, count(it, half, 2, s + 1))
                    lo = outp[s][:, 0:T * E8].rearrange("p (t e) -> p t e", e=E8)
                    step(dve.tensor_tensor(gate[:, 0, :, :], lo, bc(ffn_bg[:, :].unsqueeze(1), G), ALU.add))
                    step(dve.tensor_reduce(gate1[:, 0, :], gate[:, 0, :, :], AX, ALU.max))
                    step(dve.tensor_tensor(fd[s][:, :, :], gate[:, 0, :, :], bc(gate1[:, 0, :].unsqueeze(2), G), ALU.subtract))
                    dve.sem_inc(fd_ready, 1)
                    step(dve.tensor_scalar(gate[:, 1, :, :], fd[s][:, :, :], 0.0, None, ALU.is_equal))
                    step(dve.tensor_tensor(gate[:, 1, :, :], gate[:, 1, :, :], bc(rank_e8[:, :].unsqueeze(1), G), ALU.mult))
                    step(dve.tensor_reduce(gate1[:, 1, :], gate[:, 1, :, :], AX, ALU.max))
                    step(dve.tensor_tensor(gate[:, 2, :, :], gate[:, 1, :, :], bc(gate1[:, 1, :].unsqueeze(2), G), ALU.is_equal))
                    dve.wait_ge(fexp_done, count(it, half, 2, s + 1))
                    step(dve.tensor_reduce(gate1[:, 2, :], fe[s][:, :, :], AX, ALU.add))
                    step(dve.reciprocal(gate1[:, 3, :], gate1[:, 2, :]))
                    step(dve.tensor_tensor(selp[s][:, :, :], gate[:, 2, :, :], bc(gate1[:, 3, :].unsqueeze(2), G), ALU.mult))
                    dve.sem_inc(selp_ready, 1)
                    for t in range(T):
                        dve.wait_ge(d_ready, count(it, half, 2 * T, s * T + t + 1))
                        step(dve.tensor_tensor(dtmp[:, t % 2, :, :], wide[t % 4][:, :].rearrange("p (e d) -> p e d", d=D),
                                               bc(selp[s][:, t, :].unsqueeze(2), [P, E8, D]), ALU.mult))
                        dve.sem_inc(d_done, 1)
                        step(dve.tensor_reduce(acc[:, t, :], dtmp[:, t % 2, :, :].rearrange("p e d -> p d e"), AX, ALU.add))
                    step(dve.tensor_tensor(h[s][:, :, :], h[s][:, :, :], acc[:, :, :], ALU.add))
                    dve.wait_ge(bd_ready, count(it, half, 2, s + 1))
                    step(dve.tensor_tensor(h[s][:, :, :], outp[s][:, :].rearrange("p (t d) -> p t d", d=D), h[s][:, :, :], ALU.add))
                    layernorm(h[s][:, :, :], s)
                    split(2, s)
                for s in range(2):
                    dve.wait_ge(silu1_done, count(it, half, 4, 2 * s + 2))
                    step(dve.tensor_scalar(yconv[s], up[:, s, 0:SEQ], ssm_taps[:, 0:1], None, ALU.mult))
                    for k in range(1, TAPS):
                        step(dve.scalar_tensor_tensor(yconv[s], up[:, s, k:k + SEQ], ssm_taps[:, k:k + 1], yconv[s], ALU.mult, ALU.add))
                    dve.sem_inc(conv_done, 1)
                for s in range(2):
                    dve.wait_ge(silu2_done, count(it, half, 2, s + 1))
                    step(dve.tensor_tensor_scan(gst[:, s, 0:SEQ], bc(ssm_bn[:, 2:3], [P, SEQ]), ysilu[s], 0.0, ALU.mult, ALU.add))
                    dve.sem_inc(scan_done, 1)
                for s in range(2):
                    tiles = bass.ds((it * 2 + (half * 2 * PAIRS + s)) * T, T)
                    dve.wait_ge(mout_ready, count(it, half, 2, s + 1))
                    step(dve.tensor_tensor(h[s][:, :, :], outp[s][:, :].rearrange("p (t d) -> p t d", d=D), h[s][:, :, :], ALU.add))
                    step(dve.tensor_tensor(h_all[:, tiles, :], h[s][:, :, :], bc(ssm_b2[:, :].unsqueeze(1), SH), ALU.add))
                    layernorm(h_all[:, tiles, :], s)
                    split(3, s)
                for s in range(2):
                    tiles = bass.ds((it * 2 + (half * 2 * PAIRS + s)) * T, T)
                    dve.wait_ge(rlog_ready, count(it, half, 2, s + 1))
                    step(dve.tensor_tensor(lg[s][:, :, :], outp[s][:, :].rearrange("p (t e) -> p t e", e=EX),
                                           bc(moe_br[:, :].unsqueeze(1), [P, T, EX]), ALU.add))
                    for t in range(T):
                        alone(dve)
                        step(dve.max(v8[s][:, t, :], lg[s][:, t, :]))
                        alone(dve)
                        step(dve.max_index(i8[s][:, t, :], v8[s][:, t, :], lg[s][:, t, :]))
                    step(dve.tensor_copy(top_val[:, tiles, :], v8[s][:, :, 0:TOP]))
                    step(dve.tensor_copy(top_idx[:, tiles, :], i8[s][:, :, 0:TOP]))

            dve.wait_ge(bd_loaded, 16 * (2 * CH + T))
            for half in range(HALVES):
                dve.wait_ge(idx_loaded, 32 * (half + 1))
                if half == 1:
                    dve.wait_ge(w1_split, EX // STAGE_E)
                for s in range(2):
                    step(dve.memset(up[:, s, 0:pad], 0.0))
                    step(dve.memset(up[:, s, pad + SEQ:2 * pad + SEQ], 0.0))
                looped(PAIRS, DVE_MAIN, lambda it, half=half: main(it, half))
                tiles = slice(half * TH, (half + 1) * TH)
                OH = [P, TH, EX]
                for k in range(TOP):
                    step(dve.tensor_tensor(pick[k], bc(iota_e[:, :].unsqueeze(1), OH),
                                           bc(top_idx[:, tiles, k].unsqueeze(2), OH), ALU.is_equal))
                step(dve.tensor_tensor(picks, pick[0], pick[1], ALU.add))
                dve.sem_inc(picks_ready, 1)
                step(dve.tensor_tensor(gates[:, tiles, 2], top_val[:, tiles, 1], top_val[:, tiles, 0], ALU.subtract))
                dve.sem_inc(gdiff_ready, 1)
                step(dve.memset(seg_keep[:, :, :], 1.0))
                step(dve.memset(seg_keep[:, :, 0:1], 0.0))
                step(dve.memset(cnt[:, :, 0:1], 0.0))
                dve.wait_ge(cnt_ready, 4 * (half + 1))
                step(dve.tensor_tensor_scan(cum[:, :, :].rearrange("p e t -> p (e t)"), seg_keep[:, :, :].rearrange("p e t -> p (e t)"),
                                            cnt[:, :, :].rearrange("p e t -> p (e t)"), 0.0, ALU.mult, ALU.add))
                step(dve.tensor_scalar(nb_i[:, :], cum[:, :, TH], float(P - 1), None, ALU.add))
                step(dve.tensor_scalar(nb_i[:, :], nb_i[:, :], 7, None, ALU.arith_shift_right))
                step(dve.tensor_copy(nb[:, 0, :], nb_i[:, :]))
                step(dve.tensor_tensor_scan(nb[:, 1, :], bc(seg_keep[:, 0, 1:2], [P, EX]), nb[:, 0, :], 0.0, ALU.mult, ALU.add))
                step(dve.tensor_tensor(nb[:, 2, :], nb[:, 1, :], nb[:, 0, :], ALU.subtract))
                step(dve.tensor_scalar(nb[:, 4, :], nb[:, 2, :], iota_p[:, 0:1], None, ALU.is_le))
                step(dve.tensor_reduce(eb[:, :], nb[:, 4, :], AX, ALU.add))
                dve.sem_inc(eb_ready, 1)
                step(dve.tensor_scalar(nb[:, 3, :], nb[:, 2, :], float(P), None, ALU.mult))
                for k in range(4):
                    dve.wait_ge(place_mm, 4 * half + k + 1)
                    step(dve.tensor_tensor(place[:, 8 * k:8 * (k + 1), :], wide[k][:, :].rearrange("p (t e) -> p t e", e=EX),
                                           cum[:, :, 8 * k:8 * (k + 1)].rearrange("p e t -> p t e"), ALU.add))
                step(dve.tensor_tensor(place, place, bc(nb[:, 3, :].unsqueeze(1), OH), ALU.add))
                for k in range(TOP):
                    step(dve.tensor_tensor(prod, place, pick[k], ALU.mult))
                    step(dve.tensor_reduce(slot_f[:, k, :], prod, AX, ALU.add))
                step(dve.tensor_copy(slot_i[:, 0, :, :], slot_f[:, :, :]))
                step(dve.tensor_scalar(slot_i[:, 1, :, :], slot_i[:, 0, :, :], ~(GROUP * P - 1), None, ALU.bitwise_and))
                step(dve.tensor_scalar(slot_i[:, 2, :, :], slot_i[:, 0, :, :], P - 1, 2, ALU.bitwise_and, ALU.logical_shift_left))
                step(dve.tensor_scalar(slot_i[:, 3, :, :], slot_i[:, 0, :, :], 7, GROUP - 1, ALU.logical_shift_right, ALU.bitwise_and))
                step(dve.tensor_tensor(slot_i[:, 1, :, :], slot_i[:, 1, :, :], slot_i[:, 2, :, :], ALU.bitwise_or))
                step(dve.tensor_tensor(rows[half][:, :, :], slot_i[:, 1, :, :], slot_i[:, 3, :, :], ALU.bitwise_or))
                dve.sem_inc(rows_ready, 1)
                dve.wait_ge(gexp_done, half + 1)
                step(dve.tensor_scalar(gates[:, tiles, 0], gates[:, tiles, 2], 1.0, None, ALU.add))
                step(dve.reciprocal(gates[:, tiles, 0], gates[:, tiles, 0]))
                step(dve.tensor_tensor(gates[:, tiles, 1], gates[:, tiles, 2], gates[:, tiles, 0], ALU.mult))
                dve.wait_ge(expert_mm, half + 1)
                step(dve.tensor_scalar(expert_f[:, :], outp[0][0:1, 0:BLOCKS], -1.0, None, ALU.add))
                of_block = expert_f[:, :].rearrange("p (g j) -> p g j", j=GROUP)
                for j in range(GROUP - 2, -1, -1):
                    dst = of_block[:, :, GROUP - 1] if j else expert[half][:, :]
                    step(dve.scalar_tensor_tensor(dst, of_block[:, :, GROUP - 1], float(EX), of_block[:, :, j], ALU.mult, ALU.add))
                dve.sem_inc(expert_ready, 1)

            for u in range(2):
                dve.sem_inc(yb_stored[u], 16)
                dve.sem_inc(yb_ready, 1)
            dve.wait_ge(b2_loaded, 16)
            for half in range(HALVES):
                def results(g):
                    u = parity(g)
                    es = experts(dve, half, g)
                    dve.wait_ge(yb_mm, g + (half * GROUPS + 1))
                    dve.wait_ge(yb_stored[u], 16 * g.i + 16 * (half * GROUPS // 2 + 1))
                    for j, e in enumerate(es):
                        last = dve.tensor_tensor(yb[:, u, j, :], outp[u][:, j * D:(j + 1) * D],
                                                 moe_b2[:, bass.ds(e, 1), :].rearrange("p a n -> p (a n)"), ALU.add)
                    last.then_inc(yb_ready, 1)

                pipeline(dve, results)
            for g in range(SEQS):
                half, t0 = g * T // TH, g * T % TH
                tiles = slice(g * T, (g + 1) * T)
                dve.wait_ge(gathered[g], 16 * TOP * T)
                for k in range(TOP):
                    y = yg[half][:, k, t0:t0 + T, :]
                    step(dve.tensor_tensor(y, y, bc(gates[:, tiles, k].unsqueeze(2), SH), ALU.mult))
                    step(dve.tensor_tensor(h_all[:, tiles, :], h_all[:, tiles, :], y, ALU.add))
                dve.sem_inc(out_ready, 1)


DVE_MAIN = 288


def kernel(**inputs):
    import numpy as _np
    import concourse.bacc as _bacc
    from concourse import mybir as _mybir
    from concourse.bass_utils import run_bass_kernel_spmd as _run

    nc = _bacc.Bacc("TRN2", target_bir_lowering=False, num_devices=1)
    arrays, handles = {}, {}
    for name, v in inputs.items():
        v = _np.ascontiguousarray(v)
        arrays[f"in_{name}"] = v
        handles[name] = nc.dram_tensor(f"in_{name}", v.shape, _mybir.dt.from_np(v.dtype), kind="ExternalInput").ap()
    result = nc.dram_tensor("out_0", (SEQS, SEQ, D), F32, kind="ExternalOutput").ap()
    lm_tower(nc, handles, result)
    r = _run(nc, [arrays], core_ids=[0])
    return r.results[0]["out_0"]
```

```python
from contextlib import ExitStack

import concourse.bass as bass
from concourse import mybir

ALU = mybir.AluOpType
ACT = mybir.ActivationFunctionType
AX = mybir.AxisListType.X
F32 = mybir.dt.float32
BF16 = mybir.dt.bfloat16
F16 = mybir.dt.float16
I32 = mybir.dt.int32
U32 = mybir.dt.uint32

P = 128
D = 64
SEQS, SEQ = 8, 1024
T = SEQ // P
HALVES = 2
TH = SEQS * T // HALVES
VOCAB = 128
HID = 256
CH = HID // P
E8 = 8
TAPS = 5
STATE = 8
EX = 64
HID2 = 128
TOP = 2
LN_EPS = 1e-5
BN_EPS = 1e-5
BLOCKS = TH * P * TOP // P + EX
GROUP = 4
GROUPS = BLOCKS // GROUP
SLOTS = BLOCKS * P
W65 = D + 1
PARTS = 3
EX_BITS = 6
STAGE_E = 16
RSQRT_SEED = 0x5F3759DF


def lm_tower(nc, a, out):
    ctx = ExitStack()
    with ctx:
        def sb(name, shape, dt=F32):
            return ctx.enter_context(nc.sbuf_tensor(name, shape, dt))

        def sem(name):
            return ctx.enter_context(nc.semaphore(name))

        idx_dram = nc.dram_tensor("idx_dram", [2, SEQS * SEQ], BF16)
        xs_dram = [nc.dram_tensor(f"xs_dram{h}", [SLOTS, 2 * D], F16) for h in range(HALVES)]
        ys_dram = [nc.dram_tensor(f"ys_dram{h}", [SLOTS, D], F32) for h in range(HALVES)]

        table_parts = sb("table_parts", [VOCAB, 3, 2, D], BF16)
        ffn_w1 = sb("ffn_w1", [P, PARTS, HID], BF16)
        ffn_b1 = sb("ffn_b1", [P, CH])
        ffn_wg = sb("ffn_wg", [P, CH, E8])
        ffn_bg = sb("ffn_bg", [P, E8])
        ffn_wd = sb("ffn_wd", [P, CH, E8, D])
        ffn_bd = sb("ffn_bd", [T * E8, T, D])
        ssm_w1t = sb("ssm_w1t", [P, PARTS, P], BF16)
        ssm_col = sb("ssm_col", [P, 8])
        ssm_taps = sb("ssm_taps", [P, TAPS])
        ssm_bc = sb("ssm_bc", [P, 2, STATE])
        ssm_bn = sb("ssm_bn", [P, 6])
        ssm_w2bc = sb("ssm_w2bc", [P, D])
        ssm_w2d = sb("ssm_w2d", [P, D])
        ssm_b2 = sb("ssm_b2", [P, D])
        moe_wr = sb("moe_wr", [P, PARTS, EX], BF16)
        moe_br = sb("moe_br", [P, EX])
        moe_w1 = sb("moe_w1", [P, PARTS, EX, HID2], BF16)
        moe_b1 = sb("moe_b1", [HID2, EX])
        moe_w2 = sb("moe_w2", [HID2, EX, D])
        ident = sb("ident", [P, P])
        ident16 = sb("ident16", [P, P], F16)
        before = sb("before", [P, P], BF16)
        ones = sb("ones", [P, P], BF16)
        iota_p = sb("iota_p", [P, 1])
        iota_e = sb("iota_e", [P, EX])
        rank_e8 = sb("rank_e8", [P, E8])

        idx_all = sb("idx_all", [P, 2, TH * P], BF16)
        idx_row = idx_all[:, :, 0:2 * SEQ]

        h_all = sb("h_all", [P, HALVES * TH, D])
        xn_all = sb("xn_all", [P, HALVES * TH, 2 * D], F16)
        top_val = sb("top_val", [P, HALVES * TH, TOP])
        top_idx = sb("top_idx", [P, HALVES * TH, TOP])

        hots = sb("hots", [P, 2, 2, SEQ], BF16)
        hot = [hots[:, s, :, :] for s in range(2)]
        h = [sb(f"h{s}", [P, T, D]) for s in range(2)]
        xca = sb("xca", [P, EX * (TH + 1) // 2])
        xc, acc = (xca[:, k * T * D:(k + 1) * T * D].rearrange("p (t d) -> p t d", d=D) for k in range(2))
        seg_keep = xca[:, :].bitcast(BF16).rearrange("p (e t) -> p e t", e=EX)
        stat = sb("stat", [P, 6, T])
        stat_i = sb("stat_i", [P, T], I32)
        xn = [sb(f"xn{s}", [P, T, W65]) for s in range(2)]
        xs = [sb(f"xs{s}", [P, T, 4, D], F16) for s in range(2)]
        xt = [sb(f"xt{s}", [P, SEQ], F16) for s in range(2)]
        xt_high, xt_low = ([hots[:, s, k, :].bitcast(F16) for s in range(2)] for k in range(2))
        ering = sb("ering", [P, 4, 512])
        ht = sb("ht", [P, 2, CH, SEQ])
        gate = sb("gate", [P, 8, T, E8])
        gate1 = sb("gate1", [P, 4, T])
        selp = [sb(f"selp{s}", [P, T, E8]) for s in range(2)]
        fd = [sb(f"fd{s}", [P, T, E8]) for s in range(2)]
        fe = [sb(f"fe{s}", [P, T, E8]) for s in range(2)]
        selt = [sb(f"selt{s}", [T * E8, P]) for s in range(2)]
        pad = TAPS // 2
        up = sb("up", [P, 2, EX * (TH + 1) // 2])
        gst = sb("gst", [P, 2, EX * (TH + 1) // 2])
        lg = [up[:, s, pad:pad + T * EX].rearrange("p (t e) -> p t e", e=EX) for s in range(2)]
        v8 = [sb(f"v8{s}", [P, T, 8]) for s in range(2)]
        i8 = [sb(f"i8{s}", [P, T, 8], U32) for s in range(2)]
        dtmp = [gst[:, s, 0:SEQ].rearrange("p (a e d) -> p a e d", a=2, d=D) for s in range(2)]
        used = [0]

        def early(rows_, cols, dt=F32):
            v = gst[0:rows_, used[0] // (EX * (TH + 1) // 2), used[0] % (EX * (TH + 1) // 2):][:, 0:cols]
            used[0] += cols
            return v if dt == F32 else v.bitcast(dt)

        emb, emb_t, tok_w = early(VOCAB, 2 * D), early(2 * D, VOCAB), early(D, 2 * D)
        tok_b, tok_wt, ssm_w2 = early(P, D), early(2 * D, D), early(D, P)
        ssm_w1 = early(P, 2 * D)
        table = early(VOCAB, 2 * D).rearrange("p (k d) -> p k d", k=2)
        ids = early(SEQS * T, P, I32)
        used[0] = EX * (TH + 1) // 2
        ids_i = early(SEQS * T, 2 * P, I32).rearrange("p (k n) -> p k n", k=2)
        ids_f = early(SEQS * T, 3 * P).rearrange("p (k n) -> p k n", k=3)
        ids_b = early(SEQS * T, P, BF16).rearrange("p (k n) -> p k n", k=2)
        ffn_w1f = ering[:, 0, 0:HID]
        moe_wrf = ering[:, 1, 0:EX]
        ssm_w1f = ering[:, 2, 0:P]
        moe_b1r = ering[0:EX, 3, 0:HID2]
        moe_w1f = h_all[:, TH:, :].rearrange("p t d -> p (t d)")[:, 0:STAGE_E * HID2]
        yconv = [ht[:, s, 0, :] for s in range(2)]
        ysilu = [ht[:, s, 1, :] for s in range(2)]

        pick = [ht[:, k, 0, :].bitcast(BF16).rearrange("p (t e) -> p t e", e=EX) for k in range(TOP)]
        picks = ht[:, 0, 1, :].bitcast(BF16).rearrange("p (t e) -> p t e", e=EX)
        cnt = up[:, :, :].rearrange("p a b -> p (a b)").rearrange("p (e t) -> p e t", e=EX)
        cum = gst[:, :, :].rearrange("p a b -> p (a b)").rearrange("p (e t) -> p e t", e=EX)
        place = up[:, :, :].rearrange("p a b -> p (a b)")[:, 0:TH * EX].rearrange("p (t e) -> p t e", e=EX)
        prod = gst[:, :, :].rearrange("p a b -> p (a b)")[:, 0:TH * EX].rearrange("p (t e) -> p t e", e=EX)
        nb = gate[:, 0:5, :, :].rearrange("p k t e -> p k (t e)")
        nb_i = sb("nb_i", [P, EX], I32)
        eb = sb("eb", [P, 1])
        slot_f = sb("slot_f", [P, TOP, TH])
        slot_i = sb("slot_i", [P, 4, TOP, TH], I32)
        rows = [sb(f"rows{k}", [P, TOP, TH], I32) for k in range(HALVES)]
        expert = [sb(f"expert{k}", [1, GROUPS], I32) for k in range(HALVES)]
        expert_f = sb("expert_f", [1, BLOCKS])
        gates = sb("gates", [P, HALVES * TH, 3])

        xb = ering[:, 2, :].bitcast(F16).rearrange("p (u j d) -> p u j d", u=2, d=2 * D)
        xbt = ering[:, 0:2, 0:GROUP * P // 2].bitcast(F16)
        hbt = ht[:, 1, 1, :].rearrange("p (u n) -> p u n", u=2)
        moe_b2 = idx_all[:, :, :].rearrange("p a b -> p (a b)").bitcast(F32).rearrange("p (e d) -> p e d", d=D)
        yb = ering[:, 3, :].rearrange("p (u j d) -> p u j d", u=2, d=D)
        yg = [xn_all[:, :, :].rearrange("p t d -> p (t d)").bitcast(F32).rearrange("p (k t d) -> p k t d", k=TOP, d=D),
              idx_all[:, :, :].rearrange("p a b -> p (a b)").bitcast(F32).rearrange("p (k t d) -> p k t d", k=TOP, d=D)]
        zeros = xn_all[:, TH:, :].rearrange("p t d -> p (t d)").bitcast(F32)

        wide = [ctx.enter_context(nc.psum_tensor(f"wide{i}", [P, 512], F32)) for i in range(4)]
        trp = [ctx.enter_context(nc.psum_tensor(f"trp{i}", [P, 512], F32)) for i in range(2)]
        outp = [ctx.enter_context(nc.psum_tensor(f"outp{i}", [P, 512], F32)) for i in range(2)]

        ids_loaded = sem("ids_loaded")
        w_loaded = sem("w_loaded")
        bd_loaded = sem("bd_loaded")
        moe_loaded = sem("moe_loaded")
        consts = sem("consts")
        seg_done = sem("seg_done")
        bd_zero = sem("bd_zero")
        zero_ready = sem("zero_ready")
        zero_stored = sem("zero_stored")
        ids_ready = sem("ids_ready")
        idx_stored = sem("idx_stored")
        idx_loaded = [sem(f"idx_loaded{s}") for s in range(2)]
        setup_t = sem("setup_t")
        setup_c = sem("setup_c")
        table_mm = sem("table_mm")
        table_ready = sem("table_ready")
        bn_var = sem("bn_var")
        bn_rstd = sem("bn_rstd")
        decay_ready = sem("decay_ready")
        setup_done = sem("setup_done")
        LN = ("attention", "experts8", "ssm", "router")
        hot_ready, ctx_done = sem("hot_ready"), sem("ctx_done")
        xn_ready = [sem(f"xn_ready_{name}") for name in LN]
        tr_ready = [sem(f"tr_ready_{name}") for name in LN]
        xt_ready = [sem(f"xt_ready_{name}") for name in LN]
        fd_ready, selp_ready, d_done = sem("fd_ready"), sem("selp_ready"), sem("d_done")
        conv_done, scan_done = sem("conv_done"), sem("scan_done")
        tok_mm, s_ready, pv_done = sem("tok_mm"), sem("s_ready"), sem("pv_done")
        h_ready, flog_ready, d_ready = sem("h_ready"), sem("flog_ready"), sem("d_ready")
        selt_mm, bd_ready, u_ready = sem("selt_mm"), sem("bd_ready"), sem("u_ready")
        logits_read = sem("logits_read")
        mout_ready, rlog_ready = sem("mout_ready"), sem("rlog_ready")
        tanh_done, exp_done = sem("tanh_done"), sem("exp_done")
        gelu_done, fexp_done, selt_done = sem("gelu_done"), sem("fexp_done"), sem("selt_done")
        silu1_done, silu2_done, xn_saved = sem("silu1_done"), sem("silu2_done"), sem("xn_saved")
        dve_step, waits_passed = sem("dve_step"), sem("waits_passed")
        picks_ready, place_mm, cnt_mm, cnt_ready = sem("picks_ready"), sem("place_mm"), sem("cnt_mm"), sem("cnt_ready")
        eb_ready, expert_mm, expert_ready, rows_ready = sem("eb_ready"), sem("expert_mm"), sem("expert_ready"), sem("rows_ready")
        gdiff_ready, gexp_done = sem("gdiff_ready"), sem("gexp_done")
        scattered = [sem(f"scattered{k}") for k in range(HALVES)]
        gathered = [sem(f"gathered{k}") for k in range(HALVES * TH // T)]
        xb_loaded = [sem(f"xb_loaded{u}") for u in range(2)]
        yb_stored = [sem(f"yb_stored{u}") for u in range(2)]
        xbt_mm, xbt_ready, hb_mm, hb_ready = sem("xbt_mm"), sem("xbt_ready"), sem("hb_mm"), sem("hb_ready")
        yb_mm, yb_ready = sem("yb_mm"), sem("yb_ready")
        w1_loaded, w1_split, b2_loaded, split_step = sem("w1_loaded"), sem("w1_split"), sem("b2_loaded"), sem("split_step")
        out_ready, out_stored = sem("out_ready"), sem("out_stored")

        N_SETUP_LOADS = 27
        TURNED = (3, 2, 2, 2)
        SJ = 2 * T
        LAST = SEQS - 1
        HALF = T // 2
        UNIT_LOOPS = SEQS // 2 - 1

        def row(v):
            return v.rearrange("(a n) -> a n", a=1)

        def bcast_rows(v, n):
            return row(v).to_broadcast([n, v.shape[0]])

        class Group:
            def __init__(self, i, n):
                self.i, self.n = i, n

            def __add__(self, k):
                return self.n + k if self.i is None else 2 * self.i + (self.n + k)

            def count(self, per, k):
                return self.n * per + k if self.i is None else self.i * (2 * per) + (self.n * per + k)

            def of_parity(self):
                return self.n // 2 + 1 if self.i is None else self.i + (self.n // 2 + 1)

            def tiles(self):
                return slice(self.n * T, (self.n + 1) * T) if self.i is None else bass.ds(self.i * (2 * T) + self.n * T, T)

            def before(self):
                return Group(self.i, self.n - 1)

            def after(self):
                return Group(self.i, self.n + 1)

        def parity(g):
            return g.n % 2

        def turn_bank(k):
            return k % 2

        SSM_AT = 7
        ZEROS = SLOTS * D // P // (TH * D)

        def experts(eng, half, g):
            at = slice(g.n, g.n + 1) if g.i is None else bass.ds(g.i * 2 + g.n, 1)
            packed = eng.value_load(expert[half][0:1, at])
            return packed, unpacked(eng, packed)

        def unpacked(eng, packed):
            return [eng.snap((packed >> (EX_BITS * j)) & (EX - 1)) for j in range(GROUP)]

        def pipeline(eng, *steps):
            ahead = len(steps) - 1
            for n in range(-ahead, 0):
                for k, f in enumerate(steps):
                    if n + ahead - k >= 0:
                        f(Group(None, n + ahead - k))
            rounds = (GROUPS - ahead) // 2
            with eng.Fori(0, rounds) as i:
                for n in range(2):
                    for k, f in enumerate(steps):
                        f(Group(i, n + ahead - k))
            for n in range(2 * rounds, GROUPS):
                for k, f in enumerate(steps):
                    if n + ahead - k < GROUPS:
                        f(Group(None, n + ahead - k))

        def alone(eng):
            eng.sem_inc(waits_passed, 1)

        block = ctx.enter_context(nc.Block())

        @block.sync
        def _(sp):
            sp.dma_start(ids[:, :], a["x"].rearrange("b (t p) -> (b t) p", p=P)).then_inc(ids_loaded, 16)
            loads = [
                (emb[:, 0:D], a["L0_tok_emb1"]), (emb[:, D:2 * D], a["L0_tok_emb2"]),
                (tok_w[:, :], a["L0_tok_W"]), (tok_b[:, :], bcast_rows(a["L0_tok_b"], P)),
                (ffn_w1f[0:D, :], a["L0_ffn_W1"]), (ffn_w1f[D:P, :], a["L0_ffn_W1"]), (ffn_bg[:, :], bcast_rows(a["L0_ffn_bg"], P)),
                (ssm_w1[:, 0:D], a["L1_attn_w1"]), (ssm_w1[:, D:2 * D], a["L1_attn_w1"]), (ssm_w2[:, :], a["L1_attn_w2"]),
                (ssm_b2[:, :], bcast_rows(a["L1_attn_b2"], P)),
                (ssm_taps[:, :], a["L1_attn_wd"].rearrange("e a k -> e (a k)")),
                (ssm_bc[:, 0, :], a["L1_attn_Bm"]), (ssm_bc[:, 1, :], a["L1_attn_Cm"]),
                (moe_wrf[0:D, :], a["L1_ffn_Wr"]), (moe_wrf[D:P, :], a["L1_ffn_Wr"]), (moe_b1r, a["L1_ffn_b1"]), (moe_br[:, :], bcast_rows(a["L1_ffn_br"], P)),
                (ffn_wg[:, :, :], a["L0_ffn_Wg"].rearrange("(c p) e -> p c e", p=P)),
            ]
            for i, name in enumerate(("b1", "bd", "gamma", "beta", "rmean", "rvar", "A", "Dv")):
                loads.append((ssm_col[:, i:i + 1], a["L1_attn_" + name].rearrange("(p a) -> p a", a=1)))
            assert len(loads) == N_SETUP_LOADS
            for dst, src in loads:
                sp.dma_start(dst, src).then_inc(w_loaded, 16)
            for c in range(CH):
                sp.dma_start(ffn_b1[:, c:c + 1], a["L0_ffn_b1"].rearrange("(c p a) -> c p a", p=P, a=1)[c]).then_inc(bd_loaded, 16)
                sp.dma_start(ffn_wd[:, c, :, :], a["L0_ffn_Wd"][:, c * P:(c + 1) * P, :].rearrange("e p d -> p e d")).then_inc(bd_loaded, 16)
            sp.wait_ge(bd_zero, 1)
            for t in range(T):
                sp.dma_start(ffn_bd[t * E8:(t + 1) * E8, t, :], a["L0_ffn_bd"]).then_inc(bd_loaded, 16)
            sp.wait_ge(ids_ready, 1)
            for k in range(2):
                sp.dma_start(idx_dram[k, :].rearrange("(t p) -> t p", p=P), ids_b[:, k, :]).then_inc(idx_stored, 16)
            sp.wait_ge(idx_stored, 32)

            def load_idx(n):
                sp.dma_start(idx_row[:, :, n % 2 * SEQ:(n % 2 + 1) * SEQ],
                             idx_dram[:, n * SEQ:(n + 1) * SEQ].rearrange("(a k) n -> a k n", a=1).to_broadcast([P, 2, SEQ])
                             ).then_inc(idx_loaded[n % 2], 16)

            def next_idx(n):
                sp.wait_ge(hot_ready, n - 1)
                load_idx(n)

            for n in range(2):
                load_idx(n)
            sp.wait_ge(zero_ready, 1)
            zero_cols = TH * D
            per = SLOTS * D // P // zero_cols
            for k in range(HALVES):
                for i in range(per):
                    sp.dma_start(xs_dram[k][:, :].bitcast(F32).rearrange("(p r) d -> p (r d)", p=P)[:, i * zero_cols:(i + 1) * zero_cols],
                                 zeros).then_inc(zero_stored, 16)
            sp.dma_start(moe_w2[:, :, :], a["L1_ffn_W2"].rearrange("e k n -> k e n")).then_inc(moe_loaded, 16)
            for c in range(EX // STAGE_E):
                if c:
                    sp.wait_ge(w1_split, c)
                w = a["L1_ffn_W1"][c * STAGE_E:(c + 1) * STAGE_E].rearrange("e k n -> k e n")
                for k in range(2):
                    sp.dma_start(moe_w1f[k * D:(k + 1) * D, :].rearrange("p (e n) -> p e n", n=HID2), w).then_inc(w1_loaded, 16)
                if c < 2:
                    next_idx(c + 2)
            for n in range(4, SEQS):
                next_idx(n)
            sp.wait_ge(hot_ready, SEQS)
            sp.dma_start(moe_b2.rearrange("p e d -> p (e d)"),
                         bcast_rows(a["L1_ffn_b2"].rearrange("e d -> (e d)"), P)).then_inc(b2_loaded, 16)

            for half in range(HALVES):
                src = xs_dram[half][:, :].rearrange("(g p j) d -> g p (j d)", p=P, j=GROUP)
                dst = ys_dram[half][:, :].rearrange("(g p j) d -> g p (j d)", p=P, j=GROUP)
                n = GROUPS // 2
                if half == 0:
                    sp.wait_ge(pv_done, SEQS * SJ)
                sp.wait_ge(scattered[half], 16 * TOP * TH)

                def load(i, u):
                    sp.dma_start(xb[:, u, :, :].rearrange("p j d -> p (j d)"),
                                 src[bass.ds(2 * i + u, 1)].rearrange("a p n -> p (a n)")).then_inc(xb_loaded[u], 16)

                def store(i, u, back=0):
                    sp.wait_ge(yb_ready, 2 * i + (half * GROUPS + u + 3 - 2 * back))
                    sp.dma_start(dst[bass.ds(2 * i + (u - 2 * back), 1)].rearrange("a p n -> p (a n)"),
                                 yb[:, u, :, :].rearrange("p j d -> p (j d)")).then_inc(yb_stored[u], 16)

                for u in range(2):
                    if half:
                        sp.wait_ge(xbt_mm, half * GROUPS - 1 + u)
                    load(0, u)
                for u in range(2):
                    sp.wait_ge(xbt_mm, half * GROUPS + u + 1)
                    load(1, u)
                with sp.Fori(1, n - 1) as i:
                    for u in range(2):
                        sp.wait_ge(xbt_mm, 2 * i + (half * GROUPS + u + 1))
                        load(i + 1, u)
                        store(i, u, back=1)
                for i in (n - 2, n - 1):
                    for u in range(2):
                        store(i, u)

            out_v = out.rearrange("b (t p) d -> b p t d", p=P)
            for g in range(SEQS):
                sp.wait_ge(out_ready, g + 1)
                sp.dma_start(out_v[g], h_all[:, g * T:(g + 1) * T, :]).then_inc(out_stored, 16)
            sp.wait_ge(zero_stored, 16 * HALVES * per)
            sp.wait_ge(out_stored, 16 * SEQS)

        @block.gpsimd
        def _(pool):
            pool.memset(ident[:, :], 0.0).then_inc(consts, 1)
            pool.memset(before[:, :], 1.0).then_inc(consts, 1)
            pool.memset(ones[:, :], 1.0).then_inc(consts, 1)
            pool.wait_ge(consts, 3)
            pool.affine_select(out=ident[:, :], in_=ident[:, :], compare_op=ALU.not_equal, fill=1.0,
                               base=0, pattern=[[-1, P]], channel_multiplier=1).then_inc(consts, 1)
            pool.affine_select(out=before[:, :], in_=before[:, :], compare_op=ALU.is_gt, fill=0.0,
                               base=0, pattern=[[1, P]], channel_multiplier=-1).then_inc(consts, 1)
            pool.iota(iota_p[:, :], [[0, 1]], base=0, channel_multiplier=1,
                      allow_small_or_imprecise_dtypes=True).then_inc(consts, 1)
            pool.iota(iota_e[:, :], [[1, EX]], base=0, channel_multiplier=0,
                      allow_small_or_imprecise_dtypes=True).then_inc(consts, 1)
            pool.iota(rank_e8[:, :], [[-1, E8]], base=E8, channel_multiplier=0,
                      allow_small_or_imprecise_dtypes=True).then_inc(consts, 1)
            pool.wait_ge(consts, 8)
            pool.tensor_copy(ident16[:, :], ident[:, :]).then_inc(consts, 1)
            pool.wait_ge(bn_var, 2)
            pool.tensor_tensor(ssm_bn[:, 5:6], ssm_bn[:, 4:5], ssm_bn[:, 3:4], ALU.pow).then_inc(bn_rstd, 1)
            at = 0
            for c in range(EX // STAGE_E):
                pool.wait_ge(w1_loaded, 32 * (c + 1))
                for part in range(PARTS):
                    dst = moe_w1[:, part, c * STAGE_E:(c + 1) * STAGE_E, :].rearrange("p e n -> p (e n)")
                    pool.tensor_copy(dst, moe_w1f).then_inc(split_step, 1)
                    at += 1
                    pool.wait_ge(split_step, at)
                    if part < PARTS - 1:
                        pool.tensor_tensor(moe_w1f, moe_w1f, dst, ALU.subtract).then_inc(split_step, 1)
                        at += 1
                        pool.wait_ge(split_step, at)
                pool.sem_inc(w1_split, 1)
            for half in range(HALVES):
                pool.wait_ge(rows_ready, half + 1)
                pool.wait_ge(xn_saved, SEQS // HALVES * (half + 1))
                if half == 0:
                    pool.wait_ge(zero_stored, 16 * HALVES * (SLOTS * D // P // (TH * D)))
                for t in range(TH):
                    for k in range(TOP):
                        pool.indirect_dma_start(
                            out=xs_dram[half][:, :],
                            out_offset=bass.IndirectOffsetOnAxis(ap=rows[half][:, k, t:t + 1], axis=0),
                            in_=xn_all[:, half * TH + t, :], in_offset=None).then_inc(scattered[half], 16)
            for half in range(HALVES):
                if half == 0:
                    pool.wait_ge(scattered[1], 16 * TOP * TH)
                for u in range(2):
                    pool.wait_ge(yb_stored[u], 16 * (half + 1) * GROUPS // 2 + 16)
                for t in range(TH):
                    for k in range(TOP):
                        pool.indirect_dma_start(
                            out=yg[half][:, k, t, :], out_offset=None, in_=ys_dram[half][:, :],
                            in_offset=bass.IndirectOffsetOnAxis(ap=rows[half][:, k, t:t + 1], axis=0)
                        ).then_inc(gathered[(half * TH + t) // T], 16)

        @block.scalar
        def _(act):
            act.wait_ge(setup_t, 5)
            act.activation(emb_t[:, :], trp[0][:, 0:P], ACT.Copy).then_inc(setup_c, 1)
            act.activation(tok_wt[:, :], trp[0][:, P:P + D], ACT.Copy).then_inc(setup_c, 1)
            act.activation(ssm_w1f, trp[0][:, 2 * P:3 * P], ACT.Copy).then_inc(setup_c, 1)
            act.activation(moe_b1[:, :], trp[0][:, 3 * P:3 * P + EX], ACT.Copy).then_inc(setup_c, 1)
            act.wait_ge(w_loaded, 16 * N_SETUP_LOADS)
            act.activation(ssm_bn[:, 2:3], ssm_col[:, 6:7], ACT.Exp).then_inc(decay_ready, 1)

            def evacuate(q, stage):
                s = parity(q)
                for k in range(TURNED[stage]):
                    act.wait_ge(tr_ready[stage], q.count(TURNED[stage], k + 1))
                    if stage == 0:
                        dst, src = (xt, xt_high, xt_low)[k][s][:, :], trp[turn_bank(k)][:, :].bitcast(F16)
                    else:
                        dst, src = xt[s][:, k * 512:(k + 1) * 512], trp[turn_bank(k)][:, :].bitcast(F16)[:, 0:512]
                    act.activation(dst, src, ACT.Copy).then_inc(xt_ready[stage], 1)

            def tanh(q):
                s = parity(q)
                act.wait_ge(tok_mm, q + 1)
                act.activation(h[s][:, :, :].rearrange("p t d -> p (t d)"), outp[s][:, :], ACT.Tanh).then_inc(tanh_done, 1)

            def exponentials(q, first, last, earlier=True):
                for i in range(first, last):
                    act.wait_ge(s_ready, q.count(SJ, i + 1))
                    if i >= 4 or earlier:
                        act.wait_ge(pv_done, q.count(SJ, i - 3))
                    act.activation(ering[:, i % 4, :], wide[i % 4][:, :], ACT.Exp, scale=D ** -0.5).then_inc(exp_done, 1)

            def gelu(q):
                for g in range(2):
                    for c in range(CH):
                        b = g * 2 + c
                        act.wait_ge(h_ready, q.count(4, b + 1))
                        act.activation(ht[:, parity(q), c, g * 512:(g + 1) * 512], wide[b][:, :], ACT.Gelu,
                                       bias=ffn_b1[:, c:c + 1]).then_inc(gelu_done, 1)

            def gate_exp(q):
                s = parity(q)
                act.wait_ge(fd_ready, q + 1)
                act.activation(fe[s][:, :, :], fd[s][:, :, :], ACT.Exp).then_inc(fexp_done, 1)

            def selection(q):
                s = parity(q)
                act.wait_ge(selt_mm, q + 1)
                act.activation(selt[s][:, :], outp[s][0:T * E8, 64:64 + P], ACT.Copy).then_inc(selt_done, 1)

            def silu1(q):
                for g in range(2):
                    act.wait_ge(u_ready, q.count(2, g + 1))
                    act.activation(up[:, parity(q), pad + g * 512:pad + (g + 1) * 512], trp[g][:, :], ACT.Silu,
                                   bias=ssm_col[:, 0:1]).then_inc(silu1_done, 1)

            def silu2(q):
                s = parity(q)
                act.wait_ge(conv_done, q + 1)
                act.activation(ysilu[s], yconv[s], ACT.Silu, bias=ssm_bn[:, 1:2], scale=ssm_bn[:, 0:1]).then_inc(silu2_done, 1)

            def save_rows(q):
                act.activation(xn_all[:, q.tiles(), :], xs[parity(q)][:, :, 1:3, :].rearrange("p t k d -> p t (k d)"),
                               ACT.Copy).then_inc(xn_saved, 1)

            def unit(q, front=True, back=True, pre=True):
                prev = q.before()
                if front:
                    evacuate(q, 0)
                    exponentials(q, 0, SSM_AT + 3, earlier=back)
                if back:
                    evacuate(prev, 2)
                if front:
                    exponentials(q, SSM_AT + 3, SSM_AT + 4, earlier=back)
                if back:
                    silu1(prev)
                if front:
                    exponentials(q, SSM_AT + 4, 2 * T, earlier=back)
                if back:
                    silu2(prev)
                if front:
                    evacuate(q, 1)
                    gelu(q)
                if back:
                    evacuate(prev, 3)
                    save_rows(prev)
                if front:
                    gate_exp(q)
                if pre:
                    tanh(q.after())
                if front:
                    selection(q)

            def route(half):
                for k in range(4):
                    act.wait_ge(cnt_mm, 4 * half + k + 1)
                    bank = (trp + outp)[k]
                    act.activation(cnt[:, 16 * k:16 * (k + 1), 1:TH + 1],
                                   bank[:, :].rearrange("p (e t) -> p e t", t=TH), ACT.Copy).then_inc(cnt_ready, 1)
                act.wait_ge(gdiff_ready, half + 1)
                act.activation(gates[:, half * TH:(half + 1) * TH, 2], gates[:, half * TH:(half + 1) * TH, 2],
                               ACT.Exp).then_inc(gexp_done, 1)

            act.wait_ge(setup_done, 1)
            act.wait_ge(bd_loaded, 16 * (2 * CH + T))
            tanh(Group(None, 0))
            unit(Group(None, 0), back=False)
            act.wait_ge(zero_stored, 16 * HALVES * ZEROS)
            with act.Fori(0, UNIT_LOOPS) as i:
                unit(Group(i, 1))
                unit(Group(i, 2))
            route(0)
            unit(Group(None, LAST), pre=False)
            unit(Group(None, SEQS), front=False, pre=False)
            route(1)
            for half in range(HALVES):
                def turned(g):
                    u = parity(g)
                    act.wait_ge(xbt_mm, g + (half * GROUPS + 1))
                    act.activation(xbt[:, u, :], trp[u][:, 0:GROUP * P // 2].bitcast(F16), ACT.Copy).then_inc(xbt_ready, 1)

                def hidden(g):
                    u = parity(g)
                    _, es = experts(act, half, g)
                    act.wait_ge(hb_mm, g + (half * GROUPS + 1))
                    for j, e in enumerate(es):
                        last = act.activation(hbt[:, u, j * P:(j + 1) * P], wide[u][:, j * P:(j + 1) * P], ACT.Relu,
                                              bias=moe_b1[:, bass.ds(e, 1)])
                    last.then_inc(hb_ready, 1)

                pipeline(act, turned, hidden)

        @block.tensor
        def _(pe):
            pe.wait_ge(consts, 9)
            pe.wait_ge(w_loaded, 16 * N_SETUP_LOADS)
            pe.transpose(trp[0][:, 0:P], emb[:, :], ident[:, :]).then_inc(setup_t, 1)
            pe.transpose(trp[0][:, P:P + D], tok_w[:, :], ident[0:D, 0:D]).then_inc(setup_t, 1)
            pe.transpose(trp[0][:, 2 * P:3 * P], ssm_w1[:, :], ident[:, :]).then_inc(setup_t, 1)
            pe.transpose(trp[1][:, 0:D], ssm_w2[:, :], ident[0:D, 0:D]).then_inc(setup_t, 1)
            pe.transpose(trp[0][:, 3 * P:3 * P + EX], moe_b1r, ident[0:EX, 0:EX]).then_inc(setup_t, 1)
            pe.wait_ge(setup_c, 2)
            for k in range(2):
                pe.matmul(outp[k][:, 0:D], emb_t[k * D:(k + 1) * D, :], tok_wt[k * D:(k + 1) * D, :],
                          start=True, stop=True).then_inc(table_mm, 1)
            pe.wait_ge(table_ready, 1)
            pe.wait_ge(setup_c, 4)
            pe.wait_ge(setup_done, 1)
            pe.wait_ge(bd_loaded, 16 * (2 * CH + T))

            def transposes(q, stage, after_ssm=True):
                if stage == 1 and after_ssm:
                    pe.wait_ge(silu1_done, q.count(2, 0))
                for k in range(TURNED[stage]):
                    pe.wait_ge(xn_ready[stage], q.count(TURNED[stage], k + 1))
                    if k == 2:
                        pe.wait_ge(xt_ready[stage], q.count(TURNED[stage], 1))
                    alone(pe)
                    first = (1, 0, 2)[k] if stage == 0 else 1
                    for j in range(T if stage == 0 else HALF):
                        t = j if stage == 0 else k * HALF + j
                        rows_ = xs[parity(q)][:, t, first:first + 2, :].rearrange("p k d -> p (k d)")
                        last = pe.transpose(trp[turn_bank(k)][:, :].bitcast(F16)[:, j * P:(j + 1) * P], rows_, ident16[:, :])
                    last.then_inc(tr_ready[stage], 1)

            def xt_there(q, stage, k=None):
                pe.wait_ge(xt_ready[stage], q.count(TURNED[stage], TURNED[stage] if k is None else k + 1))

            def by_parts(out_, weights, moving, weights_move=False):
                for part in range(PARTS):
                    w = weights(part)
                    last = pe.matmul(out_, moving if weights_move else w, w if weights_move else moving,
                                     start=(part == 0), stop=(part == PARTS - 1))
                return last

            def embedding(q):
                s = parity(q)
                pe.wait_ge(hot_ready, q + 1)
                for t in range(T):
                    for k in range(2):
                        for part in range(3):
                            last = pe.matmul(outp[s][:, t * D:(t + 1) * D], hot[s][:, k, t * P:(t + 1) * P],
                                             table_parts[:, part, k, :], start=(k + part == 0), stop=(k + part == 3))
                last.then_inc(tok_mm, 1)

            def scores(q, i, earlier):
                s = parity(q)
                if i >= 4:
                    pe.wait_ge(exp_done, q.count(SJ, i - 3))
                elif earlier:
                    pe.wait_ge(d_done, q.count(T, i - 3))
                m, g = i % T, i // T
                pe.matmul(wide[i % 4][:, :], xt[s][:, m * P:(m + 1) * P], xt_high[s][:, g * 512:(g + 1) * 512],
                          start=True, stop=False)
                pe.matmul(wide[i % 4][:, :], xt[s][:, m * P:(m + 1) * P], xt_low[s][:, g * 512:(g + 1) * 512],
                          start=False, stop=True).then_inc(s_ready, 1)

            def weighted(q, i):
                s = parity(q)
                m, g = i % T, i // T
                pe.wait_ge(exp_done, q.count(SJ, i + 1))
                if m == 0 and g == 1:
                    pe.wait_ge(ctx_done, q.count(2, 1))
                for n in range(4):
                    last = pe.matmul(outp[s][:, n * W65:(n + 1) * W65], ering[:, i % 4, n * P:(n + 1) * P],
                                     xn[s][:, m, :], start=(m == 0 and n == 0), stop=(m == T - 1),
                                     skip_group_check=True)
                last.then_inc(pv_done, 1)

            def attention(q, earlier, beside):
                lag = 2
                for i in range(SJ + lag):
                    if i < SJ:
                        scores(q, i, earlier)
                    if i >= lag:
                        weighted(q, i - lag)
                        beside(i - lag)

            def hidden_layer(q, back):
                s = parity(q)
                transposes(q, 1, back)
                for g in range(2):
                    xt_there(q, 1, g)
                    for c in range(CH):
                        by_parts(wide[g * 2 + c][:, :], lambda part: ffn_w1[:, part, c * P:(c + 1) * P],
                                 xt[s][:, g * 512:(g + 1) * 512]).then_inc(h_ready, 1)
                pe.wait_ge(gelu_done, q.count(4, 4))
                for t in range(T):
                    for c in range(CH):
                        last = pe.matmul(outp[s][:, t * E8:(t + 1) * E8], ht[:, s, c, t * P:(t + 1) * P],
                                         ffn_wg[:, c, :], start=(c == 0), stop=(c == CH - 1), skip_group_check=True)
                    if t == T - 1:
                        last.then_inc(flog_ready, 1)
                    if t == 3:
                        expert_layer(q, [0])
                        if back:
                            router(q.before())
                expert_layer(q, range(1, 4))

            def expert_layer(q, tiles):
                for t in tiles:
                    if t >= 4:
                        pe.wait_ge(d_done, q.count(T, t - 3))
                    for c in range(CH):
                        last = pe.matmul(wide[t % 4][:, :], ht[:, parity(q), c, t * P:(t + 1) * P],
                                         ffn_wd[:, c, :, :].rearrange("p e d -> p (e d)"), start=(c == 0), stop=(c == CH - 1))
                    last.then_inc(d_ready, 1)

            def selection_turned(q):
                s = parity(q)
                pe.wait_ge(selp_ready, q + 1)
                alone(pe)
                pe.transpose(outp[s][0:T * E8, 64:64 + P], selp[s][:, :, :].rearrange("p t e -> p (t e)"), ident[:, :]).then_inc(selt_mm, 1)

            def expert_biases(q):
                s = parity(q)
                pe.wait_ge(selt_done, q + 1)
                pe.matmul(outp[s][:, :], selt[s][:, :], ffn_bd[:, :, :].rearrange("p t d -> p (t d)"),
                          start=True, stop=True).then_inc(bd_ready, 1)

            def ssm_in(q):
                xt_there(q, 2)
                for g in range(2):
                    by_parts(trp[g][:, :], lambda part: ssm_w1t[:, part, :],
                             xt[parity(q)][:, g * 512:(g + 1) * 512]).then_inc(u_ready, 1)

            def ssm_out(q):
                s = parity(q)
                pe.wait_ge(scan_done, q + 1)
                for t in range(T):
                    pe.matmul(outp[s][:, t * D:(t + 1) * D], gst[:, s, t * P:(t + 1) * P], ssm_w2bc[:, :],
                              start=True, stop=False)
                    last = pe.matmul(outp[s][:, t * D:(t + 1) * D], ysilu[s][:, t * P:(t + 1) * P], ssm_w2d[:, :],
                                     start=False, stop=True)
                last.then_inc(mout_ready, 1)

            def router(q):
                s = parity(q)
                transposes(q, 3)
                for t in range(T):
                    if t % HALF == 0:
                        xt_there(q, 3, t // HALF)
                    last = by_parts(outp[s][:, t * EX:(t + 1) * EX], lambda part: moe_wr[:, part, :],
                                    xt[s][:, t * P:(t + 1) * P], weights_move=True)
                last.then_inc(rlog_ready, 1)

            def unit(q, front=True, back=True, pre=True):
                prev = q.before()
                if front:
                    transposes(q, 0)
                    xt_there(q, 0)

                    def beside(i):
                        if back and i == SSM_AT:
                            transposes(prev, 2)
                        if back and i == SSM_AT + 1:
                            ssm_in(prev)

                    attention(q, back, beside)
                elif back:
                    transposes(prev, 2)
                    ssm_in(prev)
                if back:
                    ssm_out(prev)
                if front:
                    hidden_layer(q, back)
                elif back:
                    router(prev)
                if pre:
                    if back:
                        pe.wait_ge(logits_read, prev + 1)
                    embedding(q.after())
                if front:
                    expert_layer(q, range(4, T))
                    selection_turned(q)
                    expert_biases(q)

            def route(half):
                pe.wait_ge(picks_ready, half + 1)
                for k in range(4):
                    pe.matmul((trp + outp)[k][:, :], ones[:, :],
                              picks[:, :, 16 * k:16 * (k + 1)].rearrange("p t e -> p e t"),
                              start=True, stop=True).then_inc(cnt_mm, 1)
                for k in range(4):
                    pe.matmul(wide[k][:, :], before[:, :], picks[:, 8 * k:8 * (k + 1), :].rearrange("p t e -> p (t e)"),
                              start=True, stop=True).then_inc(place_mm, 1)
                pe.wait_ge(eb_ready, half + 1)
                pe.matmul(outp[0][0:1, 0:BLOCKS], eb[:, :], ident[:, 0:BLOCKS], start=True, stop=True).then_inc(expert_mm, 1)

            embedding(Group(None, 0))
            unit(Group(None, 0), back=False)
            with pe.Fori(0, UNIT_LOOPS) as i:
                unit(Group(i, 1))
                unit(Group(i, 2))
            route(0)
            pe.wait_ge(expert_ready, 1)
            unit(Group(None, LAST), pre=False)
            unit(Group(None, SEQS), front=False, pre=False)
            route(1)

            pe.wait_ge(expert_ready, HALVES)
            pe.wait_ge(moe_loaded, 16)
            pe.wait_ge(w1_split, EX // STAGE_E)
            even_group = pe.alloc_register("even_group")
            odd_group = [None]
            for half in range(HALVES):
                before_ = half * GROUPS

                def turn(g):
                    u = parity(g)
                    if g.i is None:
                        pe.wait_ge(xb_loaded[u], 16 * (before_ // 2 + g.n // 2 + 1))
                    else:
                        pe.wait_ge(xb_loaded[u], 16 * g.i + 16 * (before_ // 2 + g.n // 2 + 1))
                    alone(pe)
                    for j in range(GROUP):
                        last = pe.transpose(trp[u][:, 0:GROUP * P // 2].bitcast(F16)[:, j * P:(j + 1) * P], xb[:, u, j, :], ident16[:, :])
                    last.then_inc(xbt_mm, 1)

                def up_projection(g):
                    u = parity(g)
                    packed, es = experts(pe, half, g)
                    if u == 0:
                        pe.reg_mov(even_group, packed)
                    else:
                        odd_group[0] = es
                    pe.wait_ge(xbt_ready, g + (before_ + 1))
                    for j, e in enumerate(es):
                        last = by_parts(wide[u][:, j * P:(j + 1) * P],
                                        lambda part: moe_w1[:, part, bass.ds(e, 1), :].rearrange("p a n -> p (a n)"),
                                        xbt[:, u, j * P:(j + 1) * P])
                    last.then_inc(hb_mm, 1)

                def down_projection(g):
                    u = parity(g)
                    es = odd_group[0] if u else unpacked(pe, pe.snap(even_group))
                    pe.wait_ge(hb_ready, g + (before_ + 1))
                    pe.wait_ge(yb_ready, g + (before_ + 1))
                    for j, e in enumerate(es):
                        last = pe.matmul(outp[u][:, j * D:(j + 1) * D], hbt[:, u, j * P:(j + 1) * P],
                                         moe_w2[:, bass.ds(e, 1), :].rearrange("p a n -> p (a n)"), start=True, stop=True)
                    last.then_inc(yb_mm, 1)

                pipeline(pe, turn, up_projection, down_projection)

        @block.vector
        def _(dve):
            at = [0]
            base = [None]

            def step(ins):
                at[0] += 1
                ins.then_inc(dve_step, 1)
                dve.wait_ge(dve_step, at[0] if base[0] is None else base[0] + at[0])

            def all_done():
                dve.wait_ge(dve_step, at[0] if base[0] is None else base[0] + at[0])

            def halves(op):
                for k in range(2):
                    at[0] += 1
                    op(slice(k * HALF, (k + 1) * HALF)).then_inc(dve_step, 1)
                    dve.wait_ge(dve_step, at[0] - 1 if base[0] is None else base[0] + (at[0] - 1))

            def looped(n, per, body):
                start = at[0]
                with dve.Fori(0, n) as it:
                    base[0] = it * per
                    body(it)
                    base[0] = None
                assert at[0] - start == per, at[0] - start
                at[0] = start + n * per

            step(dve.memset(ffn_bd[:, :, :], 0.0))
            dve.sem_inc(bd_zero, 1)
            step(dve.memset(zeros, 0.0))
            dve.sem_inc(zero_ready, 1)
            for s in range(2):
                step(dve.memset(xn[s][:, :, D:W65], 1.0))
            dve.wait_ge(ids_loaded, 16)
            step(dve.tensor_scalar(ids_i[:, 0, :], ids[:, :], 7, None, ALU.arith_shift_right))
            step(dve.tensor_scalar(ids_i[:, 1, :], ids[:, :], VOCAB - 1, None, ALU.bitwise_and))
            step(dve.tensor_copy(ids_f[:, 0, :], ids_i[:, 0, :]))
            step(dve.tensor_scalar(ids_f[:, 1, :], ids_f[:, 0, :], 0.0, float(VOCAB), ALU.is_lt, ALU.mult))
            step(dve.tensor_tensor(ids_f[:, 2, :], ids_f[:, 0, :], ids_f[:, 1, :], ALU.add))
            step(dve.tensor_scalar(ids_b[:, 0, :], ids_f[:, 2, :], 0.0, float(VOCAB - 1), ALU.max, ALU.min))
            dve.tensor_copy(ids_b[:, 1, :], ids_i[:, 1, :]).then_inc(ids_ready, 1)
            dve.wait_ge(w_loaded, 16 * N_SETUP_LOADS)
            dve.memset(ssm_bn[:, 3:4], -0.5).then_inc(bn_var, 1)
            dve.tensor_scalar(ssm_bn[:, 4:5], ssm_col[:, 5:6], BN_EPS, None, ALU.add).then_inc(bn_var, 1)
            dve.wait_ge(bn_rstd, 1)
            step(dve.tensor_tensor(ssm_bn[:, 0:1], ssm_bn[:, 5:6], ssm_col[:, 2:3], ALU.mult))
            step(dve.tensor_tensor(ssm_bn[:, 4:5], ssm_col[:, 1:2], ssm_col[:, 4:5], ALU.subtract))
            step(dve.tensor_tensor(ssm_bn[:, 4:5], ssm_bn[:, 4:5], ssm_bn[:, 0:1], ALU.mult))
            step(dve.tensor_tensor(ssm_bn[:, 1:2], ssm_bn[:, 4:5], ssm_col[:, 3:4], ALU.add))
            step(dve.tensor_tensor(ssm_bc[:, 0, :], ssm_bc[:, 0, :], ssm_bc[:, 1, :], ALU.mult))
            step(dve.tensor_reduce(ssm_bn[:, 3:4], ssm_bc[:, 0, :], AX, ALU.add))
            dve.wait_ge(setup_t, 5)
            step(dve.tensor_scalar(ssm_w2bc[:, :], trp[1][:, 0:D], ssm_bn[:, 3:4], None, ALU.mult))
            step(dve.tensor_scalar(ssm_w2d[:, :], trp[1][:, 0:D], ssm_col[:, 7:8], None, ALU.mult))
            dve.wait_ge(table_mm, 2)
            step(dve.tensor_copy(table[:, 0, :], outp[0][:, 0:D]))
            step(dve.tensor_tensor(table[:, 1, :], outp[1][:, 0:D], tok_b[:, :], ALU.add))
            for part in range(3):
                step(dve.tensor_copy(table_parts[:, part, :, :], table[:, :, :]))
                if part < 2:
                    step(dve.tensor_tensor(table[:, :, :], table[:, :, :], table_parts[:, part, :, :], ALU.subtract))
            dve.sem_inc(table_ready, 1)
            dve.wait_ge(setup_c, 4)
            for src, parts in ((ffn_w1f, ffn_w1), (ssm_w1f, ssm_w1t), (moe_wrf, moe_wr)):
                for part in range(PARTS):
                    step(dve.tensor_copy(parts[:, part, :], src))
                    if part < PARTS - 1:
                        step(dve.tensor_tensor(src, src, parts[:, part, :], ALU.subtract))
            dve.wait_ge(decay_ready, 1)
            dve.wait_ge(consts, 9)
            dve.sem_inc(setup_done, 2)

            def bc(ap, shape):
                return ap.to_broadcast(shape)

            SH = [P, T, D]

            def layernorm(src, s):
                alone(dve)
                step(dve.tensor_reduce(stat[:, 0, :], src, AX, ALU.add))
                step(dve.scalar_tensor_tensor(xc[:, :, :], bc(stat[:, 0, :].unsqueeze(2), SH), -1.0 / D, src, ALU.mult, ALU.add))
                step(dve.tensor_tensor(xn[s][:, :, 0:D], xc[:, :, :], xc[:, :, :], ALU.mult))
                step(dve.tensor_reduce(stat[:, 1, :], xn[s][:, :, 0:D], AX, ALU.add))
                step(dve.tensor_scalar(stat[:, 1, :], stat[:, 1, :], 1.0 / D, LN_EPS, ALU.mult, ALU.add))
                step(dve.tensor_scalar(stat_i[:, :], stat[:, 1, :].bitcast(I32), 1, None, ALU.arith_shift_right))
                step(dve.tensor_scalar(stat[:, 2, :].bitcast(I32), stat_i[:, :], -1.0, float(RSQRT_SEED), ALU.mult, ALU.add))
                for _ in range(3):
                    step(dve.scalar_tensor_tensor(stat[:, 3, :], stat[:, 2, :], -0.5, stat[:, 2, :], ALU.mult, ALU.mult))
                    step(dve.tensor_tensor(stat[:, 3, :], stat[:, 3, :], stat[:, 1, :], ALU.mult))
                    step(dve.scalar_tensor_tensor(stat[:, 2, :], stat[:, 3, :], 1.5, stat[:, 2, :], ALU.add, ALU.mult))
                halves(lambda t: dve.tensor_tensor(xn[s][:, t, 0:D], xc[:, t, :],
                                                   bc(stat[:, 2, t].unsqueeze(2), [P, HALF, D]), ALU.mult))

            def split(stage, s):
                halves(lambda t: dve.tensor_copy(xs[s][:, t, 1, :], xn[s][:, t, 0:D]))
                halves(lambda t: dve.tensor_tensor(xs[s][:, t, 2, :], xn[s][:, t, 0:D], xs[s][:, t, 1, :], ALU.subtract))
                if stage > 0:
                    dve.sem_inc(xn_ready[stage], 1)
                all_done()
                dve.sem_inc(xn_ready[stage], 1)
                if stage == 0:
                    step(dve.tensor_copy(xs[s][:, :, 0, :], xs[s][:, :, 1, :]))
                    dve.sem_inc(xn_ready[stage], 1)
                    step(dve.tensor_copy(xs[s][:, :, 3, :], xs[s][:, :, 2, :]))
                    dve.sem_inc(xn_ready[stage], 1)

            def context(q, g):
                s = parity(q)
                dve.wait_ge(pv_done, q.count(SJ, (g + 1) * T))
                o = outp[s][:, 0:4 * W65].rearrange("p (t d) -> p t d", d=W65)
                step(dve.reciprocal(stat[:, 4, 0:4], o[:, :, D]))
                step(dve.tensor_tensor(xc[:, 0:4, :], o[:, :, 0:D], bc(stat[:, 4, 0:4].unsqueeze(2), [P, 4, D]), ALU.mult))
                dve.sem_inc(ctx_done, 1)
                step(dve.tensor_tensor(h[s][:, 4 * g:4 * g + 4, :], h[s][:, 4 * g:4 * g + 4, :], xc[:, 0:4, :], ALU.add))

            G = [P, T, E8]

            def expert_gate(q):
                s = parity(q)
                dve.wait_ge(flog_ready, q + 1)
                lo = outp[s][:, 0:T * E8].rearrange("p (t e) -> p t e", e=E8)
                step(dve.tensor_tensor(gate[:, 0, :, :], lo, bc(ffn_bg[:, :].unsqueeze(1), G), ALU.add))
                step(dve.tensor_reduce(gate1[:, 0, :], gate[:, 0, :, :], AX, ALU.max))
                step(dve.tensor_tensor(fd[s][:, :, :], gate[:, 0, :, :], bc(gate1[:, 0, :].unsqueeze(2), G), ALU.subtract))
                dve.sem_inc(fd_ready, 1)
                step(dve.tensor_scalar(gate[:, 1, :, :], fd[s][:, :, :], 0.0, None, ALU.is_equal))
                step(dve.tensor_tensor(gate[:, 1, :, :], gate[:, 1, :, :], bc(rank_e8[:, :].unsqueeze(1), G), ALU.mult))
                step(dve.tensor_reduce(gate1[:, 1, :], gate[:, 1, :, :], AX, ALU.max))
                step(dve.tensor_tensor(gate[:, 2, :, :], gate[:, 1, :, :], bc(gate1[:, 1, :].unsqueeze(2), G), ALU.is_equal))
                dve.wait_ge(fexp_done, q + 1)
                step(dve.tensor_reduce(gate1[:, 2, :], fe[s][:, :, :], AX, ALU.add))
                step(dve.reciprocal(gate1[:, 3, :], gate1[:, 2, :]))
                step(dve.tensor_tensor(selp[s][:, :, :], gate[:, 2, :, :], bc(gate1[:, 3, :].unsqueeze(2), G), ALU.mult))
                dve.sem_inc(selp_ready, 1)

            def select(q, tiles):
                s = parity(q)
                for t in tiles:
                    dve.wait_ge(d_ready, q.count(T, t + 1))
                    step(dve.tensor_tensor(dtmp[s][:, t % 2, :, :], wide[t % 4][:, :].rearrange("p (e d) -> p e d", d=D),
                                           bc(selp[s][:, t, :].unsqueeze(2), [P, E8, D]), ALU.mult))
                    dve.sem_inc(d_done, 1)
                    step(dve.tensor_reduce(acc[:, t, :], dtmp[s][:, t % 2, :, :].rearrange("p e d -> p d e"), AX, ALU.add))

            def add_experts(q):
                s = parity(q)
                step(dve.tensor_tensor(h[s][:, :, :], h[s][:, :, :], acc[:, :, :], ALU.add))
                dve.wait_ge(bd_ready, q + 1)
                step(dve.tensor_tensor(h[s][:, :, :], outp[s][:, :].rearrange("p (t d) -> p t d", d=D), h[s][:, :, :], ALU.add))

            def convolution(q):
                s = parity(q)
                dve.wait_ge(silu1_done, q.count(2, 2))
                step(dve.tensor_scalar(yconv[s], up[:, s, 0:SEQ], ssm_taps[:, 0:1], None, ALU.mult))
                for k in range(1, TAPS):
                    step(dve.scalar_tensor_tensor(yconv[s], up[:, s, k:k + SEQ], ssm_taps[:, k:k + 1], yconv[s], ALU.mult, ALU.add))
                dve.sem_inc(conv_done, 1)

            def scan(q):
                s = parity(q)
                dve.wait_ge(silu2_done, q + 1)
                step(dve.tensor_tensor_scan(gst[:, s, 0:SEQ], bc(ssm_bn[:, 2:3], [P, SEQ]), ysilu[s], 0.0, ALU.mult, ALU.add))
                dve.sem_inc(scan_done, 1)

            def add_ssm(q):
                s = parity(q)
                dve.wait_ge(mout_ready, q + 1)
                if q.i is not None:
                    done = EX // STAGE_E * (2 * PARTS - 1)
                    dve.wait_ge(split_step, q.i * (done // 2 - 1) + (done - 2 * (done // 2 - 1)))
                step(dve.tensor_tensor(h[s][:, :, :], outp[s][:, :].rearrange("p (t d) -> p t d", d=D), h[s][:, :, :], ALU.add))
                step(dve.tensor_tensor(h_all[:, q.tiles(), :], h[s][:, :, :], bc(ssm_b2[:, :].unsqueeze(1), SH), ALU.add))
                layernorm(h_all[:, q.tiles(), :], s)
                split(3, s)

            def logits(q):
                s = parity(q)
                dve.wait_ge(rlog_ready, q + 1)
                step(dve.tensor_tensor(lg[s][:, :, :], outp[s][:, :].rearrange("p (t e) -> p t e", e=EX),
                                       bc(moe_br[:, :].unsqueeze(1), [P, T, EX]), ALU.add))
                dve.sem_inc(logits_read, 1)

            def top_two(q):
                s = parity(q)
                alone(dve)
                for t in range(T):
                    last = dve.max(v8[s][:, t, :], lg[s][:, t, :])
                step(last)
                alone(dve)
                for t in range(T):
                    last = dve.max_index(i8[s][:, t, :], v8[s][:, t, :], lg[s][:, t, :])
                step(last)
                step(dve.tensor_copy(top_val[:, q.tiles(), :], v8[s][:, :, 0:TOP]))
                step(dve.tensor_copy(top_idx[:, q.tiles(), :], i8[s][:, :, 0:TOP]))

            def one_hot(q):
                s = parity(q)
                dve.wait_ge(idx_loaded[s], q.of_parity() * 16)
                step(dve.tensor_scalar(hot[s][:, :, :], idx_row[:, :, s * SEQ:(s + 1) * SEQ], iota_p[:, 0:1], None, ALU.is_equal))
                dve.sem_inc(hot_ready, 1)

            def first_rows(q):
                s = parity(q)
                dve.wait_ge(tanh_done, q + 1)
                layernorm(h[s][:, :, :], s)
                split(0, s)

            def unit(q, front=True, back=True, pre=True):
                prev, s = q.before(), parity(q)
                if back:
                    layernorm(h[1 - s][:, :, :], 1 - s)
                    split(2, 1 - s)
                if front:
                    context(q, 0)
                if back:
                    convolution(prev)
                if front:
                    context(q, 1)
                if back:
                    scan(prev)
                if front:
                    layernorm(h[s][:, :, :], s)
                    split(1, s)
                if back:
                    add_ssm(prev)
                if pre:
                    one_hot(q.after())
                if back:
                    logits(prev)
                if front:
                    expert_gate(q)
                    select(q, range(4))
                if pre:
                    first_rows(q.after())
                if front:
                    select(q, range(4, T))
                    add_experts(q)
                if back:
                    top_two(prev)

            def route(half):
                tiles = slice(half * TH, (half + 1) * TH)
                OH = [P, TH, EX]
                for k in range(TOP):
                    step(dve.tensor_tensor(pick[k], bc(iota_e[:, :].unsqueeze(1), OH),
                                           bc(top_idx[:, tiles, k].unsqueeze(2), OH), ALU.is_equal))
                step(dve.tensor_tensor(picks, pick[0], pick[1], ALU.add))
                dve.sem_inc(picks_ready, 1)
                step(dve.tensor_tensor(gates[:, tiles, 2], top_val[:, tiles, 1], top_val[:, tiles, 0], ALU.subtract))
                dve.sem_inc(gdiff_ready, 1)
                step(dve.memset(seg_keep[:, :, :], 1.0))
                step(dve.memset(seg_keep[:, :, 0:1], 0.0))
                step(dve.memset(cnt[:, :, 0:1], 0.0))
                dve.wait_ge(cnt_ready, 4 * (half + 1))
                step(dve.tensor_tensor_scan(cum[:, :, :].rearrange("p e t -> p (e t)"), seg_keep[:, :, :].rearrange("p e t -> p (e t)"),
                                            cnt[:, :, :].rearrange("p e t -> p (e t)"), 0.0, ALU.mult, ALU.add))
                step(dve.tensor_scalar(nb_i[:, :], cum[:, :, TH], float(P - 1), None, ALU.add))
                step(dve.tensor_scalar(nb_i[:, :], nb_i[:, :], 7, None, ALU.arith_shift_right))
                step(dve.tensor_copy(nb[:, 0, :], nb_i[:, :]))
                step(dve.tensor_tensor_scan(nb[:, 1, :], bc(seg_keep[:, 0, 1:2], [P, EX]), nb[:, 0, :], 0.0, ALU.mult, ALU.add))
                step(dve.tensor_tensor(nb[:, 2, :], nb[:, 1, :], nb[:, 0, :], ALU.subtract))
                step(dve.tensor_scalar(nb[:, 4, :], nb[:, 2, :], iota_p[:, 0:1], None, ALU.is_le))
                step(dve.tensor_reduce(eb[:, :], nb[:, 4, :], AX, ALU.add))
                dve.sem_inc(eb_ready, 1)
                step(dve.tensor_scalar(nb[:, 3, :], nb[:, 2, :], float(P), None, ALU.mult))
                for k in range(4):
                    dve.wait_ge(place_mm, 4 * half + k + 1)
                    step(dve.tensor_tensor(place[:, 8 * k:8 * (k + 1), :], wide[k][:, :].rearrange("p (t e) -> p t e", e=EX),
                                           cum[:, :, 8 * k:8 * (k + 1)].rearrange("p e t -> p t e"), ALU.add))
                dve.wait_ge(expert_mm, half + 1)
                step(dve.tensor_scalar(expert_f[:, :], outp[0][0:1, 0:BLOCKS], -1.0, None, ALU.add))
                of_block = expert_f[:, :].rearrange("p (g j) -> p g j", j=GROUP)
                for j in range(GROUP - 2, -1, -1):
                    dst = of_block[:, :, GROUP - 1] if j else expert[half][:, :]
                    step(dve.scalar_tensor_tensor(dst, of_block[:, :, GROUP - 1], float(EX), of_block[:, :, j], ALU.mult, ALU.add))
                dve.sem_inc(expert_ready, 1)
                step(dve.tensor_tensor(place, place, bc(nb[:, 3, :].unsqueeze(1), OH), ALU.add))
                for k in range(TOP):
                    step(dve.tensor_tensor(prod, place, pick[k], ALU.mult))
                    step(dve.tensor_reduce(slot_f[:, k, :], prod, AX, ALU.add))
                step(dve.tensor_copy(slot_i[:, 0, :, :], slot_f[:, :, :]))
                step(dve.tensor_scalar(slot_i[:, 1, :, :], slot_i[:, 0, :, :], ~(GROUP * P - 1), None, ALU.bitwise_and))
                step(dve.tensor_scalar(slot_i[:, 2, :, :], slot_i[:, 0, :, :], P - 1, 2, ALU.bitwise_and, ALU.logical_shift_left))
                step(dve.tensor_scalar(slot_i[:, 3, :, :], slot_i[:, 0, :, :], 7, GROUP - 1, ALU.logical_shift_right, ALU.bitwise_and))
                step(dve.tensor_tensor(slot_i[:, 1, :, :], slot_i[:, 1, :, :], slot_i[:, 2, :, :], ALU.bitwise_or))
                step(dve.tensor_tensor(rows[half][:, :, :], slot_i[:, 1, :, :], slot_i[:, 3, :, :], ALU.bitwise_or))
                dve.sem_inc(rows_ready, 1)
                dve.wait_ge(gexp_done, half + 1)
                step(dve.tensor_scalar(gates[:, tiles, 0], gates[:, tiles, 2], 1.0, None, ALU.add))
                step(dve.reciprocal(gates[:, tiles, 0], gates[:, tiles, 0]))
                step(dve.tensor_tensor(gates[:, tiles, 1], gates[:, tiles, 2], gates[:, tiles, 0], ALU.mult))

            dve.wait_ge(bd_loaded, 16 * (2 * CH + T))
            for s in range(2):
                step(dve.memset(up[:, s, 0:pad], 0.0))
                step(dve.memset(up[:, s, pad + SEQ:2 * pad + SEQ], 0.0))
            one_hot(Group(None, 0))
            first_rows(Group(None, 0))
            unit(Group(None, 0), back=False)

            def two_units(i):
                unit(Group(i, 1))
                unit(Group(i, 2))

            looped(UNIT_LOOPS, DVE_MAIN, two_units)
            route(0)
            for s in range(2):
                step(dve.memset(up[:, s, 0:pad], 0.0))
                step(dve.memset(up[:, s, pad + SEQ:2 * pad + SEQ], 0.0))
            unit(Group(None, LAST), pre=False)
            unit(Group(None, SEQS), front=False, pre=False)
            route(1)

            for u in range(2):
                dve.sem_inc(yb_stored[u], 16)
                dve.sem_inc(yb_ready, 1)
            dve.wait_ge(b2_loaded, 16)
            for half in range(HALVES):
                def results(g):
                    u = parity(g)
                    _, es = experts(dve, half, g)
                    dve.wait_ge(yb_mm, g + (half * GROUPS + 1))
                    dve.wait_ge(yb_stored[u], 16 * g.i + 16 * (half * GROUPS // 2 + 1))
                    for j, e in enumerate(es):
                        last = dve.tensor_tensor(yb[:, u, j, :], outp[u][:, j * D:(j + 1) * D],
                                                 moe_b2[:, bass.ds(e, 1), :].rearrange("p a n -> p (a n)"), ALU.add)
                    last.then_inc(yb_ready, 1)

                pipeline(dve, results)
            for g in range(SEQS):
                half, t0 = g * T // TH, g * T % TH
                tiles = slice(g * T, (g + 1) * T)
                dve.wait_ge(gathered[g], 16 * TOP * T)
                for k in range(TOP):
                    y = yg[half][:, k, t0:t0 + T, :]
                    step(dve.tensor_tensor(y, y, bc(gates[:, tiles, k].unsqueeze(2), SH), ALU.mult))
                    step(dve.tensor_tensor(h_all[:, tiles, :], h_all[:, tiles, :], y, ALU.add))
                dve.sem_inc(out_ready, 1)


DVE_MAIN = 276


def kernel(**inputs):
    import numpy as _np
    import concourse.bacc as _bacc
    from concourse import mybir as _mybir
    from concourse.bass_utils import run_bass_kernel_spmd as _run

    nc = _bacc.Bacc("TRN2", target_bir_lowering=False, num_devices=1)
    arrays, handles = {}, {}
    for name, v in inputs.items():
        v = _np.ascontiguousarray(v)
        arrays[f"in_{name}"] = v
        handles[name] = nc.dram_tensor(f"in_{name}", v.shape, _mybir.dt.from_np(v.dtype), kind="ExternalInput").ap()
    result = nc.dram_tensor("out_0", (SEQS, SEQ, D), F32, kind="ExternalOutput").ap()
    lm_tower(nc, handles, result)
    r = _run(nc, [arrays], core_ids=[0])
    return r.results[0]["out_0"]
```
